# Optimizing a Trainium2 kernel written in Bass

```python
import numpy as np
import jax
import jax.numpy as jnp

def _softmax(x, axis=-1):
    return jax.nn.softmax(x, axis=axis)

def _gelu(x):
    return jax.nn.gelu(x, approximate=True)

def _silu(x):
    return jax.nn.silu(x)

def _sigmoid(x):
    return jax.nn.sigmoid(x)

def _layernorm(x, axis=-1, eps=1e-05):
    m = jnp.mean(x, axis=axis, keepdims=True)
    v = jnp.var(x, axis=axis, keepdims=True)
    return (x - m) / jnp.sqrt(v + eps)

def _scatter_add(tgt, idx, src, axis=0):
    return tgt.at[idx].add(src)

def _segment_sum(src, seg, n):
    return jax.ops.segment_sum(src, seg, n)
kernel_name = 'mk_adaln_d2_jaxref_r8_e86b7f'

def setup_inputs(seed: int=0):
    np.random.seed(seed)
    _w = jnp.asarray

    def _L0_attn_setup():
        import jax, jax.numpy as jnp
        import numpy as np
        B, N = (2, 256)
        H, R = (8, 64)
        IN_DIM, OUT_DIM = (64, 64)
        D = IN_DIM + OUT_DIM
        INIT = 1.0
        key = jax.random.key(seed)
        k1, k2, k3, k4 = jax.random.split(key, 4)
        x = jax.random.normal(k1, (B, N, D), dtype=jnp.float32)
        Wq = jax.random.normal(k2, (H * R, D), dtype=jnp.float32) * (INIT / np.sqrt(H * R * D))
        Wk = jax.random.normal(k3, (H * R, D), dtype=jnp.float32) * (INIT / np.sqrt(H * R * D))
        Wv = jax.random.normal(k4, (H * D, D), dtype=jnp.float32) * (INIT / np.sqrt(H * D * D))
        Wk = Wk.at[:, -1].set(0.0)
        rows = np.arange(1, H + 1) * D - 1
        Wv = Wv.at[rows, :IN_DIM].set(0.0)
        return {'x': x, 'Wq': Wq, 'Wk': Wk, 'Wv': Wv}
    _L0_attn_in = _L0_attn_setup()

    def _L0_ffn_setup():
        import jax, jax.numpy as jnp
        import numpy as np
        H = 8
        KD = 128
        TOPK = 8
        NUM_KEYS = 32
        N_EXPERTS = NUM_KEYS * NUM_KEYS
        N_DIM = 128
        BN_EPS = 1e-05

        def gelu_new(x):
            c = jnp.sqrt(jnp.asarray(2.0 / jnp.pi, x.dtype))
            return 0.5 * x * (1.0 + jnp.tanh(c * (x + 0.044715 * x * x * x)))
        key = jax.random.key(seed)
        ks = jax.random.split(key, 5)
        b, s = (2, 128)
        x = jax.random.normal(ks[0], (b, s, N_DIM), dtype=jnp.float32)
        w_q = jax.random.normal(ks[1], (N_DIM, 2 * H * KD), dtype=jnp.float32) * 0.02
        bn_gamma = jnp.ones((2 * H * KD,), dtype=jnp.float32)
        bn_beta = jnp.zeros((2 * H * KD,), dtype=jnp.float32)
        keys = jax.random.normal(ks[2], (H, NUM_KEYS, 2, KD), dtype=jnp.float32) * 0.02
        down_embed = jax.random.normal(ks[3], (N_EXPERTS, N_DIM), dtype=jnp.float32) * 0.02
        up_embed = jax.random.normal(ks[4], (N_EXPERTS, N_DIM), dtype=jnp.float32) * 0.02
        return {'x': x, 'w_q': w_q, 'bn_gamma': bn_gamma, 'bn_beta': bn_beta, 'keys': keys, 'down_embed': down_embed, 'up_embed': up_embed}
    _L0_ffn_in = _L0_ffn_setup()
    _L0_c = _w((lambda *s: np.random.randn(*s).astype(np.float32) * 0.05)(8, 128))
    _L0_wmod = _w((lambda *s: np.random.randn(*s).astype(np.float32) * 0.05)(128, 6 * 128) * 128 ** (-0.5))

    def _L1_attn_setup():
        import jax, jax.numpy as jnp
        import numpy as np
        EPS = 1e-12
        key = jax.random.key(seed)
        k1, k2 = jax.random.split(key)
        b, n, d = (4, 512, 128)
        x = jax.random.normal(k1, (b, n, d), dtype=jnp.float32)
        W_qkva = jax.random.normal(k2, (3 * d, d), dtype=jnp.float32) * 0.02
        gamma = jnp.ones((d,), dtype=jnp.float32)
        return {'x': x, 'W_qkva': W_qkva, 'gamma': gamma}
    _L1_attn_in = _L1_attn_setup()

    def _L1_ffn_setup():
        import jax, jax.numpy as jnp
        import numpy as np
        DIM = 128

        def _reference_tuple_inner(x, W_r, W_k, W_v, mu_r, mu_k):
            B, T, C = x.shape
            x_prev = jnp.concatenate([jnp.zeros((B, 1, C), x.dtype), x[:, :-1, :]], axis=1)
            xr = mu_r * x + (1.0 - mu_r) * x_prev
            xk = mu_k * x + (1.0 - mu_k) * x_prev
            r = jax.nn.sigmoid(jnp.einsum('btc,dc->btd', xr, W_r))
            k = jnp.einsum('btc,dc->btd', xk, W_k)
            k_act = jnp.square(jax.nn.relu(k))
            out = r * jnp.einsum('btc,dc->btd', k_act, W_v)
            new_state = x[:, -1, :]
            return (out, new_state)
        key = jax.random.key(seed)
        ks = jax.random.split(key, 6)
        B, T, C = (8, 256, DIM)
        x = jax.random.normal(ks[0], (B, T, C), dtype=jnp.float32)
        s = 1.0 / np.sqrt(C)
        W_r = jax.random.uniform(ks[1], (C, C), jnp.float32, -s, s)
        W_k = jax.random.uniform(ks[2], (C, C), jnp.float32, -s, s)
        W_v = jax.random.uniform(ks[3], (C, C), jnp.float32, -s, s)
        mu_r = jax.random.uniform(ks[4], (C,), jnp.float32)
        mu_k = jax.random.uniform(ks[5], (C,), jnp.float32)
        return {'x': x, 'W_r': W_r, 'W_k': W_k, 'W_v': W_v, 'mu_r': mu_r, 'mu_k': mu_k}
    _L1_ffn_in = _L1_ffn_setup()
    _L1_c = _w((lambda *s: np.random.randn(*s).astype(np.float32) * 0.05)(8, 128))
    _L1_wmod = _w((lambda *s: np.random.randn(*s).astype(np.float32) * 0.05)(128, 6 * 128) * 128 ** (-0.5))
    _d = {'L0_attn_x': _L0_attn_in['x'], 'L0_attn_Wq': _L0_attn_in['Wq'], 'L0_attn_Wk': _L0_attn_in['Wk'], 'L0_attn_Wv': _L0_attn_in['Wv'], 'L0_ffn_w_q': _L0_ffn_in['w_q'], 'L0_ffn_bn_gamma': _L0_ffn_in['bn_gamma'], 'L0_ffn_bn_beta': _L0_ffn_in['bn_beta'], 'L0_ffn_keys': _L0_ffn_in['keys'], 'L0_ffn_down_embed': _L0_ffn_in['down_embed'], 'L0_ffn_up_embed': _L0_ffn_in['up_embed'], 'L0_c': _L0_c, 'L0_wmod': _L0_wmod, 'L1_attn_W_qkva': _L1_attn_in['W_qkva'], 'L1_attn_gamma': _L1_attn_in['gamma'], 'L1_ffn_W_r': _L1_ffn_in['W_r'], 'L1_ffn_W_k': _L1_ffn_in['W_k'], 'L1_ffn_W_v': _L1_ffn_in['W_v'], 'L1_ffn_mu_r': _L1_ffn_in['mu_r'], 'L1_ffn_mu_k': _L1_ffn_in['mu_k'], 'L1_c': _L1_c, 'L1_wmod': _L1_wmod}
    _x0 = _d['L0_attn_x']
    _d['L0_attn_x'] = jax.random.normal(jax.random.fold_in(jax.random.key(seed), 1), (8, 1024, 128), dtype=_x0.dtype)
    del _x0
    return _d

def reference(L0_attn_x, L0_attn_Wq, L0_attn_Wk, L0_attn_Wv, L0_ffn_w_q, L0_ffn_bn_gamma, L0_ffn_bn_beta, L0_ffn_keys, L0_ffn_down_embed, L0_ffn_up_embed, L0_c, L0_wmod, L1_attn_W_qkva, L1_attn_gamma, L1_ffn_W_r, L1_ffn_W_k, L1_ffn_W_v, L1_ffn_mu_r, L1_ffn_mu_k, L1_c, L1_wmod):

    def _L0_attn_ref(x, Wq, Wk, Wv):
        import jax, jax.numpy as jnp
        import numpy as np
        B, N = (2, 256)
        H, R = (8, 64)
        IN_DIM, OUT_DIM = (64, 64)
        D = IN_DIM + OUT_DIM
        INIT = 1.0
        b, n, d = x.shape
        Q = (x @ Wq.T).reshape(b, n, H, R)
        K = (x @ Wk.T).reshape(b, n, H, R)
        V = (x @ Wv.T).reshape(b, n, H, d)
        attn = jnp.einsum('bnhr,bmhr->bhnm', Q, K)
        attn = jax.nn.softmax(attn, axis=-1)
        out = jnp.einsum('bhnm,bmhd->bnd', attn, V)
        return out

    def _L0_ffn_ref(x, w_q, bn_gamma, bn_beta, keys, down_embed, up_embed):
        import jax, jax.numpy as jnp
        import numpy as np
        H = 8
        KD = 128
        TOPK = 8
        NUM_KEYS = 32
        N_EXPERTS = NUM_KEYS * NUM_KEYS
        N_DIM = 128
        BN_EPS = 1e-05

        def gelu_new(x):
            c = jnp.sqrt(jnp.asarray(2.0 / jnp.pi, x.dtype))
            return 0.5 * x * (1.0 + jnp.tanh(c * (x + 0.044715 * x * x * x)))
        b, n, d = x.shape
        q = jnp.einsum('bnd,de->bne', x, w_q)
        mean = jnp.mean(q, axis=(0, 1))
        var = jnp.var(q, axis=(0, 1))
        q = (q - mean) * jax.lax.rsqrt(var + BN_EPS) * bn_gamma + bn_beta
        q = q.reshape(b, n, 2, H, KD).transpose(2, 0, 1, 3, 4)
        sim = jnp.einsum('pbnhd,hkpd->pbnhk', q, keys)
        sx, ix = jax.lax.top_k(sim[0], TOPK)
        sy, iy = jax.lax.top_k(sim[1], TOPK)
        all_scores = (sx[..., :, None] + sy[..., None, :]).reshape(b, n, H, TOPK * TOPK)
        all_indices = (ix[..., :, None] * NUM_KEYS + iy[..., None, :]).reshape(b, n, H, TOPK * TOPK)
        scores, pk = jax.lax.top_k(all_scores, TOPK)
        indices = jnp.take_along_axis(all_indices, pk, axis=-1)
        wd = down_embed[indices]
        wu = up_embed[indices]
        h = jnp.einsum('bnd,bnhkd->bnhk', x, wd)
        h = gelu_new(h)
        h = jax.nn.softmax(scores, axis=-1) * h
        out = jnp.einsum('bnhk,bnhkd->bnd', h, wu)
        return out

    def _L1_attn_ref(x, W_qkva, gamma):
        import jax, jax.numpy as jnp
        import numpy as np
        EPS = 1e-12
        d = gamma.shape[0]
        scale = d ** 0.5
        norm = jnp.maximum(jnp.linalg.norm(x, axis=-1, keepdims=True), EPS)
        xn = x / norm * scale * gamma
        h = jnp.einsum('bnd,ed->bne', xn, W_qkva)
        q, kv, a = jnp.split(h, 3, axis=-1)
        a = jax.nn.sigmoid(a)

        def binop(e_i, e_j):
            a_i, kv_i = e_i
            a_j, kv_j = e_j
            return (a_j * a_i, a_j * kv_i + kv_j)
        _, y = jax.lax.associative_scan(binop, (a, kv), axis=1)
        return q * y

    def _L1_ffn_ref(x, W_r, W_k, W_v, mu_r, mu_k):
        import jax, jax.numpy as jnp
        import numpy as np
        DIM = 128

        def _reference_tuple_inner(x, W_r, W_k, W_v, mu_r, mu_k):
            B, T, C = x.shape
            x_prev = jnp.concatenate([jnp.zeros((B, 1, C), x.dtype), x[:, :-1, :]], axis=1)
            xr = mu_r * x + (1.0 - mu_r) * x_prev
            xk = mu_k * x + (1.0 - mu_k) * x_prev
            r = jax.nn.sigmoid(jnp.einsum('btc,dc->btd', xr, W_r))
            k = jnp.einsum('btc,dc->btd', xk, W_k)
            k_act = jnp.square(jax.nn.relu(k))
            out = r * jnp.einsum('btc,dc->btd', k_act, W_v)
            new_state = x[:, -1, :]
            return (out, new_state)
        return _reference_tuple_inner(x, W_r, W_k, W_v, mu_r, mu_k)[0]
    x = L0_attn_x
    mod = (_silu(L0_c) @ L0_wmod).reshape(L0_c.shape[0], 6, 1, -1)
    sa, ca, ga, sb, cb, gb = (mod[:, 0], mod[:, 1], mod[:, 2], mod[:, 3], mod[:, 4], mod[:, 5])
    ga = (2 * (ga >= 0) - 1) * jnp.maximum(jnp.abs(ga), 0.25)
    gb = (2 * (gb >= 0) - 1) * jnp.maximum(jnp.abs(gb), 0.25)
    h = _layernorm(x, axis=-1) * (1 + ca) + sa
    x = x + ga * _L0_attn_ref(h, L0_attn_Wq, L0_attn_Wk, L0_attn_Wv)
    h = _layernorm(x, axis=-1) * (1 + cb) + sb
    x = x + gb * _L0_ffn_ref(h, L0_ffn_w_q, L0_ffn_bn_gamma, L0_ffn_bn_beta, L0_ffn_keys, L0_ffn_down_embed, L0_ffn_up_embed)
    mod = (_silu(L1_c) @ L1_wmod).reshape(L1_c.shape[0], 6, 1, -1)
    sa, ca, ga, sb, cb, gb = (mod[:, 0], mod[:, 1], mod[:, 2], mod[:, 3], mod[:, 4], mod[:, 5])
    ga = (2 * (ga >= 0) - 1) * jnp.maximum(jnp.abs(ga), 0.25)
    gb = (2 * (gb >= 0) - 1) * jnp.maximum(jnp.abs(gb), 0.25)
    h = _layernorm(x, axis=-1) * (1 + ca) + sa
    x = x + ga * _L1_attn_ref(h, L1_attn_W_qkva, L1_attn_gamma)
    h = _layernorm(x, axis=-1) * (1 + cb) + sb
    x = x + gb * _L1_ffn_ref(h, L1_ffn_W_r, L1_ffn_W_k, L1_ffn_W_v, L1_ffn_mu_r, L1_ffn_mu_k)
    return x

_drawn_inputs = setup_inputs


def setup_inputs(seed=0):
    import zlib

    import numpy as np

    out = dict(_drawn_inputs(seed))
    spreads = {'L0_ffn_bn_gamma': (1.0, 0.6), 'L0_ffn_bn_beta': (0.0, 0.8), 'L1_attn_gamma': (1.0, 0.6)}
    factors = {'L0_attn_Wq': 8.0,
     'L0_attn_Wk': 8.0,
     'L0_attn_Wv': 8.0,
     'L0_ffn_w_q': 8.0,
     'L0_ffn_keys': 8.0,
     'L0_ffn_down_embed': 8.0,
     'L0_ffn_up_embed': 8.0,
     'L0_c': 8.0,
     'L0_wmod': 8.0,
     'L1_attn_W_qkva': 3.322,
     'L1_ffn_W_r': 8.0,
     'L1_ffn_W_k': 2.98,
     'L1_ffn_W_v': 2.753,
     'L1_ffn_mu_r': 8.0,
     'L1_ffn_mu_k': 4.644}
    for name, (base, spread) in spreads.items():
        noise = np.random.default_rng([zlib.crc32(name.encode()), seed]).standard_normal(out[name].shape)
        drawn = base * np.exp(spread * noise) if base else spread * noise
        out[name] = jnp.asarray(drawn.astype(out[name].dtype))
    for name, factor in factors.items():
        out[name] = (out[name] * factor).astype(out[name].dtype)
    return out
```

```python
from contextlib import ExitStack

import concourse.bass as bass
from concourse import mybir

P = 128
B, N, D = 8, 1024, 128
TB = N // P
TT = B * TB
H, R = 8, 64
G = 16
NK, TOPK = 32, 8
STEPS_A = 73
LN_EPS, BN_EPS, NORM_EPS = 1e-5, 1e-5, 1e-12
HALF = N // 2

ALU = mybir.AluOpType
ACT = mybir.ActivationFunctionType
AX = mybir.AxisListType
F32 = mybir.dt.float32
F32R = mybir.dt.float32r
BF16 = mybir.dt.bfloat16
U32 = mybir.dt.uint32


def spread(ap, axis, count):
    ap = ap.unsqueeze(axis)
    shape = list(ap.shape)
    shape[axis] = count
    return ap.broadcast_to(shape)


class Chain:

    def __init__(self, eng, sem, base):
        self.eng, self.sem, self.base, self.n = eng, sem, base, 0

    def __call__(self, instruction):
        self.n += 1
        instruction.then_inc(self.sem, 1)
        self.eng.wait_ge(self.sem, self.base + self.n)


def layernorm(nc, dve, link, src, centred, stats, dst, scale, shift, var_ready, rstd_ready, n):
    tiles = src.shape[1]
    link(nc.vector.tensor_reduce(stats[:, 0, 0:tiles], src, AX.X, ALU.add))
    link(nc.vector.tensor_scalar(stats[:, 0, 0:tiles], stats[:, 0, 0:tiles], 1.0 / D, None, ALU.mult))
    link(nc.vector.tensor_tensor(centred, src, spread(stats[:, 0, 0:tiles], 2, D), ALU.subtract))
    link(nc.vector.tensor_tensor(dst, centred, centred, ALU.mult))
    link(nc.vector.tensor_reduce(stats[:, 1, 0:tiles], dst, AX.X, ALU.add))
    nc.vector.tensor_scalar(stats[:, 2, 0:tiles], stats[:, 1, 0:tiles], 1.0 / D, LN_EPS,
                            ALU.mult, ALU.add).then_inc(var_ready, 1)
    dve.wait_ge(rstd_ready, n)
    link(nc.vector.tensor_tensor(centred, centred, spread(stats[:, 3, 0:tiles], 2, D), ALU.mult))
    link(nc.vector.tensor_tensor(centred, centred, scale, ALU.mult))
    return nc.vector.tensor_tensor(dst, centred, shift, ALU.add)


def build_modulation(nc, tag, cT, wmod, mod, gb_keep, ones, banks):
    with ExitStack() as ctx:
        c_sb = ctx.enter_context(nc.sbuf_tensor(f"c_sb{tag}", [P, B], F32))
        w_sb = ctx.enter_context(nc.sbuf_tensor(f"wmod_sb{tag}", [P, 6 * D], F32))
        e_sb = ctx.enter_context(nc.sbuf_tensor(f"e_sb{tag}", [P, 3, B], F32))
        scb = ctx.enter_context(nc.sbuf_tensor(f"scb{tag}", [P, B, P], F32))
        tmp = ctx.enter_context(nc.sbuf_tensor(f"gate_tmp{tag}", [P, 2, B, D], F32))
        loaded = ctx.enter_context(nc.semaphore(f"mod_loaded{tag}"))
        exp_done = ctx.enter_context(nc.semaphore(f"mod_exp{tag}"))
        silu_ready = ctx.enter_context(nc.semaphore(f"mod_silu{tag}"))
        bank_full = ctx.enter_context(nc.semaphore(f"mod_full{tag}"))
        bank_free = ctx.enter_context(nc.semaphore(f"mod_free{tag}"))
        steps = ctx.enter_context(nc.semaphore(f"mod_steps{tag}"))
        block = ctx.enter_context(nc.Block())

        @block.sync
        def _(sp):
            sp.dma_start(c_sb[:], cT).then_inc(loaded, 16)
            sp.dma_start(w_sb[:], wmod).then_inc(loaded, 16)

        @block.scalar
        def _(act):
            act.wait_ge(loaded, 32)
            nc.scalar.activation(e_sb[:, 0, :], c_sb[:], ACT.Exp, scale=-1.0).then_inc(exp_done, 1)

        @block.tensor
        def _(pe):
            pe.wait_ge(loaded, 32)
            pe.wait_ge(silu_ready, 1)
            for b in range(B):
                if b >= 2:
                    pe.wait_ge(bank_free, b - 1)
                for k in range(2):
                    mm = nc.tensor.matmul(banks[b % 2][:, k * 512:k * 512 + 384], scb[:, b, :],
                                          w_sb[:, k * 384:(k + 1) * 384], start=True, stop=True)
                mm.then_inc(bank_full, 1)

        @block.vector
        def _(dve):
            link = Chain(dve, steps, 0)
            if ones is not None:
                link(nc.vector.memset(ones[:], 1.0))
            dve.wait_ge(exp_done, 1)
            link(nc.vector.tensor_scalar(e_sb[:, 1, :], e_sb[:, 0, :], 1.0, None, ALU.add))
            link(nc.vector.reciprocal(e_sb[:, 2, :], e_sb[:, 1, :]))
            link(nc.vector.tensor_tensor(e_sb[:, 1, :], e_sb[:, 2, :], c_sb[:], ALU.mult))
            nc.vector.tensor_copy(scb[:], spread(e_sb[:, 1, :], 2, P)).then_inc(silu_ready, 1)
            for b in range(B):
                dve.wait_ge(bank_full, b + 1)
                for k in range(2):
                    cp = nc.vector.tensor_copy(
                        mod[:, 3 * k:3 * k + 3, b, :],
                        banks[b % 2][:, k * 512:k * 512 + 384].rearrange("p (j d) -> p j d", j=3))
                    if k == 0:
                        cp.then_inc(steps, 1)
                        link.n += 1
                cp.then_inc(bank_free, 1)
            dve.wait_ge(bank_free, B)
            dve.wait_ge(steps, link.n)
            for j in (1, 4):
                link(nc.vector.tensor_scalar(mod[:, j], mod[:, j], 1.0, None, ALU.add))
            for j, out in ((2, mod[:, 2]), (5, gb_keep)):
                g = mod[:, j]
                link(nc.vector.tensor_scalar(tmp[:, 0], g, 0.0, 2.0, ALU.is_ge, ALU.mult))
                link(nc.vector.scalar_tensor_tensor(tmp[:, 1], g, -1.0, g, ALU.mult, ALU.max))
                link(nc.vector.tensor_scalar(tmp[:, 1], tmp[:, 1], 0.25, None, ALU.max))
                link(nc.vector.scalar_tensor_tensor(out, tmp[:, 0], -1.0, tmp[:, 1], ALU.add, ALU.mult))


def build_attention(nc, x_dram, wq, wk, wv, xt, pbuf, mod, ident, ident_dram, half_neg, bank2, ring, obank):
    with ExitStack() as ctx:
        def sb(name, shape, dt=F32):
            return ctx.enter_context(nc.sbuf_tensor(name, shape, dt))

        def sem(name):
            return ctx.enter_context(nc.semaphore(name))

        wq_sb = sb("wq_sb", [P, H, 2 * R])
        wk_sb = sb("wk_sb", [P, H, R])
        wv_sb = sb("wv_sb", [P, H, D])
        h_tok = sb("h_tok", [P, TB, D])
        hT = sb("hT", [P, N])
        centred = sb("centred", [P, TB, D])
        stats = sb("stats", [P, 4, TB])
        q_hh = [sb(f"q_hh{i}", [P, N], F32R) for i in range(2)]
        q_lm = [sb(f"q_lm{i}", [R + 1, N], F32R) for i in range(2)]
        k_hl = [sb(f"k_hl{i}", [P, N], F32R) for i in range(2)]
        k_h1 = [sb(f"k_h1{i}", [R + 1, N], F32R) for i in range(2)]
        v_one = [sb(f"v_one{i}", [P, TB, D + 1]) for i in range(3)]
        maxes = sb("maxes", [P, 2, TB, 2])
        row_max = sb("row_max", [P, 2, TB])
        neg_max = sb("neg_max", [TB, P], F32R)
        recip = sb("recip", [P, TB])
        acc = sb("acc", [P, TB, D])
        probs = pbuf[:].rearrange("p (s m n) -> p s m n", s=2, m=TB)

        x_loaded = sem("x_loaded")
        w_loaded = sem("w_loaded")
        var_ready = sem("var_ready")
        rstd_ready = sem("rstd_ready")
        h_ready = sem("h_ready")
        hT_ready = sem("hT_ready")
        ring_full = [sem(f"ring_full{r}") for r in range(2)]
        hi_ready = sem("hi_ready")
        lo_ready = sem("lo_ready")
        k2_ready = sem("k2_ready")
        v_ready = sem("v_ready")
        rows_maxed = sem("rows_maxed")
        max_ready = sem("max_ready")
        neg_ready = sem("neg_ready")
        row_ready = sem("row_ready")
        st_full = [sem(f"st_full{r}") for r in range(2)]
        st_free = [sem(f"st_free{r}") for r in range(2)]
        o_full = [sem(f"o_full{r}") for r in range(2)]
        o_read = [sem(f"o_read{r}") for r in range(2)]
        consts = sem("attn_consts")
        steps = sem("attn_steps")
        turns = sem("turns")
        primed = [hT_ready, lo_ready, v_ready, rows_maxed, neg_ready, row_ready, *st_free, *o_read]

        uses = [("t", 0), ("t", 1)]

        def projection_uses(h):
            return [(w, h, k) for w in "qkv" for k in range(2)]

        def row_uses(h, i):
            return [("a", h, i, k) for k in range(2)]

        uses += projection_uses(0)
        for i in range(TB):
            uses += row_uses(0, i)
        uses += [("r", 0)] + projection_uses(1)
        for h in range(H):
            if h + 1 < H:
                for i in range(TB):
                    uses += row_uses(h + 1, i)
                uses += [("r", h + 1)]
            if h + 2 < H:
                uses += projection_uses(h + 2)
        bank_of = {key: n % 2 for n, key in enumerate(uses)}
        turn_of = {key: n // 2 for n, key in enumerate(uses)}
        per_ring = len(uses) // 2
        assert len(uses) % 2 == 0
        steps_per_batch = STEPS_A

        def released(key):
            kind, h = key[0], key[1]
            if kind == "t":
                return hT_ready, 2, h + 1
            if kind in "qk":
                return lo_ready, 4 * H, 4 * h + 2 * (kind == "k") + key[2] + 1
            if kind == "v":
                return v_ready, 2 * H, 2 * h + key[2] + 1
            if kind == "a":
                return rows_maxed, 2 * TB * H, 2 * TB * h + 2 * key[2] + key[3] + 1
            return neg_ready, H, h + 1

        block = ctx.enter_context(nc.Block())

        @block.sync
        def _(sp):
            sp.dma_start(wq_sb[:], wq).then_inc(w_loaded, 16)
            sp.dma_start(wk_sb[:], wk).then_inc(w_loaded, 16)
            sp.dma_start(wv_sb[:], wv).then_inc(w_loaded, 16)
            sp.dma_start(ident[:], ident_dram).then_inc(w_loaded, 16)
            for b in range(B):
                sp.dma_start(xt[:, b * TB:(b + 1) * TB, :], x_dram[:, b * TB:(b + 1) * TB, :]).then_inc(x_loaded, 16)
            with sp.Fori(0, B) as b:
                for h in range(H):
                    sp.wait_ge(neg_ready, b * H + h + 2)
                    for i in range(TB):
                        sp.dma_start(q_lm[h % 2][R:R + 1, i * P:(i + 1) * P].bitcast(F32), neg_max[i:i + 1, :].bitcast(F32)).then_inc(row_ready, 16)

        @block.gpsimd
        def _(pool):
            for s in primed:
                nc.gpsimd.sem_inc(s, 1)
            pool.wait_ge(consts, 6)
            with pool.Fori(0, B) as b:
                pool.wait_ge(var_ready, b + 1)
                nc.gpsimd.tensor_tensor(stats[:, 3, :], stats[:, 2, :], half_neg[:, 0:TB], ALU.pow).then_inc(rstd_ready, 1)
                for h in range(H):
                    pool.wait_ge(hi_ready, (b * H + h) * 4 + 4)
                    if h >= 2:
                        pool.wait_ge(st_full[1], (b * H + h - 1) * (TB // 2))
                    nc.gpsimd.sem_inc(turns, 1)
                    nc.gpsimd.tensor_copy(k_h1[h % 2][0:R, :], k_hl[h % 2][0:R, :].bitcast(F32)).then_inc(k2_ready, 1)

        @block.scalar
        def _(act):
            with act.Fori(0, B) as b:
                def wait_full(key):
                    act.wait_ge(ring_full[bank_of[key]], b * per_ring + turn_of[key] + 1)

                for k in range(2):
                    wait_full(("t", k))
                    nc.scalar.activation(hT[:, k * HALF:(k + 1) * HALF], ring[bank_of[("t", k)]][:], ACT.Copy).then_inc(hT_ready, 1)

                def projections(h):
                    s = h % 2
                    if h >= 2:
                        act.wait_ge(st_full[1], (b * H + h - 1) * (TB // 2))
                    for k in range(2):
                        cols = slice(k * HALF, (k + 1) * HALF)
                        wait_full(("q", h, k))
                        nc.scalar.activation(q_hh[s][:, cols], ring[bank_of[("q", h, k)]][:], ACT.Copy).then_inc(hi_ready, 1)
                    for k in range(2):
                        cols = slice(k * HALF, (k + 1) * HALF)
                        wait_full(("k", h, k))
                        nc.scalar.activation(k_hl[s][0:R, cols], ring[bank_of[("k", h, k)]][0:R, :], ACT.Copy).then_inc(hi_ready, 1)

                def negated_max(h):
                    wait_full(("r", h))
                    act.wait_ge(row_ready, (b * H + h) * 16 * TB + 1)
                    bank = bank_of[("r", h)]
                    nc.scalar.activation(neg_max[:], ring[bank][0:TB, 0:P], ACT.Copy, scale=-1.0).then_inc(neg_ready, 1)

                projections(0)
                negated_max(0)
                projections(1)
                for h in range(H):
                    if h >= 2:
                        act.wait_ge(o_full[1], (b * H + h - 1) * (TB // 2))
                    for i in range(TB):
                        act.wait_ge(st_full[i % 2], (b * H + h) * (TB // 2) + i // 2 + 1)
                        nc.scalar.activation(probs[:, h % 2, i, :], bank2[i % 2][:], ACT.Exp).then_inc(st_free[i % 2], 1)
                        if i == 5 and h + 1 < H:
                            negated_max(h + 1)
                    if h + 2 < H:
                        projections(h + 2)

        @block.vector
        def _(dve):
            nc.vector.memset(half_neg[:], -0.5).then_inc(consts, 1)
            for t in k_h1:
                nc.vector.memset(t[R:R + 1, :].bitcast(F32), 1.0).then_inc(consts, 1)
            for t in v_one:
                nc.vector.memset(t[:, :, D:D + 1], 1.0).then_inc(consts, 1)
            dve.wait_ge(consts, 6)
            with dve.Fori(0, B) as b:
                link = Chain(dve, steps, b * steps_per_batch)

                def wait_full(key):
                    dve.wait_ge(ring_full[bank_of[key]], b * per_ring + turn_of[key] + 1)

                xb = xt[:, bass.ds(b * TB, TB), :]
                dve.wait_ge(x_loaded, 16 * B)
                layernorm(nc, dve, link, xb, centred[:], stats, h_tok[:], mod[:, 1, bass.ds(b, 1), :].rearrange("p o d -> p (o d)").unsqueeze(1).broadcast_to([P, TB, D]),
                          mod[:, 0, bass.ds(b, 1), :].rearrange("p o d -> p (o d)").unsqueeze(1).broadcast_to([P, TB, D]),
                          var_ready, rstd_ready, b + 1).then_inc(h_ready, 1)

                def projections(h):
                    s = h % 2
                    if h >= 2:
                        dve.wait_ge(st_full[1], (b * H + h - 1) * (TB // 2))
                    for w, n0 in (("q", 0), ("k", 2)):
                        for k in range(2):
                            cols = slice(k * HALF, (k + 1) * HALF)
                            bank = bank_of[(w, h, k)]
                            hi, lo = (q_hh[s], q_lm[s][0:R, cols]) if w == "q" else (k_hl[s], k_hl[s][R:P, cols])
                            dve.wait_ge(hi_ready, (b * H + h) * 4 + n0 + k + 1)
                            nc.vector.tensor_tensor(lo, ring[bank][0:R, :], hi[0:R, cols].bitcast(F32), ALU.subtract).then_inc(lo_ready, 1)
                    for k in range(2):
                        wait_full(("v", h, k))
                        bank = bank_of[("v", h, k)]
                        nc.vector.tensor_copy(v_one[h % 3][:, 4 * k:4 * k + 4, 0:D],
                                              ring[bank][:].rearrange("p (m d) -> p m d", m=4)).then_inc(v_ready, 1)

                def row_maxima(h, i):
                    for k in range(2):
                        wait_full(("a", h, i, k))
                        bank = bank_of[("a", h, i, k)]
                        nc.vector.tensor_reduce(maxes[:, h % 2, i, k:k + 1], ring[bank][:], AX.X, ALU.max).then_inc(rows_maxed, 1)

                def whole_max(h):
                    dve.wait_ge(rows_maxed, (b * H + h + 1) * 2 * TB + 1)
                    nc.vector.tensor_tensor(row_max[:, h % 2, :], maxes[:, h % 2, :, 0], maxes[:, h % 2, :, 1], ALU.max).then_inc(max_ready, 1)

                def gather_output(h, i):
                    dve.wait_ge(o_full[i % 2], (b * H + h) * (TB // 2) + i // 2 + 1)
                    o = obank[i % 2]
                    link(nc.vector.reciprocal(recip[:, i:i + 1], o[:, D:D + 1]))
                    dve.wait_ge(o_read[i % 2], (b * H + h) * (TB // 2) + i // 2 + 1)
                    if h == 0:
                        out = nc.vector.tensor_scalar(acc[:, i, :], o[:, 0:D], recip[:, i:i + 1], None, ALU.mult)
                    else:
                        out = nc.vector.scalar_tensor_tensor(acc[:, i, :], o[:, 0:D], recip[:, i:i + 1], acc[:, i, :], ALU.mult, ALU.add)
                    out.then_inc(o_read[i % 2], 1)

                projections(0)
                for i in range(TB):
                    row_maxima(0, i)
                whole_max(0)
                projections(1)
                for h in range(H):
                    for i in range(TB):
                        if h + 1 < H and i < TB // 2:
                            row_maxima(h + 1, 2 * i)
                            row_maxima(h + 1, 2 * i + 1)
                            if i == TB // 2 - 1:
                                whole_max(h + 1)
                        if h >= 1:
                            gather_output(h - 1, i)
                    if h + 2 < H:
                        projections(h + 2)
                for i in range(TB):
                    gather_output(H - 1, i)
                for r in range(2):
                    dve.wait_ge(o_read[r], (b + 1) * (H * TB // 2) + 1)
                gate = mod[:, 2, bass.ds(b, 1), :].rearrange("p o d -> p (o d)").unsqueeze(1).broadcast_to([P, TB, D])
                link(nc.vector.tensor_tensor(acc[:], acc[:], gate, ALU.mult))
                link(nc.vector.tensor_tensor(xb, xb, acc[:], ALU.add))
                assert link.n == steps_per_batch, link.n

        @block.tensor
        def _(pe):
            pe.wait_ge(w_loaded, 64)
            pe.wait_ge(consts, 6)
            with pe.Fori(0, B) as b:
                def take(key):
                    at = uses.index(key) - 2
                    sem_, per_batch, count = released(uses[at])
                    pe.wait_ge(sem_, b * per_batch + (count if at >= 0 else count - per_batch) + 1)
                    return ring[bank_of[key]]

                def give(key, instruction):
                    instruction.then_inc(ring_full[bank_of[key]], 1)

                pe.wait_ge(h_ready, b + 1)
                for k in range(2):
                    bank = take(("t", k))
                    for i in range(4):
                        mm = nc.tensor.transpose(bank[:, i * P:(i + 1) * P], h_tok[:, 4 * k + i, :], ident[:])
                    give(("t", k), mm)
                pe.wait_ge(hT_ready, 2 * b + 3)

                def projections(h):
                    for w, weight in (("q", wq_sb[:, h, :]), ("k", wk_sb[:, h, :])):
                        for k in range(2):
                            bank = take((w, h, k))
                            m = weight.shape[1]
                            give((w, h, k), nc.tensor.matmul(bank[0:m, :], weight, hT[:, k * HALF:(k + 1) * HALF], start=True, stop=True))
                    for k in range(2):
                        bank = take(("v", h, k))
                        for i in range(4):
                            t = 4 * k + i
                            mm = nc.tensor.matmul(bank[:, i * D:(i + 1) * D], hT[:, t * P:(t + 1) * P], wv_sb[:, h, :], start=True, stop=True)
                        give(("v", h, k), mm)

                def score_rows(h, i):
                    s = h % 2
                    if i == 0:
                        pe.wait_ge(lo_ready, (b * H + h) * 4 + 5)
                    for k in range(2):
                        bank = take(("a", h, i, k))
                        give(("a", h, i, k), nc.tensor.matmul(bank[:], q_hh[s][:, i * P:(i + 1) * P], k_hl[s][:, k * HALF:(k + 1) * HALF], start=True, stop=True))

                def max_rows(h):
                    pe.wait_ge(max_ready, b * H + h + 1)
                    bank = take(("r", h))
                    give(("r", h), nc.tensor.transpose(bank[0:TB, 0:P], row_max[:, h % 2, :], ident[:]))

                def scores(h, i):
                    s = h % 2
                    if i == 0:
                        pe.wait_ge(row_ready, (b * H + h + 1) * 16 * TB + 1)
                        pe.wait_ge(k2_ready, b * H + h + 1)
                    pe.wait_ge(st_free[i % 2], (b * H + h) * (TB // 2) + i // 2 + 1)
                    cols = slice(i * P, (i + 1) * P)
                    for k in range(2):
                        half = slice(k * HALF, (k + 1) * HALF)
                        nc.tensor.matmul(bank2[i % 2][:, half], k_hl[s][:, cols], q_hh[s][:, half], start=True, stop=False)
                    for k in range(2):
                        half = slice(k * HALF, (k + 1) * HALF)
                        mm = nc.tensor.matmul(bank2[i % 2][:, half], k_h1[s][:, cols], q_lm[s][:, half], start=False, stop=True)
                    mm.then_inc(st_full[i % 2], 1)

                def products(h, i):
                    if i == 0:
                        for r in range(2):
                            pe.wait_ge(st_free[r], (b * H + h + 1) * (TB // 2) + 1)
                        pe.wait_ge(v_ready, (b * H + h) * 2 + 3)
                    pe.wait_ge(o_read[i % 2], (b * H + h) * (TB // 2) + i // 2 + 1)
                    for m in range(TB):
                        mm = nc.tensor.matmul(obank[i % 2][:, 0:D + 1], probs[:, h % 2, m, i * P:(i + 1) * P], v_one[h % 3][:, m, :],
                                              start=(m == 0), stop=(m == TB - 1))
                    mm.then_inc(o_full[i % 2], 1)

                projections(0)
                for i in range(TB):
                    score_rows(0, i)
                max_rows(0)
                projections(1)
                for h in range(H):
                    for i in range(TB):
                        scores(h, i)
                        if h + 1 < H and i < TB // 2:
                            score_rows(h + 1, 2 * i)
                            score_rows(h + 1, 2 * i + 1)
                        if h >= 1:
                            products(h - 1, i)
                        if i == 5 and h + 1 < H:
                            max_rows(h + 1)
                    if h + 2 < H:
                        projections(h + 2)
                for i in range(TB):
                    products(H - 1, i)


def build_product_key_table(nc, a, xt, hc, mod, ones, half_neg, ident, banks, wide, w_eff, sim_bias, mean_col):
    ntok = TT * P
    with ExitStack() as ctx:
        def sb(name, shape, dt=F32):
            return ctx.enter_context(nc.sbuf_tensor(name, shape, dt))

        def sem(name):
            return ctx.enter_context(nc.semaphore(name))

        wq_sb = sb("pk_wq", [P, G, P])
        wqT = sb("pk_wqT", [P, G, D])
        keysT = sb("keysT", [P, G, NK])
        keys_s = sb("keys_scaled", [P, G, NK])
        gamma = sb("pk_gamma", [P, G])
        beta = sb("pk_beta", [P, G])
        beta_b = sb("beta_b", [P, G, P])
        centred = sb("pk_centred", [P, TB, D])
        stats = sb("pk_stats", [P, 4, TB])
        mean_b = sb("mean_b", [P, D])
        cov = sb("cov", [P, D])
        prod = sb("pk_prod", [P, 4, D])
        var = sb("pk_var", [P, 4, G])
        loaded = sem("pk_loaded")
        var_ready = sem("pk_var_ready")
        rstd_ready = sem("pk_rstd")
        h_ready = sem("pk_h")
        sum_done = sem("pk_sum")
        mean_ready = sem("pk_mean")
        turned = sem("pk_turned")
        hc_ready = sem("pk_hc")
        gram_done = sem("pk_gram")
        cov_ready = sem("pk_cov")
        wc_full = sem("pk_wc_full")
        wc_read = sem("pk_wc_read")
        keys_ready = sem("pk_keys")
        beta_ready = sem("pk_beta_b")
        tables_done = sem("pk_tables")
        steps = sem("pk_steps")
        block = ctx.enter_context(nc.Block())

        @block.sync
        def _(sp):
            for dst, src in ((wq_sb, "w_q"), (wqT, "w_qT"), (keysT, "keysT"), (gamma, "bn_gamma"), (beta, "bn_beta")):
                sp.dma_start(dst[:], a[src]).then_inc(loaded, 16)

        @block.gpsimd
        def _(pool):
            for b in range(B):
                pool.wait_ge(var_ready, b + 1)
                nc.gpsimd.tensor_tensor(stats[:, 3, :], stats[:, 2, :], half_neg[:, 0:TB], ALU.pow).then_inc(rstd_ready, 1)
            pool.wait_ge(var_ready, B + 1)
            nc.gpsimd.tensor_tensor(var[:, 2, :], var[:, 1, :], half_neg[:, 0:G], ALU.pow).then_inc(rstd_ready, 1)

        @block.vector
        def _(dve):
            link = Chain(dve, steps, 0)
            dve.wait_ge(loaded, 80)
            nc.vector.tensor_copy(beta_b[:], spread(beta[:], 2, P)).then_inc(beta_ready, 1)
            for b in range(B):
                tiles = slice(b * TB, (b + 1) * TB)
                layernorm(nc, dve, link, xt[:, tiles, :], centred[:], stats, hc[:, tiles, :], spread(mod[:, 4, b, :], 1, TB),
                          spread(mod[:, 3, b, :], 1, TB), var_ready, rstd_ready, b + 1).then_inc(h_ready, 1)
                dve.wait_ge(h_ready, b + 1)
            dve.wait_ge(sum_done, 1)
            nc.vector.tensor_scalar(mean_b[:], banks[0][:, 0:D], 1.0 / ntok, None, ALU.mult).then_inc(mean_ready, 1)
            dve.wait_ge(mean_ready, 1)
            for b in range(B):
                tiles = slice(b * TB, (b + 1) * TB)
                nc.vector.tensor_tensor(hc[:, tiles, :], hc[:, tiles, :], spread(mean_b[:], 1, TB), ALU.subtract).then_inc(hc_ready, 1)
            dve.wait_ge(turned, 1)
            link(nc.vector.tensor_copy(mean_col[:], banks[1][:, 0:1]))
            dve.wait_ge(gram_done, 1)
            nc.vector.tensor_scalar(cov[:], banks[0][:, 0:D], 1.0 / ntok, None, ALU.mult).then_inc(cov_ready, 1)
            for k in range(4):
                groups = slice(4 * k, 4 * k + 4)
                dve.wait_ge(wc_full, k + 1)
                nc.vector.tensor_tensor(prod[:], banks[2 + k % 2][:].rearrange("p (g d) -> p g d", g=4), wqT[:, groups, :], ALU.mult).then_inc(wc_read, 1)
                dve.wait_ge(wc_read, k + 1)
                link(nc.vector.tensor_reduce(var[:, 0, groups], prod[:], AX.X, ALU.add))
            nc.vector.tensor_scalar(var[:, 1, :], var[:, 0, :], BN_EPS, None, ALU.add).then_inc(var_ready, 1)
            dve.wait_ge(rstd_ready, B + 1)
            link(nc.vector.tensor_tensor(var[:, 3, :], var[:, 2, :], gamma[:], ALU.mult))
            nc.vector.tensor_tensor(keys_s[:], keysT[:], spread(var[:, 3, :], 2, NK), ALU.mult).then_inc(keys_ready, 1)
            dve.wait_ge(tables_done, 1)
            link(nc.vector.tensor_copy(w_eff[:], wide[:, 0:512]))
            dve.wait_ge(tables_done, 2)
            link(nc.vector.tensor_copy(sim_bias[:], wide[:, 512:1024]))

        @block.tensor
        def _(pe):
            for t in range(TT):
                if t % TB == 0:
                    pe.wait_ge(h_ready, t // TB + 1)
                mm = nc.tensor.matmul(banks[0][:, 0:D], ones[:], hc[:, t, :], start=(t == 0), stop=(t == TT - 1))
            mm.then_inc(sum_done, 1)
            pe.wait_ge(mean_ready, 1)
            nc.tensor.transpose(banks[1][:, 0:P], mean_b[:], ident[:]).then_inc(turned, 1)
            for t in range(TT):
                if t % TB == 0:
                    pe.wait_ge(hc_ready, t // TB + 1)
                mm = nc.tensor.matmul(banks[0][:, 0:D], hc[:, t, :], hc[:, t, :], start=(t == 0), stop=(t == TT - 1))
            mm.then_inc(gram_done, 1)
            pe.wait_ge(loaded, 80)
            pe.wait_ge(cov_ready, 1)
            for k in range(4):
                if k >= 2:
                    pe.wait_ge(wc_read, k - 1)
                for g in range(4):
                    mm = nc.tensor.matmul(banks[2 + k % 2][:, g * D:(g + 1) * D], wq_sb[:, 4 * k + g, :], cov[:], start=True, stop=True)
                mm.then_inc(wc_full, 1)
            pe.wait_ge(keys_ready, 1)
            for g in range(G):
                mm = nc.tensor.matmul(wide[:, g * NK:(g + 1) * NK], wqT[:, g, :], keys_s[:, g, :], start=True, stop=True)
            mm.then_inc(tables_done, 1)
            pe.wait_ge(beta_ready, 1)
            for g in range(G):
                mm = nc.tensor.matmul(wide[:, 512 + g * NK:512 + (g + 1) * NK], beta_b[:, g, :], keysT[:, g, :], start=True, stop=True)
            mm.then_inc(tables_done, 1)


PAIRS = TT // 2
STEPS_HOTS = 7


def build_experts(nc, a, pbuf, hc, ident, banks, wide, w_eff, sim_bias, mean_col):
    with ExitStack() as ctx:
        def sb(name, shape, dt=F32):
            return ctx.enter_context(nc.sbuf_tensor(name, shape, dt))

        def sem(name):
            return ctx.enter_context(nc.semaphore(name))

        low_hot = pbuf[:, TT * D:].bitcast(BF16)[:, 0:P * P].rearrange("p (e t) -> p e t", e=P)
        low_ids = sb("low_ids", [P, P, P], BF16)
        count = sb("count", [P, P])
        half_mask = sb("half_mask", [P, 2])
        mask_b = sb("mask_b", [P, 2, P], BF16)
        downT = sb("downT", [P, 1024])
        up = sb("up", [P, 8, D])
        hcT = sb("hcT", [P, 2 * P])
        hT = sb("pk_hT", [P, 2 * P])
        act_g = sb("act_g", [P, 8, 2 * P])
        z = sb("z", [P, 8, 2, P])
        sims = sb("sims", [P, 2, 2, H, NK])
        top = sb("top", [P, 2, 2, H, TOPK])
        top_i = sb("top_i", [P, 2, 2, H, TOPK], U32)
        top_f = sb("top_f", [P, 2, 2 * H, TOPK])
        cand = sb("cand", [P, 2 * H, TOPK, TOPK])
        best = sb("best", [P, 2 * H, TOPK])
        best_i = sb("best_i", [P, 2 * H, TOPK], U32)
        rank_u = sb("rank_u", [P, 2, 2 * H, TOPK], U32)
        rank_f = sb("rank_f", [P, 2, 2 * H, TOPK])
        hot = sb("hot", [P, 2 * H * TOPK, TOPK])
        chosen = sb("chosen", [P, 2, 2 * H * TOPK])
        chosen_u = sb("chosen_u", [P, 3, 2 * H * TOPK], U32)
        to_turn = sb("to_turn", [P, 3, P])
        expd = sb("expd", [P, 2 * H, TOPK])
        tot = sb("tot", [P, 2, 2 * H])
        ids = sb("ids", [P, 2, P], BF16)
        rest = sb("rest", [P, 2, P])
        parts = sb("parts", [P, 3, P], BF16)
        parts_m = sb("parts_m", [P, 3, 2, P], BF16)
        high_hot = sb("high_hot", [P, 8, P], BF16)
        value_hot = sb("value_hot", [P, 6, 8, P], BF16)

        hc_stage = sb("hc_stage", [P, 2, D])
        loaded = sem("ex_loaded")
        stage_ready = sem("ex_stage")
        turns = sem("ex_turns")
        apart = sem("ex_apart")
        consts = sem("ex_consts")
        steps = sem("ex_steps")
        turned_h = sem("ex_turned_h")
        hT_ready = sem("ex_hT")
        sims_full = sem("ex_sims_full")
        sims_read = sem("ex_sims_read")
        less_max = sem("ex_less_max")
        exp_done = sem("ex_exp")
        to_turn_ready = sem("ex_to_turn")
        turned = sem("ex_turned")
        ids_ready = sem("ex_ids")
        hots_ready = sem("ex_hots")
        g_full = sem("ex_g_full")
        g_ready = sem("ex_g_ready")
        w_full = sem("ex_w_full")
        z_ready = sem("ex_z")
        out_full = sem("ex_out_full")
        out_read = sem("ex_out_read")
        sim_bank = [banks[2], banks[3]]
        turn_bank, h_bank = banks[0], banks[1]
        block = ctx.enter_context(nc.Block())

        @block.sync
        def _(sp):
            sp.dma_start(count[:], a["count"]).then_inc(loaded, 16)
            sp.dma_start(half_mask[:], a["half_mask"]).then_inc(loaded, 16)
            sp.dma_start(downT[:], a["downT"]).then_inc(loaded, 16)
            sp.dma_start(up[:], a["up"]).then_inc(loaded, 16)


        @block.scalar
        def _(act):
            def front(u):
                act.wait_ge(turned_h, u + 1)
                nc.scalar.activation(hcT[:], h_bank[:, 0:2 * P], ACT.Copy).then_inc(hT_ready, 1)
                nc.scalar.activation(hT[:], h_bank[:, 0:2 * P], ACT.Identity, bias=mean_col[:]).then_inc(hT_ready, 1)
                act.wait_ge(less_max, u + 1)
                nc.scalar.activation(expd[:], expd[:], ACT.Exp).then_inc(exp_done, 1)

            def activations(u):
                for k in range(2):
                    act.wait_ge(g_full, 2 * u + k + 1)
                    nc.scalar.activation(act_g[:, 4 * k:4 * k + 4, :], wide[k][:].rearrange("p (e t) -> p e t", e=4),
                                         ACT.Gelu_apprx_tanh).then_inc(g_ready, 1)

            def back(u):
                act.wait_ge(out_full, u + 1)
                nc.scalar.activation(hc[:, bass.ds(2 * u, 2), :], sim_bank[0][:, 0:256].rearrange("p (q d) -> p q d", q=2), ACT.Copy).then_inc(out_read, 1)

            act.wait_ge(loaded, 64)
            nc.scalar.sem_inc(out_read, 1)
            front(0)
            with act.Fori(0, PAIRS - 1) as u:
                activations(u)
                front(u + 1)
                back(u)
            activations(PAIRS - 1)
            back(PAIRS - 1)

        @block.vector
        def _(dve):
            def front(u, base):
                link = Chain(dve, steps, base)
                for q in range(2):
                    dve.wait_ge(sims_full, 2 * u + q + 1)
                    nc.vector.tensor_tensor(sims[:, q].rearrange("p s h k -> p (s h k)"), sim_bank[q][:], sim_bias[:], ALU.add).then_inc(sims_read, 1)
                    dve.wait_ge(sims_read, 2 * u + q + 1)
                nc.vector.sem_inc(apart, 1)
                for q in range(2):
                    for s in range(2):
                        for h in range(H):
                            last = nc.vector.max(top[:, s, q, h, :], sims[:, q, s, h, :])
                link(last)
                nc.vector.sem_inc(apart, 1)
                for q in range(2):
                    for s in range(2):
                        for h in range(H):
                            last = nc.vector.max_index(top_i[:, s, q, h, :], top[:, s, q, h, :], sims[:, q, s, h, :])
                link(last)
                topv = top[:].rearrange("p s q h k -> p s (q h) k")
                nc.vector.tensor_copy(top_f[:], top_i[:].rearrange("p s q h k -> p s (q h) k")).then_inc(steps, 1)
                link.n += 1
                link(nc.vector.tensor_tensor(cand[:], spread(topv[:, 0], 3, TOPK), spread(topv[:, 1], 2, TOPK), ALU.add))
                nc.vector.sem_inc(apart, 1)
                for g in range(2 * H):
                    last = nc.vector.max(best[:, g, :], cand[:, g].rearrange("p i j -> p (i j)"))
                link(last)
                nc.vector.sem_inc(apart, 1)
                for g in range(2 * H):
                    last = nc.vector.max_index(best_i[:, g, :], best[:, g, :], cand[:, g].rearrange("p i j -> p (i j)"))
                link(last)
                nc.vector.tensor_tensor(expd[:], best[:], spread(best[:, :, 0], 2, TOPK), ALU.subtract).then_inc(less_max, 1)
                nc.vector.tensor_scalar(rank_u[:, 0], best_i[:], 3, None, ALU.logical_shift_right).then_inc(steps, 1)
                link.n += 1
                link(nc.vector.tensor_scalar(rank_u[:, 1], best_i[:], 7, None, ALU.bitwise_and))
                link(nc.vector.tensor_copy(rank_f[:], rank_u[:]))
                for s in range(2):
                    rank = rank_f[:, s].rearrange("p g k -> p (g k)")
                    hot4 = hot[:].rearrange("p (g k) j -> p g k j", g=2 * H)
                    link(nc.vector.tensor_tensor(hot[:], spread(rank, 2, TOPK), spread(count[:, 0:TOPK], 1, 2 * H * TOPK), ALU.is_equal))
                    link(nc.vector.tensor_tensor(hot4, hot4, spread(top_f[:, s], 2, TOPK), ALU.mult))
                    link(nc.vector.tensor_reduce(chosen[:, s, :], hot[:], AX.X, ALU.add))
                link(nc.vector.tensor_copy(chosen_u[:, 0, :], chosen[:, 0, :]))
                nc.vector.tensor_scalar(chosen_u[:, 1, :], chosen_u[:, 0, :], 3, 5, ALU.bitwise_and, ALU.logical_shift_left).then_inc(steps, 1)
                link.n += 1
                link(nc.vector.tensor_scalar(chosen_u[:, 2, :], chosen_u[:, 0, :], 2, None, ALU.logical_shift_right))
                nc.vector.tensor_tensor(to_turn[:, 0, :], chosen_u[:, 1, :], chosen[:, 1, :], ALU.add).then_inc(steps, 1)
                link.n += 1
                link(nc.vector.tensor_copy(to_turn[:, 1, :], chosen_u[:, 2, :]))
                dve.wait_ge(exp_done, u + 1)
                link(nc.vector.tensor_reduce(tot[:, 0, :], expd[:], AX.X, ALU.add))
                link(nc.vector.reciprocal(tot[:, 1, :], tot[:, 0, :]))
                nc.vector.tensor_tensor(to_turn[:, 2, :].rearrange("p (g k) -> p g k", g=2 * H), expd[:],
                                        spread(tot[:, 1, :], 2, TOPK), ALU.mult).then_inc(to_turn_ready, 1)
                return link.n

            def one_hots(u, base):
                link = Chain(dve, steps, base)
                dve.wait_ge(turned, u + 1)
                turned_w = turn_bank[:, 256:384]
                link(nc.vector.tensor_copy(ids[:], turn_bank[:, 0:256].rearrange("p (s t) -> p s t", s=2)))
                link(nc.vector.tensor_copy(parts[:, 0, :], turned_w))
                link(nc.vector.tensor_tensor(rest[:, 0, :], turned_w, parts[:, 0, :], ALU.subtract))
                link(nc.vector.tensor_copy(parts[:, 1, :], rest[:, 0, :]))
                link(nc.vector.tensor_tensor(rest[:, 1, :], rest[:, 0, :], parts[:, 1, :], ALU.subtract))
                nc.vector.tensor_copy(parts[:, 2, :], rest[:, 1, :]).then_inc(ids_ready, 1)
                dve.wait_ge(ids_ready, u + 1)
                nc.vector.tensor_tensor(high_hot[:], spread(ids[:, 1, :], 1, 8), low_ids[:, 0:8, :], ALU.is_equal).then_inc(steps, 1)
                link.n += 1
                link(nc.vector.tensor_tensor(parts_m[:], spread(parts[:], 2, 2), spread(mask_b[:], 1, 3), ALU.mult))
                nc.vector.tensor_tensor(value_hot[:], spread(high_hot[:], 1, 6),
                                        spread(parts_m[:].rearrange("p s q t -> p (s q) t"), 2, 8), ALU.mult).then_inc(hots_ready, 1)
                nc.vector.tensor_tensor(low_hot, spread(ids[:, 0, :], 1, P), low_ids[:], ALU.is_equal).then_inc(hots_ready, 1)
                return link.n

            def weigh(u):
                dve.wait_ge(g_ready, 2 * u + 2)
                for k in range(4):
                    dve.wait_ge(w_full, 4 * u + k + 1)
                    tok = slice(32 * k, 32 * k + 32)
                    w = wide[k // 2][:, 512 * (k % 2):512 * (k % 2) + 512].rearrange("p (t q e) -> p q e t", q=2, e=8)
                    for q in range(2):
                        nc.vector.tensor_tensor(z[:, :, q, tok], w[:, q], act_g[:].rearrange("p e (q t) -> p e q t", q=2)[:, :, q, tok],
                                                ALU.mult).then_inc(z_ready, 1)

            dve.wait_ge(loaded, 64)
            nc.vector.tensor_copy(low_ids[:], spread(count[:], 2, P)).then_inc(consts, 1)
            nc.vector.tensor_copy(mask_b[:], spread(half_mask[:], 2, P)).then_inc(consts, 1)
            dve.wait_ge(consts, 2)
            n_front = front(0, 0)
            n_all = n_front + STEPS_HOTS
            with dve.Fori(0, PAIRS - 1) as u:
                base = u * n_all + n_front
                n = one_hots(u, base)
                assert n == STEPS_HOTS, n
                assert front(u + 1, base + n) == n_front
                weigh(u)
            one_hots(PAIRS - 1, (PAIRS - 1) * n_all + n_front)
            weigh(PAIRS - 1)

        @block.tensor
        def _(pe):
            def front(u):
                again = not isinstance(u, int)
                for q in range(2):
                    if not again:
                        src = hc[:, 2 * u + q, :]
                    else:
                        src = hc_stage[:, q, :]
                    mm = nc.tensor.transpose(h_bank[:, q * P:(q + 1) * P], src, ident[:])
                mm.then_inc(turned_h, 1)
                pe.wait_ge(hT_ready, 2 * u + 1)
                if again:
                    pe.wait_ge(out_read, u)
                for q in range(2):
                    nc.tensor.matmul(sim_bank[q][:], hcT[:, q * P:(q + 1) * P], w_eff[:], start=True, stop=True).then_inc(sims_full, 1)

            def activations(u):
                pe.wait_ge(hT_ready, 2 * u + 2)
                for k in range(2):
                    for e in range(4):
                        col = (4 * k + e) * P
                        mm = nc.tensor.matmul(wide[k][:, e * 2 * P:(e + 1) * 2 * P], downT[:, col:col + P], hT[:], start=True, stop=True)
                    mm.then_inc(g_full, 1)

            def turn(u):
                pe.wait_ge(to_turn_ready, u + 1)
                for s in range(3):
                    mm = nc.tensor.transpose(turn_bank[:, s * P:(s + 1) * P], to_turn[:, s, :], ident[:])
                mm.then_inc(turned, 1)

            def expert_weights(u):
                pe.wait_ge(hots_ready, 2 * u + 2)
                pe.wait_ge(g_ready, 2 * u + 2)
                for t in range(P):
                    col = 512 * (t // 32 % 2) + 16 * (t % 32)
                    for part in range(3):
                        mm = nc.tensor.matmul(wide[t // 64][:, col:col + 16], low_hot[:, :, t],
                                              value_hot[:, 2 * part:2 * part + 2, :, t].rearrange("p q e -> p (q e)"),
                                              start=(part == 0), stop=(part == 2))
                    if t % 32 == 31:
                        mm.then_inc(w_full, 1)

            def combine(u):
                pe.wait_ge(z_ready, 8 * u + 8)
                pe.wait_ge(sims_read, 2 * min(u + 2, PAIRS) if isinstance(u, int) else 2 * u + 4)
                for q in range(2):
                    for e in range(8):
                        mm = nc.tensor.matmul(sim_bank[0][:, q * D:(q + 1) * D], z[:, e, q, :], up[:, e, :], start=(e == 0), stop=(e == 7))
                mm.then_inc(out_full, 1)

            pe.wait_ge(loaded, 64)
            front(0)
            with pe.Fori(0, PAIRS - 1) as u:
                turn(u)
                activations(u)
                pe.wait_ge(stage_ready, u + 1)
                front(u + 1)
                expert_weights(u)
                combine(u)
            turn(PAIRS - 1)
            activations(PAIRS - 1)
            expert_weights(PAIRS - 1)
            combine(PAIRS - 1)

        @block.gpsimd
        def _(pool):
            with pool.Fori(0, PAIRS - 1) as u:
                pool.wait_ge(turned_h, u + 1)
                nc.gpsimd.sem_inc(turns, 1)
                nc.gpsimd.tensor_copy(hc_stage[:], hc[:, bass.ds(2 * u + 2, 2), :]).then_inc(stage_ready, 1)


STEPS_SCAN = 24


def build_second_layer(nc, a, xt, hc, gate0, mod, ident, half_neg, ring, obank, wide, out):
    with ExitStack() as ctx:
        def sb(name, shape, dt=F32):
            return ctx.enter_context(nc.sbuf_tensor(name, shape, dt))

        def sem(name):
            return ctx.enter_context(nc.semaphore(name))

        w_qkva = sb("w_qkva", [P, 3 * D])
        w_rkv = sb("w_rkv", [P, 3, D])
        cols = sb("cols", [P, 4])
        centred = sb("l1_centred", [P, TB, D])
        stats = sb("l1_stats", [P, 4, TB])
        norms = sb("norms", [P, 4, TB])
        half_pos = sb("half_pos", [P, TB])
        h_tok = sb("l1_h", [P, TB, D])
        xnT = sb("xnT", [P, N])
        decay = sb("decay", [P, N])
        y = sb("y", [P, N])
        shifted = sb("shifted", [P, N + 1])
        diff = sb("diff", [P, N])
        mixed = [sb(f"mixed{i}", [P, N]) for i in range(2)]
        rgate = sb("rgate", [P, N])
        kact = sb("kact", [P, N])
        loaded = sem("l1_loaded")
        consts = sem("l1_consts")
        steps = sem("l1_steps")
        var_ready = sem("l1_var")
        rstd_ready = sem("l1_rstd")
        h_ready = sem("l1_h_ready")
        turned = sem("l1_turned")
        hT_ready = sem("l1_hT")
        qkva_full = sem("l1_qkva")
        decay_ready = sem("l1_decay")
        y_ready = sem("l1_y")
        back_full = sem("l1_back")
        back_read = sem("l1_back_read")
        mixed_ready = sem("l1_mixed")
        rk_full = sem("l1_rk")
        rk_ready = sem("l1_rk_ready")
        kact_ready = sem("l1_kact")
        v_full = sem("l1_v")
        rv_ready = sem("l1_rv")
        x_ready = sem("l1_x")
        apart = sem("l1_apart")
        stored = sem("stored")
        block = ctx.enter_context(nc.Block())

        @block.sync
        def _(sp):
            sp.dma_start(w_qkva[:], a["w_qkva"]).then_inc(loaded, 16)
            sp.dma_start(w_rkv[:], a["w_rkv"]).then_inc(loaded, 16)
            sp.dma_start(cols[:, 0:3], a["cols"]).then_inc(loaded, 16)
            with sp.Fori(0, B) as b:
                sp.wait_ge(x_ready, b + 1)
                sp.dma_start(out[:, bass.ds(b * TB, TB), :], xt[:, bass.ds(b * TB, TB), :]).then_inc(stored, 16)
            sp.wait_ge(stored, 16 * B)

        @block.gpsimd
        def _(pool):
            pool.wait_ge(consts, 3)
            with pool.Fori(0, B) as b:
                pool.wait_ge(var_ready, 3 * b + 1)
                nc.gpsimd.tensor_tensor(stats[:, 3, :], stats[:, 2, :], half_neg[:, 0:TB], ALU.pow).then_inc(rstd_ready, 1)
                pool.wait_ge(var_ready, 3 * b + 2)
                nc.gpsimd.tensor_tensor(norms[:, 1, :], norms[:, 0, :], half_pos[:], ALU.pow).then_inc(rstd_ready, 1)
                pool.wait_ge(var_ready, 3 * b + 3)
                nc.gpsimd.tensor_tensor(stats[:, 3, :], stats[:, 2, :], half_neg[:, 0:TB], ALU.pow).then_inc(rstd_ready, 1)
                pool.wait_ge(rk_ready, 4 * b + 4)
                nc.gpsimd.tensor_tensor(kact[:], kact[:], kact[:], ALU.mult).then_inc(kact_ready, 1)

        @block.scalar
        def _(act):
            act.wait_ge(consts, 3)
            with act.Fori(0, B) as b:
                for k in range(2):
                    half = slice(k * HALF, (k + 1) * HALF)
                    act.wait_ge(turned, 4 * b + k + 1)
                    nc.scalar.activation(xnT[:, half], ring[k][:], ACT.Copy, scale=cols[:, 3:4]).then_inc(hT_ready, 1)
                for k in range(2):
                    half = slice(k * HALF, (k + 1) * HALF)
                    act.wait_ge(qkva_full, 2 * b + k + 1)
                    nc.scalar.activation(decay[:, half], obank[k][:], ACT.Sigmoid).then_inc(decay_ready, 1)
                for k in range(2):
                    act.wait_ge(turned, 4 * b + k + 3)
                    nc.scalar.activation(shifted[:, 1 + k * HALF:1 + (k + 1) * HALF], ring[k][:], ACT.Copy).then_inc(hT_ready, 1)
                for k in range(2):
                    half = slice(k * HALF, (k + 1) * HALF)
                    act.wait_ge(rk_full, 2 * b + k + 1)
                    nc.scalar.activation(kact[:, half], wide[1][:, half], ACT.Relu).then_inc(rk_ready, 1)
                    nc.scalar.activation(rgate[:, half], wide[0][:, half], ACT.Sigmoid).then_inc(rk_ready, 1)

        @block.vector
        def _(dve):
            nc.vector.memset(half_pos[:], 0.5).then_inc(consts, 1)
            nc.vector.memset(shifted[:, 0:1], 0.0).then_inc(consts, 1)
            dve.wait_ge(loaded, 48)
            nc.vector.tensor_scalar(cols[:, 3:4], cols[:, 0:1], float(D) ** 0.5, None, ALU.mult).then_inc(consts, 1)
            with dve.Fori(0, B) as b:
                link = Chain(dve, steps, b * STEPS_SCAN)
                xb = xt[:, bass.ds(b * TB, TB), :]

                def row(m):
                    return spread(m[:, bass.ds(b, 1), :].rearrange("p o d -> p (o d)"), 1, TB)

                link(nc.vector.tensor_tensor(centred[:], hc[:, bass.ds(b * TB, TB), :], row(gate0), ALU.mult))
                link(nc.vector.tensor_tensor(xb, xb, centred[:], ALU.add))
                nc.vector.sem_inc(apart, 1)
                link(layernorm(nc, dve, link, xb, centred[:], stats, h_tok[:], row(mod[:, 1]), row(mod[:, 0]), var_ready, rstd_ready, 3 * b + 1))
                link(nc.vector.tensor_tensor(centred[:], h_tok[:], h_tok[:], ALU.mult))
                nc.vector.tensor_reduce(norms[:, 0, :], centred[:], AX.X, ALU.add).then_inc(var_ready, 1)
                dve.wait_ge(rstd_ready, 3 * b + 2)
                link(nc.vector.tensor_scalar(norms[:, 2, :], norms[:, 1, :], NORM_EPS, None, ALU.max))
                link(nc.vector.reciprocal(norms[:, 3, :], norms[:, 2, :]))
                nc.vector.tensor_tensor(h_tok[:], h_tok[:], spread(norms[:, 3, :], 2, D), ALU.mult).then_inc(h_ready, 1)
                for k in range(2):
                    half = slice(k * HALF, (k + 1) * HALF)
                    dve.wait_ge(decay_ready, 2 * b + k + 1)
                    link(nc.vector.tensor_tensor_scan(y[:, half], decay[:, half], wide[1][:, half], 0.0 if k == 0 else y[:, HALF - 1:HALF], ALU.mult, ALU.add))
                for k in range(2):
                    half = slice(k * HALF, (k + 1) * HALF)
                    nc.vector.tensor_tensor(y[:, half], y[:, half], wide[0][:, half], ALU.mult).then_inc(y_ready, 1)
                for k in range(2):
                    tiles = slice(4 * k, 4 * k + 4)
                    dve.wait_ge(back_full, 4 * b + k + 1)
                    nc.vector.tensor_tensor(centred[:, tiles, :], ring[k][:].rearrange("p (t d) -> p t d", t=4), row(mod[:, 2])[:, tiles, :], ALU.mult).then_inc(back_read, 1)
                dve.wait_ge(back_read, 4 * b + 2)
                link(nc.vector.tensor_tensor(xb, xb, centred[:], ALU.add))
                nc.vector.sem_inc(apart, 1)
                layernorm(nc, dve, link, xb, centred[:], stats, h_tok[:], row(mod[:, 4]), row(mod[:, 3]), var_ready, rstd_ready, 3 * b + 3).then_inc(h_ready, 1)
                dve.wait_ge(hT_ready, 4 * b + 4)
                link(nc.vector.tensor_tensor(diff[:], shifted[:, 1:], shifted[:, 0:N], ALU.subtract))
                for i in range(2):
                    nc.vector.scalar_tensor_tensor(mixed[i][:], diff[:], cols[:, 1 + i:2 + i], shifted[:, 0:N], ALU.mult, ALU.add).then_inc(mixed_ready, 1)
                for k in range(2):
                    half = slice(k * HALF, (k + 1) * HALF)
                    dve.wait_ge(v_full, 2 * b + k + 1)
                    nc.vector.tensor_tensor(rgate[:, half], rgate[:, half], obank[k][:], ALU.mult).then_inc(rv_ready, 1)
                for k in range(2):
                    tiles = slice(4 * k, 4 * k + 4)
                    dve.wait_ge(back_full, 4 * b + k + 3)
                    nc.vector.tensor_tensor(centred[:, tiles, :], ring[k][:].rearrange("p (t d) -> p t d", t=4), row(mod[:, 5])[:, tiles, :], ALU.mult).then_inc(back_read, 1)
                dve.wait_ge(back_read, 4 * b + 4)
                nc.vector.tensor_tensor(xb, xb, centred[:], ALU.add).then_inc(x_ready, 1)
                dve.wait_ge(x_ready, b + 1)
                assert link.n == STEPS_SCAN, link.n

        @block.tensor
        def _(pe):
            pe.wait_ge(loaded, 48)
            with pe.Fori(0, B) as b:
                def turn(n):
                    for k in range(2):
                        for i in range(4):
                            mm = nc.tensor.transpose(ring[k][:, i * P:(i + 1) * P], h_tok[:, 4 * k + i, :], ident[:])
                        mm.then_inc(turned, 1)

                def turn_back(src, ready, n):
                    for k in range(2):
                        pe.wait_ge(ready, 2 * b + k + 1)
                        for i in range(4):
                            t = 4 * k + i
                            mm = nc.tensor.transpose(ring[k][:, i * P:(i + 1) * P], src[:, t * P:(t + 1) * P], ident[:])
                        mm.then_inc(back_full, 1)

                pe.wait_ge(h_ready, 2 * b + 1)
                turn(0)
                for k in range(2):
                    half = slice(k * HALF, (k + 1) * HALF)
                    pe.wait_ge(hT_ready, 4 * b + k + 1)
                    for j, bank in enumerate((wide[0][:, half], wide[1][:, half], obank[k][:])):
                        mm = nc.tensor.matmul(bank, w_qkva[:, j * D:(j + 1) * D], xnT[:, half], start=True, stop=True)
                    mm.then_inc(qkva_full, 1)
                turn_back(y, y_ready, 0)
                pe.wait_ge(h_ready, 2 * b + 2)
                turn(1)
                pe.wait_ge(mixed_ready, 2 * b + 2)
                for k in range(2):
                    half = slice(k * HALF, (k + 1) * HALF)
                    for i in range(2):
                        mm = nc.tensor.matmul(wide[i][:, half], w_rkv[:, i, :], mixed[i][:, half], start=True, stop=True)
                    mm.then_inc(rk_full, 1)
                pe.wait_ge(kact_ready, b + 1)
                for k in range(2):
                    half = slice(k * HALF, (k + 1) * HALF)
                    nc.tensor.matmul(obank[k][:], w_rkv[:, 2, :], kact[:, half], start=True, stop=True).then_inc(v_full, 1)
                turn_back(rgate, rv_ready, 1)


def build(nc, args, out):
    with ExitStack() as ctx:
        def sb(name, shape, dt=F32):
            return ctx.enter_context(nc.sbuf_tensor(name, shape, dt))

        bank2 = [ctx.enter_context(nc.psum_tensor(f"bank2_{i}", [P, N], F32)) for i in range(2)]
        ring = [ctx.enter_context(nc.psum_tensor(f"ring{i}", [P, 512], F32)) for i in range(2)]
        obank = [ctx.enter_context(nc.psum_tensor(f"obank{i}", [P, 512], F32)) for i in range(2)]
        xt = sb("xt", [P, TT, D])
        pbuf = sb("pbuf", [P, 2 * TB * N])
        gate0 = sb("gate0", [P, B, D])
        ident = sb("ident_sb", [P, P])
        ones = sb("ones", [P, P])
        half_neg = sb("half_neg", [P, TT])
        w_eff = sb("w_eff", [P, G * NK])
        sim_bias = sb("sim_bias", [P, G * NK])
        mean_col = sb("mean_col", [P, 1])
        hc = pbuf[:, 0:TT * D].rearrange("p (t d) -> p t d", t=TT)
        with nc.sbuf_tensor("mod0", [P, 6, B, D], F32) as mod:
            build_modulation(nc, 0, args["c0"], args["wmod0"], mod, gate0[:], ones,
                             bank2)
            build_attention(nc, args["x"], args["wq"], args["wk"], args["wv"], xt, pbuf, mod, ident,
                            args["ident"], half_neg, bank2, ring, obank)
            build_product_key_table(nc, args, xt, hc, mod, ones, half_neg, ident, ring + obank, bank2[0],
                                    w_eff, sim_bias, mean_col)
        build_experts(nc, args, pbuf, hc, ident, ring + obank, bank2, w_eff, sim_bias, mean_col)
        with nc.sbuf_tensor("mod1", [P, 6, B, D], F32) as mod:
            build_modulation(nc, 1, args["c1"], args["wmod1"], mod, mod[:, 5], None, bank2)
            build_second_layer(nc, args, xt, hc, gate0, mod, ident, half_neg, ring, obank, bank2, out)


def kernel(**inputs):
    import numpy as np
    import concourse.bacc as bacc
    from concourse import mybir
    from concourse.bass_utils import run_bass_kernel_spmd as run

    a = {k: np.asarray(v) for k, v in inputs.items()}
    lay = {
        "x": a["L0_attn_x"].reshape(64, 128, 128).transpose(1, 0, 2),
        "wq": np.concatenate([a["L0_attn_Wq"].reshape(8, 64, 128)] * 2, axis=1).transpose(2, 0, 1),
        "wk": a["L0_attn_Wk"].reshape(8, 64, 128).transpose(2, 0, 1),
        "wv": a["L0_attn_Wv"].reshape(8, 128, 128).transpose(2, 0, 1),
        "c0": a["L0_c"].T,
        "wmod0": a["L0_wmod"],
        "c1": a["L1_c"].T,
        "wmod1": a["L1_wmod"],
        "w_qkva": a["L1_attn_W_qkva"].T,
        "w_rkv": np.stack([a["L1_ffn_W_r"].T, a["L1_ffn_W_k"].T, a["L1_ffn_W_v"].T], axis=1),
        "cols": np.stack([a["L1_attn_gamma"], a["L1_ffn_mu_r"], a["L1_ffn_mu_k"]], axis=1),
        "w_q": a["L0_ffn_w_q"].reshape(128, 16, 128),
        "w_qT": a["L0_ffn_w_q"].reshape(128, 16, 128).transpose(2, 1, 0),
        "keysT": a["L0_ffn_keys"].transpose(3, 2, 0, 1).reshape(128, 16, 32),
        "bn_gamma": a["L0_ffn_bn_gamma"].reshape(16, 128).T,
        "bn_beta": a["L0_ffn_bn_beta"].reshape(16, 128).T,
        "downT": a["L0_ffn_down_embed"].T,
        "up": a["L0_ffn_up_embed"].reshape(8, 128, 128).transpose(1, 0, 2),
        "count": np.broadcast_to(np.arange(128, dtype=np.float32), (128, 128)),
        "half_mask": np.kron(np.eye(2, dtype=np.float32), np.ones((64, 1), np.float32)),
        "ident": np.eye(128, dtype=np.float32),
    }
    nc = bacc.Bacc("TRN2", target_bir_lowering=False, num_devices=1)
    arrays, args = {}, {}
    for name, v in lay.items():
        v = np.ascontiguousarray(v)
        arrays[f"in_{name}"] = v
        args[name] = nc.dram_tensor(f"in_{name}", v.shape, mybir.dt.from_np(v.dtype), kind="ExternalInput").ap()
    out = nc.dram_tensor("out_x", (128, 64, 128), mybir.dt.float32, kind="ExternalOutput").ap()
    build(nc, args, out)
    r = run(nc, [arrays], core_ids=[0])
    return r.results[0]["out_x"].transpose(1, 0, 2).reshape(8, 1024, 128)
```

```python
from contextlib import ExitStack

import concourse.bass as bass
from concourse import mybir

P = 128
B, N, D = 8, 1024, 128
TB = N // P
TT = B * TB
H, R = 8, 64
G = 16
NK, TOPK = 32, 8
STEPS_LOOP = 79
LN_EPS, BN_EPS, NORM_EPS = 1e-5, 1e-5, 1e-12
HALF = N // 2

ALU = mybir.AluOpType
ACT = mybir.ActivationFunctionType
AX = mybir.AxisListType
F32 = mybir.dt.float32
F32R = mybir.dt.float32r
BF16 = mybir.dt.bfloat16
U32 = mybir.dt.uint32


def spread(ap, axis, count):
    ap = ap.unsqueeze(axis)
    shape = list(ap.shape)
    shape[axis] = count
    return ap.broadcast_to(shape)


class Chain:

    def __init__(self, eng, sem, base):
        self.eng, self.sem, self.base, self.n = eng, sem, base, 0

    def __call__(self, instruction):
        self.n += 1
        instruction.then_inc(self.sem, 1)
        self.eng.wait_ge(self.sem, self.base + self.n)


def layernorm(nc, dve, link, src, centred, stats, dst, scale, shift, var_ready, rstd_ready, n):
    tiles = src.shape[1]
    link(nc.vector.tensor_reduce(stats[:, 0, 0:tiles], src, AX.X, ALU.add))
    link(nc.vector.tensor_scalar(stats[:, 0, 0:tiles], stats[:, 0, 0:tiles], 1.0 / D, None, ALU.mult))
    link(nc.vector.tensor_tensor(centred, src, spread(stats[:, 0, 0:tiles], 2, D), ALU.subtract))
    link(nc.vector.tensor_tensor(dst, centred, centred, ALU.mult))
    link(nc.vector.tensor_reduce(stats[:, 1, 0:tiles], dst, AX.X, ALU.add))
    nc.vector.tensor_scalar(stats[:, 2, 0:tiles], stats[:, 1, 0:tiles], 1.0 / D, LN_EPS,
                            ALU.mult, ALU.add).then_inc(var_ready, 1)
    dve.wait_ge(rstd_ready, n)
    link(nc.vector.tensor_tensor(centred, centred, spread(stats[:, 3, 0:tiles], 2, D), ALU.mult))
    link(nc.vector.tensor_tensor(centred, centred, scale, ALU.mult))
    return nc.vector.tensor_tensor(dst, centred, shift, ALU.add)


def build_modulation(nc, tag, cT, wmod, mod, last_gate, ones, banks):
    with ExitStack() as ctx:
        c_sb = ctx.enter_context(nc.sbuf_tensor(f"c_sb{tag}", [P, B], F32))
        w_sb = ctx.enter_context(nc.sbuf_tensor(f"wmod_sb{tag}", [P, 6 * D], F32))
        e_sb = ctx.enter_context(nc.sbuf_tensor(f"e_sb{tag}", [P, 3, B], F32))
        scb = ctx.enter_context(nc.sbuf_tensor(f"scb{tag}", [P, B, P], F32))
        tmp = ctx.enter_context(nc.sbuf_tensor(f"gate_tmp{tag}", [P, 2, B, D], F32))
        loaded = ctx.enter_context(nc.semaphore(f"mod_loaded{tag}"))
        exp_done = ctx.enter_context(nc.semaphore(f"mod_exp{tag}"))
        silu_ready = ctx.enter_context(nc.semaphore(f"mod_silu{tag}"))
        bank_full = ctx.enter_context(nc.semaphore(f"mod_full{tag}"))
        bank_free = ctx.enter_context(nc.semaphore(f"mod_free{tag}"))
        steps = ctx.enter_context(nc.semaphore(f"mod_steps{tag}"))
        block = ctx.enter_context(nc.Block())

        @block.sync
        def _(sp):
            sp.dma_start(c_sb[:], cT).then_inc(loaded, 16)
            sp.dma_start(w_sb[:], wmod).then_inc(loaded, 16)

        @block.scalar
        def _(act):
            act.wait_ge(loaded, 32)
            nc.scalar.activation(e_sb[:, 0, :], c_sb[:], ACT.Exp, scale=-1.0).then_inc(exp_done, 1)

        @block.tensor
        def _(pe):
            pe.wait_ge(loaded, 32)
            pe.wait_ge(silu_ready, 1)
            for b in range(B):
                if b >= 2:
                    pe.wait_ge(bank_free, b - 1)
                for k in range(2):
                    mm = nc.tensor.matmul(banks[b % 2][:, k * 512:k * 512 + 384], scb[:, b, :],
                                          w_sb[:, k * 384:(k + 1) * 384], start=True, stop=True)
                mm.then_inc(bank_full, 1)

        @block.vector
        def _(dve):
            link = Chain(dve, steps, 0)
            if ones is not None:
                link(nc.vector.memset(ones[:], 1.0))
            dve.wait_ge(exp_done, 1)
            link(nc.vector.tensor_scalar(e_sb[:, 1, :], e_sb[:, 0, :], 1.0, None, ALU.add))
            link(nc.vector.reciprocal(e_sb[:, 2, :], e_sb[:, 1, :]))
            link(nc.vector.tensor_tensor(e_sb[:, 1, :], e_sb[:, 2, :], c_sb[:], ALU.mult))
            nc.vector.tensor_copy(scb[:], spread(e_sb[:, 1, :], 2, P)).then_inc(silu_ready, 1)
            for b in range(B):
                dve.wait_ge(bank_full, b + 1)
                chunks = [banks[b % 2][:, k * 512:k * 512 + 384].rearrange("p (j d) -> p j d", j=3) for k in range(2)]
                nc.vector.tensor_copy(mod[:, 0:3, b, :], chunks[0]).then_inc(steps, 1)
                nc.vector.tensor_copy(mod[:, 3:5, b, :], chunks[1][:, 0:2]).then_inc(steps, 1)
                link.n += 2
                nc.vector.tensor_copy(last_gate[:, b, :], chunks[1][:, 2]).then_inc(bank_free, 1)
            dve.wait_ge(bank_free, B)
            dve.wait_ge(steps, link.n)
            for j in (1, 4):
                link(nc.vector.tensor_scalar(mod[:, j], mod[:, j], 1.0, None, ALU.add))
            for g in (mod[:, 2], last_gate[:]):
                link(nc.vector.tensor_scalar(tmp[:, 0], g, 0.0, 2.0, ALU.is_ge, ALU.mult))
                link(nc.vector.scalar_tensor_tensor(tmp[:, 1], g, -1.0, g, ALU.mult, ALU.max))
                link(nc.vector.tensor_scalar(tmp[:, 1], tmp[:, 1], 0.25, None, ALU.max))
                link(nc.vector.scalar_tensor_tensor(g, tmp[:, 0], -1.0, tmp[:, 1], ALU.add, ALU.mult))


def build_attention(nc, x_dram, w_qk, wv, xt, mod, ident, ident_dram, half_neg, bank2, ring, obank, x_scratch):
    with ExitStack() as ctx:
        def sb(name, shape, dt=F32):
            return ctx.enter_context(nc.sbuf_tensor(name, shape, dt))

        def sem(name):
            return ctx.enter_context(nc.semaphore(name))

        w_qk_sb = sb("w_qk_sb", [P, H, 2 * R])
        wv_sb = sb("wv_sb", [P, H, D])
        h_tok = sb("h_tok", [P, TB, D])
        hT = sb("hT", [P, N])
        centred = sb("centred", [P, TB, D])
        stats = sb("stats", [P, 4, TB])
        q_hh = [sb(f"q_hh{i}", [P, N], F32R) for i in range(2)]
        q_lm = [sb(f"q_lm{i}", [R + 1, N], F32R) for i in range(2)]
        k_hl = [sb(f"k_hl{i}", [P, N], F32R) for i in range(2)]
        k_h1 = [sb(f"k_h1{i}", [R + 1, N], F32R) for i in range(2)]
        v_one = [sb(f"v_one{i}", [P, TB, D + 1]) for i in range(2)]
        maxes = sb("maxes", [P, TB, 2])
        row_max = sb("row_max", [P, TB])
        neg_max = sb("neg_max", [TB, P], F32R)
        recip = sb("recip", [P, TB])
        acc = sb("acc", [P, TB, D])
        probs = sb("probs", [P, 2, TB, HALF])
        st = [bank2[i // 2][:, (i % 2) * HALF:(i % 2 + 1) * HALF] for i in range(4)]

        x_loaded = sem("x_loaded")
        w_loaded = sem("w_loaded")
        var_ready = sem("var_ready")
        rstd_ready = sem("rstd_ready")
        h_ready = sem("h_ready")
        hT_ready = sem("hT_ready")
        ring_full = [sem(f"ring_full{r}") for r in range(2)]
        hi_ready = sem("hi_ready")
        lo_ready = sem("lo_ready")
        k2_ready = sem("k2_ready")
        v_ready = sem("v_ready")
        rows_maxed = sem("rows_maxed")
        max_ready = sem("max_ready")
        neg_ready = sem("neg_ready")
        row_ready = sem("row_ready")
        st_full = [sem(f"st_full{r}") for r in range(4)]
        st_free = [sem(f"st_free{r}") for r in range(4)]
        o_full = [sem(f"o_full{r}") for r in range(2)]
        o_read = [sem(f"o_read{r}") for r in range(2)]
        x_ready = sem("x_ready")
        x_stored = sem("x_stored")
        h2_ready = sem("h2_ready")
        consts = sem("attn_consts")
        steps = sem("attn_steps")
        turns = sem("turns")
        primed = [hT_ready, lo_ready, v_ready, rows_maxed, neg_ready, row_ready, *st_free, *o_read]

        def iteration_uses(b, h):
            g, last = b * H + h, b == B - 1
            found = []
            if not (last and h == H - 1):
                found += [("a", g + 1, i, k) for i in range(TB) for k in range(2)]
                found += [("v", g + 1, k) for k in range(2)] + [("r", g + 1)]
            if h == H - 2 and not last:
                found += [("t", b + 1, k) for k in range(2)]
            if not (last and h >= H - 2):
                found += [("p", g + 2, k) for k in range(2)]
            return found

        uses = [("t", 0, 0), ("t", 0, 1), ("p", 0, 0), ("p", 0, 1)]
        uses += [("a", 0, i, k) for i in range(TB) for k in range(2)]
        uses += [("v", 0, 0), ("v", 0, 1), ("r", 0), ("p", 1, 0), ("p", 1, 1)]
        for b_ in range(B):
            for h_ in range(H):
                uses += iteration_uses(b_, h_)
        place = {key: n for n, key in enumerate(uses)}
        per_batch = place[("r", 3 * H)] - place[("r", 2 * H)]
        assert per_batch % 2 == 0

        def located(b, kind, ahead, *rest):
            b1 = b if isinstance(b, int) else 1
            return place[(kind, (b1 + ahead if kind == "t" else b1 * H + ahead), *rest)]

        def shift(b, value, per):
            return value if isinstance(b, int) else (b - 1) * per + value

        def bank_of(at):
            return at % 2

        def filled(b, at):
            return shift(b, at // 2 + 1, per_batch // 2)

        def released(b, at):
            kind, n = uses[at][0], uses[at][1]
            if kind == "t":
                return hT_ready, shift(b, 2 * n + uses[at][2] + 1, 2)
            if kind == "p":
                return lo_ready, shift(b, 4 * n + 2 * uses[at][2] + 2, 4 * H)
            if kind == "v":
                return v_ready, shift(b, 2 * n + uses[at][2] + 1, 2 * H)
            if kind == "a":
                return rows_maxed, shift(b, 2 * TB * n + 2 * uses[at][2] + uses[at][3] + 1, 2 * TB * H)
            return neg_ready, shift(b, n + 1, H)

        def batches(eng, body):
            body(0, True, False)
            with eng.Fori(1, B - 1) as b:
                body(b, False, False)
            body(B - 1, False, True)

        def product_at(s):
            if s >= 10:
                return 0, 0, s - 10
            return (1, 1, s - 2) if s >= 2 else (1, 0, s + 6)

        block = ctx.enter_context(nc.Block())

        @block.sync
        def _(sp):
            sp.dma_start(xt[:, 0:TB, :], x_dram[:, 0:TB, :]).then_inc(x_loaded, 16)
            sp.dma_start(w_qk_sb[:], w_qk).then_inc(w_loaded, 16)
            sp.dma_start(ident[:], ident_dram).then_inc(w_loaded, 16)
            sp.dma_start(wv_sb[:], wv).then_inc(w_loaded, 16)
            for b in range(1, B):
                sp.dma_start(xt[:, b * TB:(b + 1) * TB, :], x_dram[:, b * TB:(b + 1) * TB, :]).then_inc(x_loaded, 16)

            def max_row(g, h):
                sp.wait_ge(neg_ready, g + 2)
                for i in range(TB):
                    sp.dma_start(q_lm[h % 2][R:R + 1, i * P:(i + 1) * P].bitcast(F32), neg_max[i:i + 1, :].bitcast(F32)).then_inc(row_ready, 16)

            def body(b, first, last):
                for h in range(H):
                    if h == 1 and not first:
                        sp.wait_ge(x_ready, b)
                        sp.dma_start(x_scratch[:, bass.ds((b - 1) * TB, TB), :], xt[:, bass.ds((b - 1) * TB, TB), :]).then_inc(x_stored, 16)
                    if not (last and h == H - 1):
                        max_row(b * H + h + 1, h + 1)

            max_row(0, 0)
            batches(sp, body)
            sp.wait_ge(x_ready, B)
            sp.dma_start(x_scratch[:, (B - 1) * TB:, :], xt[:, (B - 1) * TB:, :]).then_inc(x_stored, 16)

        @block.gpsimd
        def _(pool):
            for s in primed:
                nc.gpsimd.sem_inc(s, 1)
            pool.wait_ge(consts, 5)

            def rstd(n):
                pool.wait_ge(var_ready, n)
                nc.gpsimd.tensor_tensor(stats[:, 3, :], stats[:, 2, :], half_neg[:, 0:TB], ALU.pow).then_inc(rstd_ready, 1)

            def second_k(g, h):
                pool.wait_ge(hi_ready, 6 * g + 6)
                if not (isinstance(g, int) and g < 2):
                    pool.wait_ge(st_full[3], 4 * (g - 1))
                nc.gpsimd.sem_inc(turns, 1)
                nc.gpsimd.tensor_copy(k_h1[h % 2][0:R, :], k_hl[h % 2][0:R, :].bitcast(F32)).then_inc(k2_ready, 1)

            def body(b, first, last):
                for h in range(H):
                    g = b * H + h
                    for s in range(2 * TB):
                        if s == 4 and not (last and h == H - 1):
                            second_k(g + 1, h + 1)
                        if not first and h == 2 and s == 1:
                            rstd(2 * b + 1)
                        if not last and h == 4 and s == 1:
                            rstd(2 * b + 2)

            rstd(1)
            second_k(0, 0)
            batches(pool, body)
            rstd(2 * B)

        @block.scalar
        def _(act):
            def wait_full(b, at):
                act.wait_ge(ring_full[bank_of(at)], filled(b, at))

            def turned_h(b, ahead):
                for k in range(2):
                    at = located(b, "t", ahead, k)
                    wait_full(b, at)
                    nc.scalar.activation(hT[:, k * HALF:(k + 1) * HALF], ring[bank_of(at)][:], ACT.Copy).then_inc(hT_ready, 1)

            def q_and_k(b, h):
                s = h % 2
                if not (isinstance(b, int) and b * H + h < 2):
                    act.wait_ge(st_full[3], 4 * (b * H + h - 1))
                for k in range(2):
                    cols = slice(k * HALF, (k + 1) * HALF)
                    at = located(b, "p", h, k)
                    wait_full(b, at)
                    bank = ring[bank_of(at)]
                    nc.scalar.activation(q_hh[s][0:R, cols], bank[0:R, :], ACT.Copy).then_inc(hi_ready, 1)
                    nc.scalar.activation(k_hl[s][0:R, cols], bank[R:P, :], ACT.Copy).then_inc(hi_ready, 1)
                    nc.scalar.activation(q_hh[s][R:P, cols], bank[0:R, :], ACT.Copy).then_inc(hi_ready, 1)

            def v_out(b, h):
                g = b * H + h
                if not (isinstance(b, int) and g < 2):
                    act.wait_ge(o_full[1], 4 * (g - 1))
                for k in range(2):
                    at = located(b, "v", h, k)
                    wait_full(b, at)
                    nc.scalar.activation(v_one[h % 2][:, 4 * k:4 * k + 4, 0:D], ring[bank_of(at)][:].rearrange("p (m d) -> p m d", m=4), ACT.Copy).then_inc(v_ready, 1)

            def negated_max(b, h):
                at = located(b, "r", h)
                wait_full(b, at)
                act.wait_ge(row_ready, (b * H + h) * 16 * TB + 1)
                nc.scalar.activation(neg_max[:], ring[bank_of(at)][0:TB, 0:P], ACT.Copy, scale=-1.0).then_inc(neg_ready, 1)

            def exponentials(b, h, s):
                g, half, i = b * H + h, s // TB, s % TB
                if i == 0 and not (isinstance(b, int) and g == 0):
                    act.wait_ge(o_full[1], 2 * (2 * g + half) - 2)
                act.wait_ge(st_full[s % 4], 4 * g + s // 4 + 1)
                nc.scalar.activation(probs[:, half, i, :], st[s % 4], ACT.Exp).then_inc(st_free[s % 4], 1)

            def body(b, first, last):
                for h in range(H):
                    more = not (last and h == H - 1)
                    for s in range(2 * TB):
                        exponentials(b, h, s)
                        if s == 12 and more:
                            v_out(b, h + 1)
                        if s == 13 and more:
                            negated_max(b, h + 1)
                        if s == 14 and h == H - 2 and not last:
                            turned_h(b, 1)
                    if not (last and h >= H - 2):
                        q_and_k(b, h + 2)

            act.wait_ge(consts, 5)
            turned_h(0, 0)
            q_and_k(0, 0)
            v_out(0, 0)
            negated_max(0, 0)
            q_and_k(0, 1)
            batches(act, body)

        @block.vector
        def _(dve):
            nc.vector.memset(half_neg[:], -0.5).then_inc(consts, 1)
            for t in k_h1:
                nc.vector.memset(t[R:R + 1, :].bitcast(F32), 1.0).then_inc(consts, 1)
            for t in v_one:
                nc.vector.memset(t[:, :, D:D + 1], 1.0).then_inc(consts, 1)
            dve.wait_ge(consts, 5)

            def wait_full(b, at):
                dve.wait_ge(ring_full[bank_of(at)], filled(b, at))

            def norm_step(link, n, src, dst, scale, shift, count, ready, before_dst=None):
                mean, total, var, rstd = (stats[:, j, :] for j in range(4))
                if n == 0:
                    nc.vector.sem_inc(turns, 1)
                    link(nc.vector.tensor_reduce(mean, src, AX.X, ALU.add))
                    link(nc.vector.tensor_scalar(mean, mean, 1.0 / D, None, ALU.mult))
                elif n == 1:
                    link(nc.vector.tensor_tensor(centred[:], src, spread(mean, 2, D), ALU.subtract))
                elif n == 2:
                    link(nc.vector.tensor_tensor(h_tok[:], centred[:], centred[:], ALU.mult))
                elif n == 3:
                    link(nc.vector.tensor_reduce(total, h_tok[:], AX.X, ALU.add))
                elif n == 4:
                    nc.vector.tensor_scalar(var, total, 1.0 / D, LN_EPS, ALU.mult, ALU.add).then_inc(var_ready, 1)
                elif n == 5:
                    dve.wait_ge(rstd_ready, count)
                    link(nc.vector.tensor_tensor(centred[:], centred[:], spread(rstd, 2, D), ALU.mult))
                elif n == 6:
                    link(nc.vector.tensor_tensor(centred[:], centred[:], scale, ALU.mult))
                else:
                    if before_dst is not None:
                        dve.wait_ge(*before_dst)
                    nc.vector.tensor_tensor(dst, centred[:], shift, ALU.add).then_inc(ready, 1)

            def tiles_of(b):
                return xt[:, bass.ds(b * TB, TB), :] if not isinstance(b, int) else xt[:, b * TB:(b + 1) * TB, :]

            def row(j, b):
                return spread(mod[:, j, bass.ds(b, 1), :].rearrange("p o d -> p (o d)"), 1, TB)

            def first_norm(link, n, b, count):
                norm_step(link, n, tiles_of(b), h_tok[:], row(1, b), row(0, b), count, h_ready)

            def second_norm(link, n, b, count):
                norm_step(link, n, tiles_of(b), tiles_of(b), row(4, b), row(3, b), count, h2_ready, (x_stored, 16 * b + 16))

            def q_and_k(b, h):
                s, g = h % 2, b * H + h
                if not (isinstance(b, int) and g < 2):
                    dve.wait_ge(st_full[3], 4 * (g - 1))
                for k in range(2):
                    cols = slice(k * HALF, (k + 1) * HALF)
                    bank = ring[bank_of(located(b, "p", h, k))]
                    dve.wait_ge(hi_ready, 6 * g + 3 * k + 3)
                    nc.vector.tensor_tensor(q_lm[s][0:R, cols], bank[0:R, :], q_hh[s][0:R, cols].bitcast(F32), ALU.subtract).then_inc(lo_ready, 1)
                    nc.vector.tensor_tensor(k_hl[s][R:P, cols], bank[R:P, :], k_hl[s][0:R, cols].bitcast(F32), ALU.subtract).then_inc(lo_ready, 1)

            def row_maxima(b, h, i):
                if i == 0 and not (isinstance(b, int) and b * H + h == 0):
                    dve.wait_ge(max_ready, b * H + h)
                for k in range(2):
                    at = located(b, "a", h, i, k)
                    wait_full(b, at)
                    nc.vector.tensor_reduce(maxes[:, i, k:k + 1], ring[bank_of(at)][:], AX.X, ALU.max).then_inc(rows_maxed, 1)

            def whole_max(b, h):
                g = b * H + h
                dve.wait_ge(rows_maxed, (g + 1) * 2 * TB + 1)
                if not (isinstance(b, int) and g == 0):
                    dve.wait_ge(neg_ready, g + 1)
                nc.vector.tensor_tensor(row_max[:], maxes[:, :, 0], maxes[:, :, 1], ALU.max).then_inc(max_ready, 1)

            def gather_output(link, g, h, half, j):
                u, tile = 2 * g + half, 4 * half + j
                dve.wait_ge(o_full[j % 2], 2 * u + j // 2 + 1)
                o = obank[j % 2]
                link(nc.vector.reciprocal(recip[:, tile:tile + 1], o[:, D:D + 1]))
                if h % H == 0:
                    out = nc.vector.tensor_scalar(acc[:, tile, :], o[:, 0:D], recip[:, tile:tile + 1], None, ALU.mult)
                else:
                    dve.wait_ge(o_read[j % 2], 2 * u + j // 2 + 1)
                    out = nc.vector.scalar_tensor_tensor(acc[:, tile, :], o[:, 0:D], recip[:, tile:tile + 1], acc[:, tile, :], ALU.mult, ALU.add)
                out.then_inc(o_read[j % 2], 1)

            def residual(link, b):
                for r in range(2):
                    dve.wait_ge(o_read[r], (b + 1) * (4 * H) + 1)
                link(nc.vector.tensor_tensor(acc[:], acc[:], row(2, b), ALU.mult))
                nc.vector.tensor_tensor(tiles_of(b), tiles_of(b), acc[:], ALU.add).then_inc(x_ready, 1)
                dve.wait_ge(x_ready, b + 1)

            def body(b, first, last, base):
                link = Chain(dve, steps, base)
                for h in range(H):
                    more = not (last and h == H - 1)
                    for s in range(2 * TB):
                        if 3 <= s <= 10 and more:
                            row_maxima(b, h + 1, s - 3)
                            if s == 10:
                                whole_max(b, h + 1)
                        behind, half, i = product_at(s)
                        if i % 2 == 1 and not (first and h < behind):
                            gather_output(link, b * H + h - behind, h - behind, half, i // 2)
                        if s == 9 and h == 0 and not first:
                            residual(link, b - 1)
                        if s >= 11 and h in (1, 2) and not first:
                            if h == 1:
                                second_norm(link, s - 11, b - 1, None)
                            elif s >= 13:
                                second_norm(link, s - 8, b - 1, 2 * b + 1)
                        if s >= 11 and h in (3, 4) and not last:
                            if h == 3:
                                first_norm(link, s - 11, b + 1, None)
                            elif s >= 13:
                                first_norm(link, s - 8, b + 1, 2 * b + 2)
                    if not (last and h >= H - 2):
                        q_and_k(b, h + 2)
                return link.n

            link = Chain(dve, steps, 0)
            dve.wait_ge(x_loaded, 16 * B)
            for n in range(8):
                first_norm(link, n, 0, 1)
            q_and_k(0, 0)
            for i in range(TB):
                row_maxima(0, 0, i)
            whole_max(0, 0)
            q_and_k(0, 1)
            done = link.n
            done += body(0, True, False, done)
            with dve.Fori(1, B - 1) as b:
                n = body(b, False, False, done + (b - 1) * STEPS_LOOP)
                assert n == STEPS_LOOP, n
            done += (B - 2) * STEPS_LOOP
            done += body(B - 1, False, True, done)
            link = Chain(dve, steps, done)
            gather_output(link, B * H - 1, H - 1, 0, 3)
            for j in range(4):
                gather_output(link, B * H - 1, H - 1, 1, j)
            residual(link, B - 1)
            for n in range(8):
                second_norm(link, n, B - 1, 2 * B)

        @block.tensor
        def _(pe):
            pe.wait_ge(w_loaded, 48)
            pe.wait_ge(consts, 5)

            def take(b, at):
                if at >= 2:
                    sem_, count = released(b, at - 2)
                    pe.wait_ge(sem_, count + 1)
                return ring[bank_of(at)]

            def give(at, instruction):
                instruction.then_inc(ring_full[bank_of(at)], 1)

            def turn_h(b, ahead):
                pe.wait_ge(h_ready, b + ahead + 1)
                for k in range(2):
                    at = located(b, "t", ahead, k)
                    bank = take(b, at)
                    for i in range(4):
                        mm = nc.tensor.transpose(bank[:, i * P:(i + 1) * P], h_tok[:, 4 * k + i, :], ident[:])
                    give(at, mm)

            def q_and_k(b, h, batch):
                pe.wait_ge(hT_ready, 2 * batch + 3)
                for k in range(2):
                    at = located(b, "p", h, k)
                    bank = take(b, at)
                    give(at, nc.tensor.matmul(bank[:], w_qk_sb[:, h % H, :], hT[:, k * HALF:(k + 1) * HALF], start=True, stop=True))

            def v_of(b, h):
                for k in range(2):
                    at = located(b, "v", h, k)
                    bank = take(b, at)
                    for i in range(4):
                        t = 4 * k + i
                        mm = nc.tensor.matmul(bank[:, i * D:(i + 1) * D], hT[:, t * P:(t + 1) * P], wv_sb[:, h % H, :], start=True, stop=True)
                    give(at, mm)

            def score_rows(b, h, i):
                s = h % 2
                if i == 0:
                    pe.wait_ge(lo_ready, (b * H + h) * 4 + 5)
                for k in range(2):
                    at = located(b, "a", h, i, k)
                    bank = take(b, at)
                    give(at, nc.tensor.matmul(bank[:], q_hh[s][:, i * P:(i + 1) * P], k_hl[s][:, k * HALF:(k + 1) * HALF], start=True, stop=True))

            def turn_max(b, h):
                pe.wait_ge(max_ready, b * H + h + 1)
                at = located(b, "r", h)
                bank = take(b, at)
                give(at, nc.tensor.transpose(bank[0:TB, 0:P], row_max[:], ident[:]))

            def scores(b, h, s):
                g, w, half, i = b * H + h, h % 2, s // TB, s % TB
                if s == 0:
                    pe.wait_ge(row_ready, (g + 1) * (16 * TB) + 1)
                    pe.wait_ge(k2_ready, g + 1)
                if not (isinstance(g, int) and g == 0 and s < 4):
                    pe.wait_ge(st_free[s % 4], 4 * g + s // 4 + 1)
                keys, queries = slice(i * P, (i + 1) * P), slice(half * HALF, (half + 1) * HALF)
                nc.tensor.matmul(st[s % 4], k_hl[w][:, keys], q_hh[w][:, queries], start=True, stop=False)
                nc.tensor.matmul(st[s % 4], k_h1[w][:, keys], q_lm[w][:, queries], start=False, stop=True).then_inc(st_full[s % 4], 1)

            def products(g, h, half, i):
                u, j = 2 * g + half, i // 2
                if i == 0:
                    for r in range(4):
                        pe.wait_ge(st_free[r], 2 * u + 3)
                    pe.wait_ge(v_ready, 2 * g + 3)
                if i % 2 == 0:
                    pe.wait_ge(o_read[j % 2], 2 * u + j // 2 + 1)
                cols = slice(j * P, (j + 1) * P)
                for m in range(4 * (i % 2), 4 * (i % 2) + 4):
                    mm = nc.tensor.matmul(obank[j % 2][:, 0:D + 1], probs[:, half, m, cols], v_one[h % 2][:, m, :], start=(m == 0), stop=(m == TB - 1))
                if i % 2 == 1:
                    mm.then_inc(o_full[j % 2], 1)

            def body(b, first, last):
                for h in range(H):
                    more = not (last and h == H - 1)
                    for s in range(2 * TB):
                        scores(b, h, s)
                        if 3 <= s <= 10 and more:
                            score_rows(b, h + 1, s - 3)
                        behind, half, i = product_at(s)
                        if not (first and h < behind):
                            products(b * H + h - behind, h - behind, half, i)
                        if s == 11 and more:
                            v_of(b, h + 1)
                        if s == 12 and more:
                            turn_max(b, h + 1)
                        if s == 13 and h == H - 2 and not last:
                            turn_h(b, 1)
                    if not (last and h >= H - 2):
                        q_and_k(b, h + 2, b + (h + 2) // H)

            turn_h(0, 0)
            q_and_k(0, 0, 0)
            for i in range(TB):
                score_rows(0, 0, i)
            v_of(0, 0)
            turn_max(0, 0)
            q_and_k(0, 1, 0)
            batches(pe, body)
            for i in (6, 7):
                products(B * H - 1, H - 1, 0, i)
            for i in range(TB):
                products(B * H - 1, H - 1, 1, i)


def build_product_key_table(nc, a, hc, ones, half_neg, ident, banks, wide, w_eff, sim_bias, mean_col):
    ntok = TT * P
    with ExitStack() as ctx:
        def sb(name, shape, dt=F32):
            return ctx.enter_context(nc.sbuf_tensor(name, shape, dt))

        def sem(name):
            return ctx.enter_context(nc.semaphore(name))

        wq_sb = sb("pk_wq", [P, G, P])
        wqT = sb("pk_wqT", [P, G, D])
        keysT = sb("keysT", [P, G, NK])
        keys_s = sb("keys_scaled", [P, G, NK])
        gamma = sb("pk_gamma", [P, G])
        beta = sb("pk_beta", [P, G])
        beta_b = sb("beta_b", [P, G, P])
        mean_b = sb("mean_b", [P, D])
        cov = sb("cov", [P, D])
        prod = sb("pk_prod", [P, 4, D])
        var = sb("pk_var", [P, 4, G])
        loaded = sem("pk_loaded")
        var_ready = sem("pk_var_ready")
        rstd_ready = sem("pk_rstd")
        sum_done = sem("pk_sum")
        mean_ready = sem("pk_mean")
        turned = sem("pk_turned")
        hc_ready = sem("pk_hc")
        gram_done = sem("pk_gram")
        cov_ready = sem("pk_cov")
        wc_full = sem("pk_wc_full")
        wc_read = sem("pk_wc_read")
        keys_ready = sem("pk_keys")
        beta_ready = sem("pk_beta_b")
        tables_done = sem("pk_tables")
        steps = sem("pk_steps")
        block = ctx.enter_context(nc.Block())

        @block.sync
        def _(sp):
            for dst, src in ((wq_sb, "w_q"), (wqT, "w_qT"), (keysT, "keysT"), (gamma, "bn_gamma"), (beta, "bn_beta")):
                sp.dma_start(dst[:], a[src]).then_inc(loaded, 16)

        @block.gpsimd
        def _(pool):
            pool.wait_ge(var_ready, 1)
            nc.gpsimd.tensor_tensor(var[:, 2, :], var[:, 1, :], half_neg[:, 0:G], ALU.pow).then_inc(rstd_ready, 1)

        @block.vector
        def _(dve):
            link = Chain(dve, steps, 0)
            dve.wait_ge(loaded, 80)
            nc.vector.tensor_copy(beta_b[:], spread(beta[:], 2, P)).then_inc(beta_ready, 1)
            dve.wait_ge(sum_done, 1)
            nc.vector.tensor_scalar(mean_b[:], banks[0][:, 0:D], 1.0 / ntok, None, ALU.mult).then_inc(mean_ready, 1)
            dve.wait_ge(mean_ready, 1)
            for b in range(B):
                tiles = slice(b * TB, (b + 1) * TB)
                nc.vector.tensor_tensor(hc[:, tiles, :], hc[:, tiles, :], spread(mean_b[:], 1, TB), ALU.subtract).then_inc(hc_ready, 1)
            dve.wait_ge(turned, 1)
            link(nc.vector.tensor_copy(mean_col[:], banks[1][:, 0:1]))
            dve.wait_ge(gram_done, 1)
            nc.vector.tensor_scalar(cov[:], banks[0][:, 0:D], 1.0 / ntok, None, ALU.mult).then_inc(cov_ready, 1)
            for k in range(4):
                groups = slice(4 * k, 4 * k + 4)
                dve.wait_ge(wc_full, k + 1)
                nc.vector.tensor_tensor(prod[:], banks[2 + k % 2][:].rearrange("p (g d) -> p g d", g=4), wqT[:, groups, :], ALU.mult).then_inc(wc_read, 1)
                dve.wait_ge(wc_read, k + 1)
                link(nc.vector.tensor_reduce(var[:, 0, groups], prod[:], AX.X, ALU.add))
            nc.vector.tensor_scalar(var[:, 1, :], var[:, 0, :], BN_EPS, None, ALU.add).then_inc(var_ready, 1)
            dve.wait_ge(rstd_ready, 1)
            link(nc.vector.tensor_tensor(var[:, 3, :], var[:, 2, :], gamma[:], ALU.mult))
            nc.vector.tensor_tensor(keys_s[:], keysT[:], spread(var[:, 3, :], 2, NK), ALU.mult).then_inc(keys_ready, 1)
            dve.wait_ge(tables_done, 1)
            link(nc.vector.tensor_copy(w_eff[:], wide[:, 0:512]))
            dve.wait_ge(tables_done, 2)
            link(nc.vector.tensor_copy(sim_bias[:], wide[:, 512:1024]))

        @block.tensor
        def _(pe):
            for t in range(TT):
                mm = nc.tensor.matmul(banks[0][:, 0:D], ones[:], hc[:, t, :], start=(t == 0), stop=(t == TT - 1))
            mm.then_inc(sum_done, 1)
            pe.wait_ge(mean_ready, 1)
            nc.tensor.transpose(banks[1][:, 0:P], mean_b[:], ident[:]).then_inc(turned, 1)
            for t in range(TT):
                if t % TB == 0:
                    pe.wait_ge(hc_ready, t // TB + 1)
                mm = nc.tensor.matmul(banks[0][:, 0:D], hc[:, t, :], hc[:, t, :], start=(t == 0), stop=(t == TT - 1))
            mm.then_inc(gram_done, 1)
            pe.wait_ge(loaded, 80)
            pe.wait_ge(cov_ready, 1)
            for k in range(4):
                if k >= 2:
                    pe.wait_ge(wc_read, k - 1)
                for g in range(4):
                    mm = nc.tensor.matmul(banks[2 + k % 2][:, g * D:(g + 1) * D], wq_sb[:, 4 * k + g, :], cov[:], start=True, stop=True)
                mm.then_inc(wc_full, 1)
            pe.wait_ge(keys_ready, 1)
            for g in range(G):
                mm = nc.tensor.matmul(wide[:, g * NK:(g + 1) * NK], wqT[:, g, :], keys_s[:, g, :], start=True, stop=True)
            mm.then_inc(tables_done, 1)
            pe.wait_ge(beta_ready, 1)
            for g in range(G):
                mm = nc.tensor.matmul(wide[:, 512 + g * NK:512 + (g + 1) * NK], beta_b[:, g, :], keysT[:, g, :], start=True, stop=True)
            mm.then_inc(tables_done, 1)


PAIRS = TT // 2
STEPS_HOTS = 3


def build_experts(nc, a, x2, x_scratch, hc, ident, ones, banks, wide, w_eff, sim_bias, mean_col):
    with ExitStack() as ctx:
        def sb(name, shape, dt=F32):
            return ctx.enter_context(nc.sbuf_tensor(name, shape, dt))

        def sem(name):
            return ctx.enter_context(nc.semaphore(name))

        low_hot = sb("low_hot", [P, P, P], BF16)
        low_ids = sb("low_ids", [P, P, P], BF16)
        count = sb("count", [P, P])
        half_mask = sb("half_mask", [P, 2])
        mask_b = sb("mask_b", [P, 2, P], BF16)
        downT = sb("downT", [P, 1024])
        up = sb("up", [P, 8, D])
        hcT = sb("hcT", [P, 2 * P])
        hT = sb("pk_hT", [P, 2 * P])
        act_g = sb("act_g", [P, 8, 2 * P])
        z = sb("z", [P, 8, 2, P])
        sims = sb("sims", [P, 2, 2, H, NK])
        top = sb("top", [P, 2, 2, H, TOPK])
        top_i = sb("top_i", [P, 2, 2, H, TOPK], U32)
        top_f = sb("top_f", [P, 2, TOPK, 2 * H], BF16)
        cand = sb("cand", [P, 2 * H, TOPK, TOPK])
        best = sb("best", [P, 2 * H, TOPK])
        best_i = sb("best_i", [P, 2 * H, TOPK], U32)
        rank_u = sb("rank_u", [P, 2, 2 * H, TOPK], U32)
        rank_f = sb("rank_f", [P, 2, P], BF16)
        hot = sb("hot", [P, 2, TOPK, P], BF16)
        chosen = sb("chosen", [P, 2, P], BF16)
        chosen_u = sb("chosen_u", [P, 3, P], U32)
        to_turn = sb("to_turn", [P, 3, P])
        expd = sb("expd", [P, 2 * H, TOPK])
        tot = sb("tot", [P, 2, 2 * H])
        ids = sb("ids", [P, 2, P], BF16)
        rest = sb("rest", [P, P])
        parts = sb("parts", [P, 3, P], BF16)
        parts_m = sb("parts_m", [P, 3, 2, P], BF16)
        high_hot = sb("high_hot", [P, 8, P], BF16)
        value_hot = sb("value_hot", [P, 6, 8, P], BF16)

        hc_stage = sb("hc_stage", [P, 2, D])
        loaded = sem("ex_loaded")
        stage_ready = sem("ex_stage")
        x_back = sem("ex_x_back")
        turns = sem("ex_turns")
        apart = sem("ex_apart")
        consts = sem("ex_consts")
        steps = sem("ex_steps")
        turned_h = sem("ex_turned_h")
        hT_ready = sem("ex_hT")
        sims_full = sem("ex_sims_full")
        sims_read = sem("ex_sims_read")
        less_max = sem("ex_less_max")
        exp_done = sem("ex_exp")
        to_turn_ready = sem("ex_to_turn")
        turned = sem("ex_turned")
        ids_ready = sem("ex_ids")
        parts_ready = sem("ex_parts")
        rest_ready = sem("ex_rest")
        hots_ready = sem("ex_hots")
        g_full = sem("ex_g_full")
        g_ready = sem("ex_g_ready")
        w_full = sem("ex_w_full")
        z_ready = sem("ex_z")
        out_full = sem("ex_out_full")
        out_read = sem("ex_out_read")
        sim_bank = [banks[2], banks[3]]
        turn_bank, h_bank = banks[0], banks[1]
        block = ctx.enter_context(nc.Block())

        @block.sync
        def _(sp):
            sp.dma_start(count[:], a["count"]).then_inc(loaded, 16)
            sp.dma_start(half_mask[:], a["half_mask"]).then_inc(loaded, 16)
            sp.dma_start(downT[:], a["downT"]).then_inc(loaded, 16)
            sp.dma_start(up[:], a["up"]).then_inc(loaded, 16)
            sp.dma_start(x2[:], x_scratch).then_inc(x_back, 16)
            sp.wait_ge(x_back, 16)


        @block.scalar
        def _(act):
            def front(u):
                act.wait_ge(turned_h, u + 1)
                nc.scalar.activation(hcT[:], h_bank[:, 0:2 * P], ACT.Copy).then_inc(hT_ready, 1)
                nc.scalar.activation(hT[:], h_bank[:, 0:2 * P], ACT.Identity, bias=mean_col[:]).then_inc(hT_ready, 1)
                for q in range(2):
                    act.wait_ge(sims_full, 2 * u + q + 1)
                    nc.scalar.activation(sims[:, q].rearrange("p s h k -> p (s h k)"), sim_bank[q][:], ACT.Copy).then_inc(sims_read, 1)

            def exponentials(u):
                act.wait_ge(less_max, u + 1)
                nc.scalar.activation(expd[:], expd[:], ACT.Exp).then_inc(exp_done, 1)

            def turned_ids(u):
                act.wait_ge(turned, u + 1)
                nc.scalar.activation(ids[:], turn_bank[:, 0:256].rearrange("p (s t) -> p s t", s=2), ACT.Copy).then_inc(ids_ready, 1)
                nc.scalar.activation(parts[:, 0, :], turn_bank[:, 256:384], ACT.Copy).then_inc(parts_ready, 1)
                act.wait_ge(rest_ready, u + 1)
                nc.scalar.activation(parts[:, 1, :], rest[:], ACT.Copy).then_inc(parts_ready, 1)

            def activations(u):
                for k in range(2):
                    act.wait_ge(g_full, 2 * u + k + 1)
                    nc.scalar.activation(act_g[:, 4 * k:4 * k + 4, :], wide[k][:].rearrange("p (e t) -> p e t", e=4),
                                         ACT.Gelu_apprx_tanh).then_inc(g_ready, 1)

            def back(u):
                act.wait_ge(out_full, u + 1)
                nc.scalar.activation(hc[:, bass.ds(2 * u, 2), :], turn_bank[:, 0:256].rearrange("p (q d) -> p q d", q=2), ACT.Copy).then_inc(out_read, 1)

            act.wait_ge(loaded, 64)
            nc.scalar.sem_inc(out_read, 1)
            front(0)
            exponentials(0)
            turned_ids(0)
            activations(0)
            front(1)
            with act.Fori(0, PAIRS - 2) as u:
                exponentials(u + 1)
                turned_ids(u + 1)
                activations(u + 1)
                front(u + 2)
                back(u)
            exponentials(PAIRS - 1)
            turned_ids(PAIRS - 1)
            activations(PAIRS - 1)
            back(PAIRS - 2)
            back(PAIRS - 1)

        @block.vector
        def _(dve):
            def front(u, base):
                link = Chain(dve, steps, base)
                dve.wait_ge(sims_read, 2 * u + 2)
                nc.vector.sem_inc(apart, 1)
                for q in range(2):
                    for s in range(2):
                        for h in range(H):
                            last = nc.vector.max(top[:, s, q, h, :], sims[:, q, s, h, :])
                link(last)
                nc.vector.sem_inc(apart, 1)
                for q in range(2):
                    for s in range(2):
                        for h in range(H):
                            last = nc.vector.max_index(top_i[:, s, q, h, :], top[:, s, q, h, :], sims[:, q, s, h, :])
                link(last)
                topv = top[:].rearrange("p s q h k -> p s (q h) k")
                nc.vector.tensor_copy(top_f[:], top_i[:].rearrange("p s q h k -> p s k (q h)")).then_inc(steps, 1)
                link.n += 1
                link(nc.vector.tensor_tensor(cand[:], spread(topv[:, 0], 3, TOPK), spread(topv[:, 1], 2, TOPK), ALU.add))
                nc.vector.sem_inc(apart, 1)
                for g in range(2 * H):
                    last = nc.vector.max(best[:, g, :], cand[:, g].rearrange("p i j -> p (i j)"))
                link(last)
                nc.vector.sem_inc(apart, 1)
                for g in range(2 * H):
                    last = nc.vector.max_index(best_i[:, g, :], best[:, g, :], cand[:, g].rearrange("p i j -> p (i j)"))
                link(last)
                nc.vector.tensor_tensor(expd[:], best[:], spread(best[:, :, 0], 2, TOPK), ALU.subtract).then_inc(less_max, 1)
                nc.vector.tensor_scalar(rank_u[:, 0], best_i[:], 3, None, ALU.logical_shift_right).then_inc(steps, 1)
                link.n += 1
                link(nc.vector.tensor_scalar(rank_u[:, 1], best_i[:], 7, None, ALU.bitwise_and))
                link(nc.vector.tensor_copy(rank_f[:].rearrange("p s (k g) -> p s k g", k=TOPK), rank_u[:].rearrange("p s g k -> p s k g")))
                link(nc.vector.tensor_tensor(hot[:], spread(rank_f[:], 2, TOPK), spread(low_ids[:, 0:TOPK, :], 1, 2), ALU.is_equal))
                hot4 = hot[:].rearrange("p s j (k g) -> p (s j) k g", k=TOPK)
                link(nc.vector.tensor_tensor(hot4, hot4, spread(top_f[:].rearrange("p s j g -> p (s j) g"), 2, TOPK), ALU.mult))
                link(nc.vector.tensor_tensor(hot[:, :, 0:4], hot[:, :, 0:4], hot[:, :, 4:8], ALU.add))
                link(nc.vector.tensor_tensor(hot[:, :, 0:2], hot[:, :, 0:2], hot[:, :, 2:4], ALU.add))
                link(nc.vector.tensor_tensor(chosen[:], hot[:, :, 0], hot[:, :, 1], ALU.add))
                link(nc.vector.scalar_tensor_tensor(chosen_u[:, 0, :], chosen[:, 0, :], float(NK), chosen[:, 1, :], ALU.mult, ALU.add))
                nc.vector.tensor_scalar(chosen_u[:, 1, :], chosen_u[:, 0, :], 127, None, ALU.bitwise_and).then_inc(steps, 1)
                link.n += 1
                link(nc.vector.tensor_scalar(chosen_u[:, 2, :], chosen_u[:, 0, :], 7, None, ALU.logical_shift_right))
                nc.vector.tensor_copy(to_turn[:, 0:2, :], chosen_u[:, 1:3, :]).then_inc(steps, 1)
                link.n += 1
                dve.wait_ge(exp_done, u + 1)
                link(nc.vector.tensor_reduce(tot[:, 0, :], expd[:], AX.X, ALU.add))
                link(nc.vector.reciprocal(tot[:, 1, :], tot[:, 0, :]))
                nc.vector.tensor_tensor(to_turn[:, 2, :].rearrange("p (k g) -> p g k", g=2 * H), expd[:],
                                        spread(tot[:, 1, :], 2, TOPK), ALU.mult).then_inc(to_turn_ready, 1)
                return link.n

            def one_hots(u, base):
                link = Chain(dve, steps, base)
                dve.wait_ge(ids_ready, u + 1)
                dve.wait_ge(parts_ready, 2 * u + 1)
                nc.vector.tensor_tensor(rest[:], turn_bank[:, 256:384], parts[:, 0, :], ALU.subtract).then_inc(rest_ready, 1)
                nc.vector.tensor_tensor(low_hot[:], spread(ids[:, 0, :], 1, P), low_ids[:], ALU.is_equal).then_inc(hots_ready, 1)
                nc.vector.tensor_tensor(high_hot[:], spread(ids[:, 1, :], 1, 8), low_ids[:, 0:8, :], ALU.is_equal).then_inc(steps, 1)
                link.n += 1
                dve.wait_ge(rest_ready, u + 1)
                dve.wait_ge(parts_ready, 2 * u + 2)
                link(nc.vector.tensor_tensor(parts[:, 2, :], rest[:], parts[:, 1, :], ALU.subtract))
                link(nc.vector.tensor_tensor(parts_m[:], spread(parts[:], 2, 2), spread(mask_b[:], 1, 3), ALU.mult))
                nc.vector.tensor_tensor(value_hot[:], spread(high_hot[:], 1, 6),
                                        spread(parts_m[:].rearrange("p s q t -> p (s q) t"), 2, 8), ALU.mult).then_inc(hots_ready, 1)
                return link.n

            def weigh(u):
                dve.wait_ge(g_ready, 2 * u + 2)
                for k in range(4):
                    dve.wait_ge(w_full, 4 * u + k + 1)
                    tok = slice(32 * k, 32 * k + 32)
                    w = wide[k // 2][:, 512 * (k % 2):512 * (k % 2) + 512].rearrange("p (t q e) -> p q e t", q=2, e=8)
                    for q in range(2):
                        nc.vector.tensor_tensor(z[:, :, q, tok], w[:, q], act_g[:].rearrange("p e (q t) -> p e q t", q=2)[:, :, q, tok],
                                                ALU.mult).then_inc(z_ready, 1)

            dve.wait_ge(loaded, 64)
            nc.vector.tensor_copy(low_ids[:], spread(count[:], 2, P)).then_inc(consts, 1)
            nc.vector.tensor_copy(mask_b[:], spread(half_mask[:], 2, P)).then_inc(consts, 1)
            dve.wait_ge(consts, 2)
            n_front = front(0, 0)
            n_all = n_front + STEPS_HOTS
            with dve.Fori(0, PAIRS - 1) as u:
                base = u * n_all + n_front
                n = one_hots(u, base)
                assert n == STEPS_HOTS, n
                assert front(u + 1, base + n) == n_front
                weigh(u)
            one_hots(PAIRS - 1, (PAIRS - 1) * n_all + n_front)
            weigh(PAIRS - 1)

        @block.tensor
        def _(pe):
            def front(u):
                again = not isinstance(u, int)
                for q in range(2):
                    if not again:
                        src = hc[:, 2 * u + q, :]
                    else:
                        src = hc_stage[:, q, :]
                    mm = nc.tensor.transpose(h_bank[:, q * P:(q + 1) * P], src, ident[:])
                mm.then_inc(turned_h, 1)
                pe.wait_ge(hT_ready, 2 * u + 1)
                if not (isinstance(u, int) and u == 0):
                    pe.wait_ge(sims_read, 2 * u)
                for q in range(2):
                    nc.tensor.matmul(sim_bank[q][:], hcT[:, q * P:(q + 1) * P], w_eff[:], start=True, stop=False)
                    nc.tensor.matmul(sim_bank[q][:], ones[0:1, :], sim_bias[0:1, :], start=False, stop=True).then_inc(sims_full, 1)

            def activations(u):
                pe.wait_ge(hT_ready, 2 * u + 2)
                for k in range(2):
                    for e in range(4):
                        col = (4 * k + e) * P
                        mm = nc.tensor.matmul(wide[k][:, e * 2 * P:(e + 1) * 2 * P], downT[:, col:col + P], hT[:], start=True, stop=True)
                    mm.then_inc(g_full, 1)

            def turn(u):
                pe.wait_ge(to_turn_ready, u + 1)
                if not (isinstance(u, int) and u == 0):
                    pe.wait_ge(out_read, u)
                for s in range(3):
                    mm = nc.tensor.transpose(turn_bank[:, s * P:(s + 1) * P], to_turn[:, s, :], ident[:])
                mm.then_inc(turned, 1)

            def expert_weights(u):
                pe.wait_ge(hots_ready, 2 * u + 2)
                pe.wait_ge(g_ready, 2 * u + 2)
                for t in range(P):
                    col = 512 * (t // 32 % 2) + 16 * (t % 32)
                    for part in range(3):
                        mm = nc.tensor.matmul(wide[t // 64][:, col:col + 16], low_hot[:, :, t],
                                              value_hot[:, 2 * part:2 * part + 2, :, t].rearrange("p q e -> p (q e)"),
                                              start=(part == 0), stop=(part == 2))
                    if t % 32 == 31:
                        mm.then_inc(w_full, 1)

            def combine(u):
                pe.wait_ge(z_ready, 8 * u + 8)
                if not (isinstance(u, int) and u == PAIRS - 1):
                    pe.wait_ge(parts_ready, 2 * u + 3)
                    pe.wait_ge(rest_ready, u + 2)
                else:
                    pe.wait_ge(out_read, u + 1)
                for q in range(2):
                    for e in range(8):
                        mm = nc.tensor.matmul(turn_bank[:, q * D:(q + 1) * D], z[:, e, q, :], up[:, e, :], start=(e == 0), stop=(e == 7))
                mm.then_inc(out_full, 1)

            pe.wait_ge(loaded, 64)
            front(0)
            turn(0)
            activations(0)
            front(1)
            with pe.Fori(0, PAIRS - 2) as u:
                expert_weights(u)
                turn(u + 1)
                pe.wait_ge(z_ready, 8 * u + 8)
                activations(u + 1)
                pe.wait_ge(stage_ready, u + 1)
                front(u + 2)
                combine(u)
            expert_weights(PAIRS - 2)
            turn(PAIRS - 1)
            combine(PAIRS - 2)
            activations(PAIRS - 1)
            expert_weights(PAIRS - 1)
            combine(PAIRS - 1)

        @block.gpsimd
        def _(pool):
            with pool.Fori(1, PAIRS - 1) as u:
                pool.wait_ge(turned_h, u + 1)
                nc.gpsimd.sem_inc(turns, 1)
                nc.gpsimd.tensor_copy(hc_stage[:], hc[:, bass.ds(2 * u + 2, 2), :]).then_inc(stage_ready, 1)


STEPS_SCAN = 24


def build_second_layer(nc, a, xt, hc, gate0, mod, gate1, ident, half_neg, ring, obank, wide, out):
    with ExitStack() as ctx:
        def sb(name, shape, dt=F32):
            return ctx.enter_context(nc.sbuf_tensor(name, shape, dt))

        def sem(name):
            return ctx.enter_context(nc.semaphore(name))

        w_qkva = sb("w_qkva", [P, 3 * D])
        w_rkv = sb("w_rkv", [P, 3, D])
        cols = sb("cols", [P, 4])
        centred = sb("l1_centred", [P, TB, D])
        stats = sb("l1_stats", [P, 4, TB])
        norms = sb("norms", [P, 4, TB])
        half_pos = sb("half_pos", [P, TB])
        h_tok = sb("l1_h", [P, TB, D])
        xnT = sb("xnT", [P, N])
        decay = sb("decay", [P, N])
        y = sb("y", [P, N])
        shifted = sb("shifted", [P, N + 1])
        diff = sb("diff", [P, N])
        mixed = [sb(f"mixed{i}", [P, N]) for i in range(2)]
        rgate = sb("rgate", [P, N])
        kact = sb("kact", [P, N])
        loaded = sem("l1_loaded")
        consts = sem("l1_consts")
        steps = sem("l1_steps")
        var_ready = sem("l1_var")
        rstd_ready = sem("l1_rstd")
        h_ready = sem("l1_h_ready")
        turned = sem("l1_turned")
        hT_ready = sem("l1_hT")
        qkva_full = sem("l1_qkva")
        decay_ready = sem("l1_decay")
        y_ready = sem("l1_y")
        back_full = sem("l1_back")
        back_read = sem("l1_back_read")
        mixed_ready = sem("l1_mixed")
        rk_full = sem("l1_rk")
        rk_ready = sem("l1_rk_ready")
        kact_ready = sem("l1_kact")
        v_full = sem("l1_v")
        rv_ready = sem("l1_rv")
        x_ready = sem("l1_x")
        apart = sem("l1_apart")
        stored = sem("stored")
        block = ctx.enter_context(nc.Block())

        @block.sync
        def _(sp):
            sp.dma_start(w_qkva[:], a["w_qkva"]).then_inc(loaded, 16)
            sp.dma_start(w_rkv[:], a["w_rkv"]).then_inc(loaded, 16)
            sp.dma_start(cols[:, 0:3], a["cols"]).then_inc(loaded, 16)
            with sp.Fori(0, B) as b:
                sp.wait_ge(x_ready, b + 1)
                sp.dma_start(out[:, bass.ds(b * TB, TB), :], xt[:, bass.ds(b * TB, TB), :]).then_inc(stored, 16)
            sp.wait_ge(stored, 16 * B)

        @block.gpsimd
        def _(pool):
            pool.wait_ge(consts, 3)
            with pool.Fori(0, B) as b:
                pool.wait_ge(var_ready, 3 * b + 1)
                nc.gpsimd.tensor_tensor(stats[:, 3, :], stats[:, 2, :], half_neg[:, 0:TB], ALU.pow).then_inc(rstd_ready, 1)
                pool.wait_ge(var_ready, 3 * b + 2)
                nc.gpsimd.tensor_tensor(norms[:, 1, :], norms[:, 0, :], half_pos[:], ALU.pow).then_inc(rstd_ready, 1)
                pool.wait_ge(var_ready, 3 * b + 3)
                nc.gpsimd.tensor_tensor(stats[:, 3, :], stats[:, 2, :], half_neg[:, 0:TB], ALU.pow).then_inc(rstd_ready, 1)
                pool.wait_ge(rk_ready, 4 * b + 4)
                nc.gpsimd.tensor_tensor(kact[:], kact[:], kact[:], ALU.mult).then_inc(kact_ready, 1)

        @block.scalar
        def _(act):
            act.wait_ge(consts, 3)
            with act.Fori(0, B) as b:
                for k in range(2):
                    half = slice(k * HALF, (k + 1) * HALF)
                    act.wait_ge(turned, 4 * b + k + 1)
                    nc.scalar.activation(xnT[:, half], ring[k][:], ACT.Copy, scale=cols[:, 3:4]).then_inc(hT_ready, 1)
                for k in range(2):
                    half = slice(k * HALF, (k + 1) * HALF)
                    act.wait_ge(qkva_full, 2 * b + k + 1)
                    nc.scalar.activation(decay[:, half], obank[k][:], ACT.Sigmoid).then_inc(decay_ready, 1)
                for k in range(2):
                    act.wait_ge(turned, 4 * b + k + 3)
                    nc.scalar.activation(shifted[:, 1 + k * HALF:1 + (k + 1) * HALF], ring[k][:], ACT.Copy).then_inc(hT_ready, 1)
                for k in range(2):
                    half = slice(k * HALF, (k + 1) * HALF)
                    act.wait_ge(rk_full, 2 * b + k + 1)
                    nc.scalar.activation(kact[:, half], wide[1][:, half], ACT.Relu).then_inc(rk_ready, 1)
                    nc.scalar.activation(rgate[:, half], wide[0][:, half], ACT.Sigmoid).then_inc(rk_ready, 1)

        @block.vector
        def _(dve):
            nc.vector.memset(half_pos[:], 0.5).then_inc(consts, 1)
            nc.vector.memset(shifted[:, 0:1], 0.0).then_inc(consts, 1)
            dve.wait_ge(loaded, 48)
            nc.vector.tensor_scalar(cols[:, 3:4], cols[:, 0:1], float(D) ** 0.5, None, ALU.mult).then_inc(consts, 1)
            with dve.Fori(0, B) as b:
                link = Chain(dve, steps, b * STEPS_SCAN)
                xb = xt[:, bass.ds(b * TB, TB), :]

                def row(m):
                    return spread(m[:, bass.ds(b, 1), :].rearrange("p o d -> p (o d)"), 1, TB)

                link(nc.vector.tensor_tensor(centred[:], hc[:, bass.ds(b * TB, TB), :], row(gate0), ALU.mult))
                link(nc.vector.tensor_tensor(xb, xb, centred[:], ALU.add))
                nc.vector.sem_inc(apart, 1)
                link(layernorm(nc, dve, link, xb, centred[:], stats, h_tok[:], row(mod[:, 1]), row(mod[:, 0]), var_ready, rstd_ready, 3 * b + 1))
                link(nc.vector.tensor_tensor(centred[:], h_tok[:], h_tok[:], ALU.mult))
                nc.vector.tensor_reduce(norms[:, 0, :], centred[:], AX.X, ALU.add).then_inc(var_ready, 1)
                dve.wait_ge(rstd_ready, 3 * b + 2)
                link(nc.vector.tensor_scalar(norms[:, 2, :], norms[:, 1, :], NORM_EPS, None, ALU.max))
                link(nc.vector.reciprocal(norms[:, 3, :], norms[:, 2, :]))
                nc.vector.tensor_tensor(h_tok[:], h_tok[:], spread(norms[:, 3, :], 2, D), ALU.mult).then_inc(h_ready, 1)
                for k in range(2):
                    half = slice(k * HALF, (k + 1) * HALF)
                    dve.wait_ge(decay_ready, 2 * b + k + 1)
                    link(nc.vector.tensor_tensor_scan(y[:, half], decay[:, half], wide[1][:, half], 0.0 if k == 0 else y[:, HALF - 1:HALF], ALU.mult, ALU.add))
                for k in range(2):
                    half = slice(k * HALF, (k + 1) * HALF)
                    nc.vector.tensor_tensor(y[:, half], y[:, half], wide[0][:, half], ALU.mult).then_inc(y_ready, 1)
                for k in range(2):
                    tiles = slice(4 * k, 4 * k + 4)
                    dve.wait_ge(back_full, 4 * b + k + 1)
                    nc.vector.tensor_tensor(centred[:, tiles, :], ring[k][:].rearrange("p (t d) -> p t d", t=4), row(mod[:, 2])[:, tiles, :], ALU.mult).then_inc(back_read, 1)
                dve.wait_ge(back_read, 4 * b + 2)
                link(nc.vector.tensor_tensor(xb, xb, centred[:], ALU.add))
                nc.vector.sem_inc(apart, 1)
                layernorm(nc, dve, link, xb, centred[:], stats, h_tok[:], row(mod[:, 4]), row(mod[:, 3]), var_ready, rstd_ready, 3 * b + 3).then_inc(h_ready, 1)
                dve.wait_ge(hT_ready, 4 * b + 4)
                link(nc.vector.tensor_tensor(diff[:], shifted[:, 1:], shifted[:, 0:N], ALU.subtract))
                for i in range(2):
                    nc.vector.scalar_tensor_tensor(mixed[i][:], diff[:], cols[:, 1 + i:2 + i], shifted[:, 0:N], ALU.mult, ALU.add).then_inc(mixed_ready, 1)
                for k in range(2):
                    half = slice(k * HALF, (k + 1) * HALF)
                    dve.wait_ge(v_full, 2 * b + k + 1)
                    nc.vector.tensor_tensor(rgate[:, half], rgate[:, half], obank[k][:], ALU.mult).then_inc(rv_ready, 1)
                for k in range(2):
                    tiles = slice(4 * k, 4 * k + 4)
                    dve.wait_ge(back_full, 4 * b + k + 3)
                    nc.vector.tensor_tensor(centred[:, tiles, :], ring[k][:].rearrange("p (t d) -> p t d", t=4), row(gate1)[:, tiles, :], ALU.mult).then_inc(back_read, 1)
                dve.wait_ge(back_read, 4 * b + 4)
                nc.vector.tensor_tensor(xb, xb, centred[:], ALU.add).then_inc(x_ready, 1)
                dve.wait_ge(x_ready, b + 1)
                assert link.n == STEPS_SCAN, link.n

        @block.tensor
        def _(pe):
            pe.wait_ge(loaded, 48)
            with pe.Fori(0, B) as b:
                def turn(n):
                    for k in range(2):
                        for i in range(4):
                            mm = nc.tensor.transpose(ring[k][:, i * P:(i + 1) * P], h_tok[:, 4 * k + i, :], ident[:])
                        mm.then_inc(turned, 1)

                def turn_back(src, ready, n):
                    for k in range(2):
                        pe.wait_ge(ready, 2 * b + k + 1)
                        for i in range(4):
                            t = 4 * k + i
                            mm = nc.tensor.transpose(ring[k][:, i * P:(i + 1) * P], src[:, t * P:(t + 1) * P], ident[:])
                        mm.then_inc(back_full, 1)

                pe.wait_ge(h_ready, 2 * b + 1)
                turn(0)
                for k in range(2):
                    half = slice(k * HALF, (k + 1) * HALF)
                    pe.wait_ge(hT_ready, 4 * b + k + 1)
                    for j, bank in enumerate((wide[0][:, half], wide[1][:, half], obank[k][:])):
                        mm = nc.tensor.matmul(bank, w_qkva[:, j * D:(j + 1) * D], xnT[:, half], start=True, stop=True)
                    mm.then_inc(qkva_full, 1)
                turn_back(y, y_ready, 0)
                pe.wait_ge(h_ready, 2 * b + 2)
                turn(1)
                pe.wait_ge(mixed_ready, 2 * b + 2)
                for k in range(2):
                    half = slice(k * HALF, (k + 1) * HALF)
                    for i in range(2):
                        mm = nc.tensor.matmul(wide[i][:, half], w_rkv[:, i, :], mixed[i][:, half], start=True, stop=True)
                    mm.then_inc(rk_full, 1)
                pe.wait_ge(kact_ready, b + 1)
                for k in range(2):
                    half = slice(k * HALF, (k + 1) * HALF)
                    nc.tensor.matmul(obank[k][:], w_rkv[:, 2, :], kact[:, half], start=True, stop=True).then_inc(v_full, 1)
                turn_back(rgate, rv_ready, 1)


def build(nc, args, out):
    with ExitStack() as ctx:
        def sb(name, shape, dt=F32):
            return ctx.enter_context(nc.sbuf_tensor(name, shape, dt))

        bank2 = [ctx.enter_context(nc.psum_tensor(f"bank2_{i}", [P, N], F32)) for i in range(2)]
        ring = [ctx.enter_context(nc.psum_tensor(f"ring{i}", [P, 512], F32)) for i in range(2)]
        obank = [ctx.enter_context(nc.psum_tensor(f"obank{i}", [P, 512], F32)) for i in range(2)]
        xt = sb("xt", [P, TT, D])
        gate0 = sb("gate0", [P, B, D])
        ident = sb("ident_sb", [P, P])
        ones = sb("ones", [P, P])
        half_neg = sb("half_neg", [P, TT])
        w_eff = sb("w_eff", [P, G * NK])
        sim_bias = sb("sim_bias", [P, G * NK])
        mean_col = sb("mean_col", [P, 1])
        banks = ring + obank
        with nc.sbuf_tensor("mod0", [P, 5, B, D], F32) as mod:
            build_modulation(nc, 0, args["c0"], args["wmod0"], mod, gate0, ones, bank2)
            build_attention(nc, args["x"], args["w_qk"], args["wv"], xt, mod, ident, args["ident"], half_neg,
                            bank2, ring, obank, out)
        build_product_key_table(nc, args, xt, ones, half_neg, ident, banks, bank2[0], w_eff, sim_bias, mean_col)
        x2 = sb("x2", [P, TT, D])
        build_experts(nc, args, x2, out, xt, ident, ones, banks, bank2, w_eff, sim_bias, mean_col)
        mod = sb("mod1", [P, 5, B, D])
        gate1 = sb("gate1", [P, B, D])
        build_modulation(nc, 1, args["c1"], args["wmod1"], mod, gate1, None, bank2)
        build_second_layer(nc, args, x2, xt, gate0, mod, gate1, ident, half_neg, ring, obank, bank2, out)


def kernel(**inputs):
    import numpy as np
    import concourse.bacc as bacc
    from concourse import mybir
    from concourse.bass_utils import run_bass_kernel_spmd as run

    a = {k: np.asarray(v) for k, v in inputs.items()}
    lay = {
        "x": a["L0_attn_x"].reshape(64, 128, 128).transpose(1, 0, 2),
        "w_qk": np.concatenate([a["L0_attn_Wq"].reshape(8, 64, 128), a["L0_attn_Wk"].reshape(8, 64, 128)], axis=1).transpose(2, 0, 1),
        "wv": a["L0_attn_Wv"].reshape(8, 128, 128).transpose(2, 0, 1),
        "c0": a["L0_c"].T,
        "wmod0": a["L0_wmod"],
        "c1": a["L1_c"].T,
        "wmod1": a["L1_wmod"],
        "w_qkva": a["L1_attn_W_qkva"].T,
        "w_rkv": np.stack([a["L1_ffn_W_r"].T, a["L1_ffn_W_k"].T, a["L1_ffn_W_v"].T], axis=1),
        "cols": np.stack([a["L1_attn_gamma"], a["L1_ffn_mu_r"], a["L1_ffn_mu_k"]], axis=1),
        "w_q": a["L0_ffn_w_q"].reshape(128, 16, 128),
        "w_qT": a["L0_ffn_w_q"].reshape(128, 16, 128).transpose(2, 1, 0),
        "keysT": a["L0_ffn_keys"].transpose(3, 2, 0, 1).reshape(128, 16, 32),
        "bn_gamma": a["L0_ffn_bn_gamma"].reshape(16, 128).T,
        "bn_beta": a["L0_ffn_bn_beta"].reshape(16, 128).T,
        "downT": a["L0_ffn_down_embed"].T,
        "up": a["L0_ffn_up_embed"].reshape(8, 128, 128).transpose(1, 0, 2),
        "count": np.broadcast_to(np.arange(128, dtype=np.float32), (128, 128)),
        "half_mask": np.tile(np.kron(np.eye(2, dtype=np.float32), np.ones((8, 1), np.float32)), (8, 1)),
        "ident": np.eye(128, dtype=np.float32),
    }
    nc = bacc.Bacc("TRN2", target_bir_lowering=False, num_devices=1)
    arrays, args = {}, {}
    for name, v in lay.items():
        v = np.ascontiguousarray(v)
        arrays[f"in_{name}"] = v
        args[name] = nc.dram_tensor(f"in_{name}", v.shape, mybir.dt.from_np(v.dtype), kind="ExternalInput").ap()
    out = nc.dram_tensor("out_x", (128, 64, 128), mybir.dt.float32, kind="ExternalOutput").ap()
    build(nc, args, out)
    r = run(nc, [arrays], core_ids=[0])
    return r.results[0]["out_x"].transpose(1, 0, 2).reshape(8, 1024, 128)
```

```python
from contextlib import ExitStack

import concourse.bass as bass
from concourse import mybir

P = 128
B, N, D = 8, 1024, 128
TB = N // P
TT = B * TB
H, R = 8, 64
G = 16
NK, TOPK = 32, 8
STEPS_LOOP = 79
LN_EPS, BN_EPS, NORM_EPS = 1e-5, 1e-5, 1e-12
HALF = N // 2

ALU = mybir.AluOpType
ACT = mybir.ActivationFunctionType
AX = mybir.AxisListType
F32 = mybir.dt.float32
F32R = mybir.dt.float32r
BF16 = mybir.dt.bfloat16
U32 = mybir.dt.uint32


def spread(ap, axis, count):
    ap = ap.unsqueeze(axis)
    shape = list(ap.shape)
    shape[axis] = count
    return ap.broadcast_to(shape)


class Chain:

    def __init__(self, eng, sem, base):
        self.eng, self.sem, self.base, self.n = eng, sem, base, 0

    def __call__(self, instruction):
        self.n += 1
        instruction.then_inc(self.sem, 1)
        self.eng.wait_ge(self.sem, self.base + self.n)


def build_modulation(nc, tag, cT, wmod, small_ident, mod, last_gate, ones, banks):
    with ExitStack() as ctx:
        c_sb = ctx.enter_context(nc.sbuf_tensor(f"c_sb{tag}", [P, B], F32))
        w_sb = ctx.enter_context(nc.sbuf_tensor(f"wmod_sb{tag}", [P, 6 * D], F32))
        e_sb = ctx.enter_context(nc.sbuf_tensor(f"e_sb{tag}", [P, 3, B], F32))
        id_sb = ctx.enter_context(nc.sbuf_tensor(f"small_ident{tag}", [B, B], F32))
        pick = ctx.enter_context(nc.sbuf_tensor(f"pick{tag}", [B, B, P], F32))
        rows = ctx.enter_context(nc.sbuf_tensor(f"mod_rows{tag}", [B, 6 * D], F32))
        tmp = ctx.enter_context(nc.sbuf_tensor(f"gate_tmp{tag}", [B, 2, D], F32))
        loaded = ctx.enter_context(nc.semaphore(f"mod_loaded{tag}"))
        exp_done = ctx.enter_context(nc.semaphore(f"mod_exp{tag}"))
        silu_ready = ctx.enter_context(nc.semaphore(f"mod_silu{tag}"))
        rows_full = ctx.enter_context(nc.semaphore(f"mod_rows_full{tag}"))
        rows_ready = ctx.enter_context(nc.semaphore(f"mod_rows_ready{tag}"))
        bank_full = ctx.enter_context(nc.semaphore(f"mod_full{tag}"))
        low_read = ctx.enter_context(nc.semaphore(f"mod_low_read{tag}"))
        high_read = ctx.enter_context(nc.semaphore(f"mod_high_read{tag}"))
        steps = ctx.enter_context(nc.semaphore(f"mod_steps{tag}"))
        block = ctx.enter_context(nc.Block())

        def part(k):
            return slice(k * 384, (k + 1) * 384)

        @block.sync
        def _(sp):
            sp.dma_start(c_sb[:], cT).then_inc(loaded, 16)
            sp.dma_start(id_sb[:], small_ident).then_inc(loaded, 16)
            sp.dma_start(w_sb[:], wmod).then_inc(loaded, 16)

        @block.scalar
        def _(act):
            act.wait_ge(loaded, 48)
            nc.scalar.activation(e_sb[:, 0, :], c_sb[:], ACT.Exp, scale=-1.0).then_inc(exp_done, 1)
            for b in range(B):
                act.wait_ge(bank_full, 2 * b + 1)
                nc.scalar.activation(mod[:, 0:3, b, :], banks[b % 2][:, 0:384].rearrange("p (j d) -> p j d", j=3), ACT.Copy).then_inc(low_read, 1)

        @block.tensor
        def _(pe):
            pe.wait_ge(loaded, 48)
            pe.wait_ge(silu_ready, 1)
            for k in range(2):
                mm = nc.tensor.matmul(banks[0][0:B, k * 512:k * 512 + 384], e_sb[:, 1, :], w_sb[:, part(k)], start=True, stop=True)
            mm.then_inc(rows_full, 1)
            pe.wait_ge(rows_ready, 1)
            for b in range(B):
                if b >= 2:
                    pe.wait_ge(low_read, b - 1)
                    pe.wait_ge(high_read, 2 * b - 2)
                for k in range(2):
                    nc.tensor.matmul(banks[b % 2][:, k * 512:k * 512 + 384], pick[:, b, :], rows[:, part(k)], start=True, stop=True).then_inc(bank_full, 1)

        @block.vector
        def _(dve):
            link = Chain(dve, steps, 0)
            if ones is not None:
                link(nc.vector.memset(ones[:], 1.0))
            dve.wait_ge(exp_done, 1)
            link(nc.vector.tensor_scalar(e_sb[:, 1, :], e_sb[:, 0, :], 1.0, None, ALU.add))
            link(nc.vector.reciprocal(e_sb[:, 2, :], e_sb[:, 1, :]))
            nc.vector.tensor_tensor(e_sb[:, 1, :], e_sb[:, 2, :], c_sb[:], ALU.mult).then_inc(silu_ready, 1)
            link(nc.vector.tensor_copy(pick[:], spread(id_sb[:], 2, P)))
            dve.wait_ge(rows_full, 1)
            link(nc.vector.tensor_copy(rows[:].rearrange("b (k j) -> b k j", k=2), banks[0][0:B, :].rearrange("b (k j) -> b k j", k=2)[:, :, 0:384]))
            for j in (1, 4):
                chunk = rows[:, j * D:(j + 1) * D]
                link(nc.vector.tensor_scalar(chunk, chunk, 1.0, None, ALU.add))
            for j in (2, 5):
                g = rows[:, j * D:(j + 1) * D]
                link(nc.vector.tensor_scalar(tmp[:, 0], g, 0.0, 2.0, ALU.is_ge, ALU.mult))
                link(nc.vector.scalar_tensor_tensor(tmp[:, 1], g, -1.0, g, ALU.mult, ALU.max))
                link(nc.vector.tensor_scalar(tmp[:, 1], tmp[:, 1], 0.25, None, ALU.max))
                gate_made = nc.vector.scalar_tensor_tensor(g, tmp[:, 0], -1.0, tmp[:, 1], ALU.add, ALU.mult)
                if j == 2:
                    link(gate_made)
            gate_made.then_inc(rows_ready, 1)
            for b in range(B):
                dve.wait_ge(bank_full, 2 * b + 2)
                chunks = banks[b % 2][:, 512:512 + 384].rearrange("p (j d) -> p j d", j=3)
                nc.vector.tensor_copy(mod[:, 3:5, b, :], chunks[:, 0:2]).then_inc(high_read, 1)
                nc.vector.tensor_copy(last_gate[:, b, :], chunks[:, 2]).then_inc(high_read, 1)


def build_attention(nc, x_dram, w_qk, wv, xt, mod, ident, ident_dram, half_neg, bank2, ring, obank, x_scratch):
    with ExitStack() as ctx:
        def sb(name, shape, dt=F32):
            return ctx.enter_context(nc.sbuf_tensor(name, shape, dt))

        def sem(name):
            return ctx.enter_context(nc.semaphore(name))

        w_qk_sb = sb("w_qk_sb", [P, H, 2 * R])
        wv_sb = sb("wv_sb", [P, H, D])
        h_tok = sb("h_tok", [P, TB, D])
        hT = sb("hT", [P, N])
        centred = sb("centred", [P, TB, D])
        stats = sb("stats", [P, 4, TB])
        q_hh = [sb(f"q_hh{i}", [P, N], F32R) for i in range(2)]
        q_lm = [sb(f"q_lm{i}", [R + 1, N], F32R) for i in range(2)]
        k_hl = [sb(f"k_hl{i}", [P, N], F32R) for i in range(2)]
        k_h1 = [sb(f"k_h1{i}", [R + 1, N], F32R) for i in range(2)]
        v_one = [sb(f"v_one{i}", [P, TB, D + 1]) for i in range(2)]
        maxes = sb("maxes", [P, TB, 2])
        row_max = sb("row_max", [P, TB], F32R)
        ident_r = sb("ident_r", [P, P], F32R)
        recip = sb("recip", [P, TB])
        acc = sb("acc", [P, TB, D])
        probs = sb("probs", [P, 2, TB, HALF])
        st = [bank2[i // 2][:, (i % 2) * HALF:(i % 2 + 1) * HALF] for i in range(4)]

        first_x_loaded = sem("first_x_loaded")
        x_loaded = sem("x_loaded")
        w_loaded = sem("w_loaded")
        var_ready = sem("var_ready")
        rstd_ready = sem("rstd_ready")
        h_ready = sem("h_ready")
        hT_ready = sem("hT_ready")
        ring_full = [sem(f"ring_full{r}") for r in range(2)]
        hi_ready = sem("hi_ready")
        lo_ready = sem("lo_ready")
        k2_ready = sem("k2_ready")
        v_ready = sem("v_ready")
        rows_maxed = sem("rows_maxed")
        max_ready = sem("max_ready")
        neg_ready = sem("neg_ready")
        st_full = [sem(f"st_full{r}") for r in range(4)]
        st_free = [sem(f"st_free{r}") for r in range(4)]
        o_full = [sem(f"o_full{r}") for r in range(2)]
        o_read = [sem(f"o_read{r}") for r in range(2)]
        x_ready = sem("x_ready")
        x_stored = sem("x_stored")
        h2_ready = sem("h2_ready")
        consts = sem("attn_consts")
        steps = sem("attn_steps")
        turns = sem("turns")
        primed = [hT_ready, lo_ready, v_ready, rows_maxed, neg_ready, *st_free, *o_read]

        def iteration_uses(b, h):
            g, last = b * H + h, b == B - 1
            found = []
            if not (last and h == H - 1):
                found += [("a", g + 1, i, k) for i in range(TB) for k in range(2)]
                found += [(kind, g + 1, k) for kind in "vr" for k in range(2)]
            if h == H - 2 and not last:
                found += [("t", b + 1, k) for k in range(2)]
            if not (last and h >= H - 2):
                found += [("p", g + 2, k) for k in range(2)]
            return found

        uses = [("t", 0, 0), ("t", 0, 1), ("p", 0, 0), ("p", 0, 1)]
        uses += [("a", 0, i, k) for i in range(TB) for k in range(2)]
        uses += [("v", 0, 0), ("v", 0, 1), ("r", 0, 0), ("r", 0, 1), ("p", 1, 0), ("p", 1, 1)]
        for b_ in range(B):
            for h_ in range(H):
                uses += iteration_uses(b_, h_)
        place = {key: n for n, key in enumerate(uses)}
        per_batch = place[("r", 3 * H, 0)] - place[("r", 2 * H, 0)]
        assert per_batch % 2 == 0

        def located(b, kind, ahead, *rest):
            b1 = b if isinstance(b, int) else 1
            return place[(kind, (b1 + ahead if kind == "t" else b1 * H + ahead), *rest)]

        def shift(b, value, per):
            return value if isinstance(b, int) else (b - 1) * per + value

        def bank_of(at):
            return at % 2

        def filled(b, at):
            return shift(b, at // 2 + 1, per_batch // 2)

        def released(b, at):
            kind, n = uses[at][0], uses[at][1]
            if kind == "t":
                return hT_ready, shift(b, 2 * n + uses[at][2] + 1, 2)
            if kind == "p":
                return lo_ready, shift(b, 4 * n + 2 * uses[at][2] + 2, 4 * H)
            if kind == "v":
                return v_ready, shift(b, 2 * n + uses[at][2] + 1, 2 * H)
            if kind == "a":
                return rows_maxed, shift(b, 2 * TB * n + 2 * uses[at][2] + uses[at][3] + 1, 2 * TB * H)
            return neg_ready, shift(b, 2 * n + uses[at][2] + 1, 2 * H)

        def batches(eng, body):
            body(0, True, False)
            with eng.Fori(1, B - 1) as b:
                body(b, False, False)
            body(B - 1, False, True)

        def product_at(s):
            if s >= 10:
                return 0, 0, s - 10
            return (1, 1, s - 2) if s >= 2 else (1, 0, s + 6)

        block = ctx.enter_context(nc.Block())

        @block.sync
        def _(sp):
            sp.dma_start(xt[:, 0:TB, :], x_dram[:, 0:TB, :]).then_inc(first_x_loaded, 16)
            sp.dma_start(w_qk_sb[:], w_qk).then_inc(w_loaded, 16)
            sp.dma_start(ident[:], ident_dram).then_inc(w_loaded, 16)
            sp.dma_start(wv_sb[:], wv).then_inc(w_loaded, 16)
            for b in range(1, B):
                sp.dma_start(xt[:, b * TB:(b + 1) * TB, :], x_dram[:, b * TB:(b + 1) * TB, :]).then_inc(x_loaded, 16)

            with sp.Fori(0, B) as b:
                sp.wait_ge(x_ready, b + 1)
                sp.dma_start(x_scratch[:, bass.ds(b * TB, TB), :], xt[:, bass.ds(b * TB, TB), :]).then_inc(x_stored, 16)

        @block.gpsimd
        def _(pool):
            for s in primed:
                nc.gpsimd.sem_inc(s, 1)
            pool.wait_ge(consts, 5)

            def rstd(n):
                pool.wait_ge(var_ready, n)
                nc.gpsimd.tensor_tensor(stats[:, 3, :], stats[:, 2, :], half_neg[:, 0:TB], ALU.pow).then_inc(rstd_ready, 1)

            def second_k(g, h):
                pool.wait_ge(hi_ready, 6 * g + 6)
                if not (isinstance(g, int) and g < 2):
                    pool.wait_ge(st_full[3], 4 * (g - 1))
                nc.gpsimd.sem_inc(turns, 1)
                nc.gpsimd.tensor_copy(k_h1[h % 2][0:R, :], k_hl[h % 2][0:R, :].bitcast(F32)).then_inc(k2_ready, 1)

            def body(b, first, last):
                for h in range(H):
                    g = b * H + h
                    for s in range(2 * TB):
                        if s == 4 and not (last and h == H - 1):
                            second_k(g + 1, h + 1)
                        if not first and h == 2 and s == 1:
                            rstd(2 * b + 1)
                        if not last and h == 4 and s == 1:
                            rstd(2 * b + 2)

            rstd(1)
            second_k(0, 0)
            batches(pool, body)
            rstd(2 * B)

        @block.scalar
        def _(act):
            def wait_full(b, at):
                act.wait_ge(ring_full[bank_of(at)], filled(b, at))

            def turned_h(b, ahead):
                for k in range(2):
                    at = located(b, "t", ahead, k)
                    wait_full(b, at)
                    nc.scalar.activation(hT[:, k * HALF:(k + 1) * HALF], ring[bank_of(at)][:], ACT.Copy).then_inc(hT_ready, 1)

            def q_and_k(b, h):
                s = h % 2
                if not (isinstance(b, int) and b * H + h < 2):
                    act.wait_ge(st_full[3], 4 * (b * H + h - 1))
                for k in range(2):
                    cols = slice(k * HALF, (k + 1) * HALF)
                    at = located(b, "p", h, k)
                    wait_full(b, at)
                    bank = ring[bank_of(at)]
                    nc.scalar.activation(q_hh[s][0:R, cols], bank[0:R, :], ACT.Copy).then_inc(hi_ready, 1)
                    nc.scalar.activation(k_hl[s][0:R, cols], bank[R:P, :], ACT.Copy).then_inc(hi_ready, 1)
                    nc.scalar.activation(q_hh[s][R:P, cols], bank[0:R, :], ACT.Copy).then_inc(hi_ready, 1)

            def v_out(b, h):
                g = b * H + h
                if not (isinstance(b, int) and g < 2):
                    act.wait_ge(o_full[1], 4 * (g - 1))
                for k in range(2):
                    at = located(b, "v", h, k)
                    wait_full(b, at)
                    nc.scalar.activation(v_one[h % 2][:, 4 * k:4 * k + 4, 0:D], ring[bank_of(at)][:].rearrange("p (m d) -> p m d", m=4), ACT.Copy).then_inc(v_ready, 1)

            def negated_max(b, h):
                for k in range(2):
                    at = located(b, "r", h, k)
                    wait_full(b, at)
                    nc.scalar.activation(q_lm[h % 2][R:R + 1, k * HALF:(k + 1) * HALF], ring[bank_of(at)][0:1, :], ACT.Copy, scale=-1.0).then_inc(neg_ready, 1)

            def exponentials(b, h, s):
                g, half, i = b * H + h, s // TB, s % TB
                if i == 0 and not (isinstance(b, int) and g == 0):
                    act.wait_ge(o_full[1], 2 * (2 * g + half) - 2)
                act.wait_ge(st_full[s % 4], 4 * g + s // 4 + 1)
                nc.scalar.activation(probs[:, half, i, :], st[s % 4], ACT.Exp).then_inc(st_free[s % 4], 1)

            def body(b, first, last):
                for h in range(H):
                    more = not (last and h == H - 1)
                    for s in range(2 * TB):
                        exponentials(b, h, s)
                        if s == 11 and more:
                            v_out(b, h + 1)
                        if s == 12 and more:
                            negated_max(b, h + 1)
                        if s == 14 and h == H - 2 and not last:
                            turned_h(b, 1)
                    if not (last and h >= H - 2):
                        q_and_k(b, h + 2)

            act.wait_ge(consts, 5)
            turned_h(0, 0)
            q_and_k(0, 0)
            v_out(0, 0)
            negated_max(0, 0)
            q_and_k(0, 1)
            batches(act, body)

        @block.vector
        def _(dve):
            nc.vector.memset(half_neg[:], -0.5).then_inc(consts, 1)
            for t in k_h1:
                nc.vector.memset(t[R:R + 1, :].bitcast(F32), 1.0).then_inc(consts, 1)
            for t in v_one:
                nc.vector.memset(t[:, :, D:D + 1], 1.0).then_inc(consts, 1)
            dve.wait_ge(consts, 5)

            def wait_full(b, at):
                dve.wait_ge(ring_full[bank_of(at)], filled(b, at))

            def norm_step(link, n, src, dst, scale, shift, count, ready, before_dst=None):
                mean, total, var, rstd = (stats[:, j, :] for j in range(4))
                if n == 0:
                    nc.vector.sem_inc(turns, 1)
                    link(nc.vector.tensor_reduce(mean, src, AX.X, ALU.add))
                    link(nc.vector.tensor_scalar(mean, mean, 1.0 / D, None, ALU.mult))
                elif n == 1:
                    link(nc.vector.tensor_tensor(centred[:], src, spread(mean, 2, D), ALU.subtract))
                elif n == 2:
                    link(nc.vector.tensor_tensor(h_tok[:], centred[:], centred[:], ALU.mult))
                elif n == 3:
                    link(nc.vector.tensor_reduce(total, h_tok[:], AX.X, ALU.add))
                elif n == 4:
                    nc.vector.tensor_scalar(var, total, 1.0 / D, LN_EPS, ALU.mult, ALU.add).then_inc(var_ready, 1)
                elif n == 5:
                    dve.wait_ge(rstd_ready, count)
                    link(nc.vector.tensor_tensor(centred[:], centred[:], spread(rstd, 2, D), ALU.mult))
                elif n == 6:
                    link(nc.vector.tensor_tensor(centred[:], centred[:], scale, ALU.mult))
                else:
                    if before_dst is not None:
                        dve.wait_ge(*before_dst)
                    nc.vector.tensor_tensor(dst, centred[:], shift, ALU.add).then_inc(ready, 1)

            def tiles_of(b):
                return xt[:, bass.ds(b * TB, TB), :] if not isinstance(b, int) else xt[:, b * TB:(b + 1) * TB, :]

            def row(j, b):
                return spread(mod[:, j, bass.ds(b, 1), :].rearrange("p o d -> p (o d)"), 1, TB)

            def first_norm(link, n, b, count):
                norm_step(link, n, tiles_of(b), h_tok[:], row(1, b), row(0, b), count, h_ready)

            def second_norm(link, n, b, count):
                norm_step(link, n, tiles_of(b), tiles_of(b), row(4, b), row(3, b), count, h2_ready, (x_stored, 16 * b + 16))

            def q_and_k(b, h):
                s, g = h % 2, b * H + h
                if not (isinstance(b, int) and g < 2):
                    dve.wait_ge(st_full[3], 4 * (g - 1))
                for k in range(2):
                    cols = slice(k * HALF, (k + 1) * HALF)
                    bank = ring[bank_of(located(b, "p", h, k))]
                    dve.wait_ge(hi_ready, 6 * g + 3 * k + 3)
                    nc.vector.tensor_tensor(q_lm[s][0:R, cols], bank[0:R, :], q_hh[s][0:R, cols].bitcast(F32), ALU.subtract).then_inc(lo_ready, 1)
                    nc.vector.tensor_tensor(k_hl[s][R:P, cols], bank[R:P, :], k_hl[s][0:R, cols].bitcast(F32), ALU.subtract).then_inc(lo_ready, 1)

            def row_maxima(b, h, i):
                if i == 0 and not (isinstance(b, int) and b * H + h == 0):
                    dve.wait_ge(max_ready, b * H + h)
                for k in range(2):
                    at = located(b, "a", h, i, k)
                    wait_full(b, at)
                    nc.vector.tensor_reduce(maxes[:, i, k:k + 1], ring[bank_of(at)][:], AX.X, ALU.max).then_inc(rows_maxed, 1)

            def whole_max(b, h):
                g = b * H + h
                dve.wait_ge(rows_maxed, (g + 1) * 2 * TB + 1)
                if not (isinstance(b, int) and g == 0):
                    dve.wait_ge(neg_ready, 2 * g + 1)
                nc.vector.tensor_tensor(row_max[:], maxes[:, :, 0], maxes[:, :, 1], ALU.max).then_inc(max_ready, 1)

            def gather_output(link, g, h, half, j):
                u, tile = 2 * g + half, 4 * half + j
                dve.wait_ge(o_full[j % 2], 2 * u + j // 2 + 1)
                o = obank[j % 2]
                link(nc.vector.reciprocal(recip[:, tile:tile + 1], o[:, D:D + 1]))
                if h % H == 0:
                    out = nc.vector.tensor_scalar(acc[:, tile, :], o[:, 0:D], recip[:, tile:tile + 1], None, ALU.mult)
                else:
                    dve.wait_ge(o_read[j % 2], 2 * u + j // 2 + 1)
                    out = nc.vector.scalar_tensor_tensor(acc[:, tile, :], o[:, 0:D], recip[:, tile:tile + 1], acc[:, tile, :], ALU.mult, ALU.add)
                out.then_inc(o_read[j % 2], 1)

            def residual(link, b):
                for r in range(2):
                    dve.wait_ge(o_read[r], (b + 1) * (4 * H) + 1)
                link(nc.vector.tensor_tensor(acc[:], acc[:], row(2, b), ALU.mult))
                nc.vector.tensor_tensor(tiles_of(b), tiles_of(b), acc[:], ALU.add).then_inc(x_ready, 1)
                dve.wait_ge(x_ready, b + 1)

            def body(b, first, last, base):
                link = Chain(dve, steps, base)
                for h in range(H):
                    more = not (last and h == H - 1)
                    for s in range(2 * TB):
                        if 3 <= s <= 10 and more:
                            row_maxima(b, h + 1, s - 3)
                            if s == 10:
                                whole_max(b, h + 1)
                        behind, half, i = product_at(s)
                        if i % 2 == 1 and not (first and h < behind):
                            gather_output(link, b * H + h - behind, h - behind, half, i // 2)
                        if s == 9 and h == 0 and not first:
                            residual(link, b - 1)
                        if s >= 11 and h in (1, 2) and not first:
                            if h == 1:
                                second_norm(link, s - 11, b - 1, None)
                            elif s >= 13:
                                second_norm(link, s - 8, b - 1, 2 * b + 1)
                        if s >= 11 and h in (3, 4) and not last:
                            if h == 3:
                                first_norm(link, s - 11, b + 1, None)
                            elif s >= 13:
                                first_norm(link, s - 8, b + 1, 2 * b + 2)
                    if not (last and h >= H - 2):
                        q_and_k(b, h + 2)
                return link.n

            link = Chain(dve, steps, 0)
            dve.wait_ge(w_loaded, 48)
            link(nc.vector.tensor_copy(ident_r[:], ident[:]))
            dve.wait_ge(first_x_loaded, 16)
            for n in range(8):
                first_norm(link, n, 0, 1)
            q_and_k(0, 0)
            for i in range(TB):
                row_maxima(0, 0, i)
            whole_max(0, 0)
            q_and_k(0, 1)
            done = link.n
            dve.wait_ge(x_loaded, 16 * (B - 1))
            done += body(0, True, False, done)
            with dve.Fori(1, B - 1) as b:
                n = body(b, False, False, done + (b - 1) * STEPS_LOOP)
                assert n == STEPS_LOOP, n
            done += (B - 2) * STEPS_LOOP
            done += body(B - 1, False, True, done)
            link = Chain(dve, steps, done)
            gather_output(link, B * H - 1, H - 1, 0, 3)
            for j in range(4):
                gather_output(link, B * H - 1, H - 1, 1, j)
            residual(link, B - 1)
            for n in range(8):
                second_norm(link, n, B - 1, 2 * B)

        @block.tensor
        def _(pe):
            pe.wait_ge(w_loaded, 48)
            pe.wait_ge(consts, 5)

            def take(b, at):
                if at >= 2:
                    sem_, count = released(b, at - 2)
                    pe.wait_ge(sem_, count + 1)
                return ring[bank_of(at)]

            def give(at, instruction):
                instruction.then_inc(ring_full[bank_of(at)], 1)

            def turn_h(b, ahead):
                pe.wait_ge(h_ready, b + ahead + 1)
                for k in range(2):
                    at = located(b, "t", ahead, k)
                    bank = take(b, at)
                    for i in range(4):
                        mm = nc.tensor.transpose(bank[:, i * P:(i + 1) * P], h_tok[:, 4 * k + i, :], ident[:])
                    give(at, mm)

            def q_and_k(b, h, batch):
                pe.wait_ge(hT_ready, 2 * batch + 3)
                for k in range(2):
                    at = located(b, "p", h, k)
                    bank = take(b, at)
                    give(at, nc.tensor.matmul(bank[:], w_qk_sb[:, h % H, :], hT[:, k * HALF:(k + 1) * HALF], start=True, stop=True))

            def v_of(b, h):
                for k in range(2):
                    at = located(b, "v", h, k)
                    bank = take(b, at)
                    for i in range(4):
                        t = 4 * k + i
                        mm = nc.tensor.matmul(bank[:, i * D:(i + 1) * D], hT[:, t * P:(t + 1) * P], wv_sb[:, h % H, :], start=True, stop=True)
                    give(at, mm)

            def score_rows(b, h, i):
                s = h % 2
                if i == 0:
                    pe.wait_ge(lo_ready, (b * H + h) * 4 + 5)
                for k in range(2):
                    at = located(b, "a", h, i, k)
                    bank = take(b, at)
                    give(at, nc.tensor.matmul(bank[:], q_hh[s][:, i * P:(i + 1) * P], k_hl[s][:, k * HALF:(k + 1) * HALF], start=True, stop=True))

            def turn_max(b, h):
                pe.wait_ge(max_ready, b * H + h + 1)
                for k in range(2):
                    at = located(b, "r", h, k)
                    bank = take(b, at)
                    for i in range(4):
                        mm = nc.tensor.matmul(bank[0:1, i * P:(i + 1) * P], row_max[:, 4 * k + i:4 * k + i + 1], ident_r[:], start=True, stop=True)
                    give(at, mm)

            def scores(b, h, s):
                g, w, half, i = b * H + h, h % 2, s // TB, s % TB
                if s == 0:
                    pe.wait_ge(neg_ready, 2 * g + 3)
                    pe.wait_ge(k2_ready, g + 1)
                if not (isinstance(g, int) and g == 0 and s < 4):
                    pe.wait_ge(st_free[s % 4], 4 * g + s // 4 + 1)
                keys, queries = slice(i * P, (i + 1) * P), slice(half * HALF, (half + 1) * HALF)
                nc.tensor.matmul(st[s % 4], k_hl[w][:, keys], q_hh[w][:, queries], start=True, stop=False)
                nc.tensor.matmul(st[s % 4], k_h1[w][:, keys], q_lm[w][:, queries], start=False, stop=True).then_inc(st_full[s % 4], 1)

            def products(g, h, half, i):
                u, j = 2 * g + half, i // 2
                if i == 0:
                    for r in range(4):
                        pe.wait_ge(st_free[r], 2 * u + 3)
                    pe.wait_ge(v_ready, 2 * g + 3)
                if i % 2 == 0:
                    pe.wait_ge(o_read[j % 2], 2 * u + j // 2 + 1)
                cols = slice(j * P, (j + 1) * P)
                for m in range(4 * (i % 2), 4 * (i % 2) + 4):
                    mm = nc.tensor.matmul(obank[j % 2][:, 0:D + 1], probs[:, half, m, cols], v_one[h % 2][:, m, :], start=(m == 0), stop=(m == TB - 1))
                if i % 2 == 1:
                    mm.then_inc(o_full[j % 2], 1)

            def body(b, first, last):
                for h in range(H):
                    more = not (last and h == H - 1)
                    for s in range(2 * TB):
                        scores(b, h, s)
                        if 3 <= s <= 10 and more:
                            score_rows(b, h + 1, s - 3)
                        behind, half, i = product_at(s)
                        if not (first and h < behind):
                            products(b * H + h - behind, h - behind, half, i)
                        if s == 11 and more:
                            v_of(b, h + 1)
                        if s == 12 and more:
                            turn_max(b, h + 1)
                        if s == 13 and h == H - 2 and not last:
                            turn_h(b, 1)
                    if not (last and h >= H - 2):
                        q_and_k(b, h + 2, b + (h + 2) // H)

            turn_h(0, 0)
            q_and_k(0, 0, 0)
            for i in range(TB):
                score_rows(0, 0, i)
            v_of(0, 0)
            turn_max(0, 0)
            q_and_k(0, 1, 0)
            batches(pe, body)
            for i in (6, 7):
                products(B * H - 1, H - 1, 0, i)
            for i in range(TB):
                products(B * H - 1, H - 1, 1, i)


def build_product_key_table(nc, a, hc, ones, half_neg, ident, banks, wide, w_eff, sim_bias, mean_col,
                            expert_loads, count, half_mask, low_ids, mask_b):
    ntok = TT * P
    with ExitStack() as ctx:
        def sb(name, shape, dt=F32):
            return ctx.enter_context(nc.sbuf_tensor(name, shape, dt))

        def sem(name):
            return ctx.enter_context(nc.semaphore(name))

        wq_sb = sb("pk_wq", [P, G, P])
        wqT = sb("pk_wqT", [P, G, D])
        keysT = sb("keysT", [P, G, NK])
        keys_s = sb("keys_scaled", [P, G, NK])
        gamma = sb("pk_gamma", [P, G])
        beta = sb("pk_beta", [P, G])
        tile_sum = sb("tile_sum", [P, D])
        mean_b = sb("mean_b", [P, D])
        cov = sb("cov", [P, D])
        prod = sb("pk_prod", [P, 4, D])
        var = sb("pk_var", [P, 4, G])
        loaded = sem("pk_loaded")
        experts_loaded = sem("pk_experts_loaded")
        consts_made = sem("pk_consts_made")
        var_ready = sem("pk_var_ready")
        rstd_ready = sem("pk_rstd")
        tile_sum_ready = sem("pk_tile_sum")
        sum_done = sem("pk_sum")
        mean_ready = sem("pk_mean")
        hc_ready = sem("pk_hc")
        gram_done = sem("pk_gram")
        cov_ready = sem("pk_cov")
        wc_full = sem("pk_wc_full")
        wc_read = sem("pk_wc_read")
        keys_ready = sem("pk_keys")
        bias_done = sem("pk_bias")
        tables_done = sem("pk_tables")
        steps = sem("pk_steps")
        block = ctx.enter_context(nc.Block())

        @block.sync
        def _(sp):
            for dst, src in ((wq_sb, "w_q"), (wqT, "w_qT"), (keysT, "keysT"), (gamma, "bn_gamma"), (beta, "bn_beta")):
                sp.dma_start(dst[:], a[src]).then_inc(loaded, 16)
            for dst, src in expert_loads:
                sp.dma_start(dst[:], a[src]).then_inc(experts_loaded, 16)
            sp.wait_ge(experts_loaded, 64)

        @block.scalar
        def _(act):
            act.wait_ge(experts_loaded, 64)
            nc.scalar.activation(low_ids[:], spread(count[:], 2, P), ACT.Copy).then_inc(consts_made, 1)
            nc.scalar.activation(mask_b[:], spread(half_mask[:], 2, P), ACT.Copy).then_inc(consts_made, 1)

        @block.gpsimd
        def _(pool):
            pool.wait_ge(var_ready, 1)
            nc.gpsimd.tensor_tensor(var[:, 2, :], var[:, 1, :], half_neg[:, 0:G], ALU.pow).then_inc(rstd_ready, 1)

        @block.vector
        def _(dve):
            link = Chain(dve, steps, 0)
            nc.vector.tensor_reduce(tile_sum[:], hc[:].rearrange("p t d -> p d t"), AX.X, ALU.add).then_inc(tile_sum_ready, 1)
            dve.wait_ge(sum_done, 1)
            nc.vector.tensor_scalar(mean_b[:], banks[0][:, 0:D], 1.0 / ntok, None, ALU.mult).then_inc(mean_ready, 1)
            dve.wait_ge(mean_ready, 1)
            for b in range(B):
                tiles = slice(b * TB, (b + 1) * TB)
                nc.vector.tensor_tensor(hc[:, tiles, :], hc[:, tiles, :], spread(mean_b[:], 1, TB), ALU.subtract).then_inc(hc_ready, 1)
            dve.wait_ge(sum_done, 2)
            link(nc.vector.tensor_scalar(mean_col[:], banks[1][:, 0:1], 1.0 / ntok, None, ALU.mult))
            dve.wait_ge(bias_done, 1)
            link(nc.vector.tensor_copy(sim_bias[:], wide[0:1, 512:1024]))
            dve.wait_ge(gram_done, 1)
            nc.vector.tensor_scalar(cov[:], banks[0][:, 0:D], 1.0 / ntok, None, ALU.mult).then_inc(cov_ready, 1)
            for k in range(4):
                groups = slice(4 * k, 4 * k + 4)
                dve.wait_ge(wc_full, k + 1)
                nc.vector.tensor_tensor(prod[:], banks[2 + k % 2][:].rearrange("p (g d) -> p g d", g=4), wqT[:, groups, :], ALU.mult).then_inc(wc_read, 1)
                dve.wait_ge(wc_read, k + 1)
                link(nc.vector.tensor_reduce(var[:, 0, groups], prod[:], AX.X, ALU.add))
            nc.vector.tensor_scalar(var[:, 1, :], var[:, 0, :], BN_EPS, None, ALU.add).then_inc(var_ready, 1)
            dve.wait_ge(rstd_ready, 1)
            link(nc.vector.tensor_tensor(var[:, 3, :], var[:, 2, :], gamma[:], ALU.mult))
            nc.vector.tensor_tensor(keys_s[:], keysT[:], spread(var[:, 3, :], 2, NK), ALU.mult).then_inc(keys_ready, 1)
            dve.wait_ge(tables_done, 1)
            link(nc.vector.tensor_copy(w_eff[:], wide[:, 0:512]))
            dve.wait_ge(consts_made, 2)

        @block.tensor
        def _(pe):
            pe.wait_ge(tile_sum_ready, 1)
            nc.tensor.matmul(banks[0][:, 0:D], ones[:], tile_sum[:], start=True, stop=True).then_inc(sum_done, 1)
            nc.tensor.matmul(banks[1][:, 0:1], tile_sum[:], ones[:, 0:1], start=True, stop=True).then_inc(sum_done, 1)
            pe.wait_ge(loaded, 80)
            for g in range(G):
                mm = nc.tensor.matmul(wide[0:1, 512 + g * NK:512 + (g + 1) * NK], beta[:, g:g + 1], keysT[:, g, :], start=True, stop=True)
            mm.then_inc(bias_done, 1)
            pe.wait_ge(mean_ready, 1)
            for t in range(TT):
                if t % TB == 0:
                    pe.wait_ge(hc_ready, t // TB + 1)
                mm = nc.tensor.matmul(banks[0][:, 0:D], hc[:, t, :], hc[:, t, :], start=(t == 0), stop=(t == TT - 1))
            mm.then_inc(gram_done, 1)
            pe.wait_ge(cov_ready, 1)
            for k in range(4):
                if k >= 2:
                    pe.wait_ge(wc_read, k - 1)
                for g in range(4):
                    mm = nc.tensor.matmul(banks[2 + k % 2][:, g * D:(g + 1) * D], wq_sb[:, 4 * k + g, :], cov[:], start=True, stop=True)
                mm.then_inc(wc_full, 1)
            pe.wait_ge(keys_ready, 1)
            for g in range(G):
                mm = nc.tensor.matmul(wide[:, g * NK:(g + 1) * NK], wqT[:, g, :], keys_s[:, g, :], start=True, stop=True)
            mm.then_inc(tables_done, 1)


PAIRS = TT // 2
STEPS_HOTS = 3


def build_experts(nc, x2, x_scratch, hc, ident, ones, banks, wide, w_eff, sim_bias, mean_col, count, low_ids, mask_b, downT, up):
    with ExitStack() as ctx:
        def sb(name, shape, dt=F32):
            return ctx.enter_context(nc.sbuf_tensor(name, shape, dt))

        def sem(name):
            return ctx.enter_context(nc.semaphore(name))

        low_hot = sb("low_hot", [P, P, P], BF16)
        hcT = sb("hcT", [P, 2 * P])
        hT = sb("pk_hT", [P, 2 * P])
        act_g = sb("act_g", [P, 8, 2 * P])
        z = sb("z", [P, 8, 2, P])
        sims = sb("sims", [P, 2, 2, H, NK])
        top = sb("top", [P, 2, 2, H, TOPK])
        top_i = sb("top_i", [P, 2, 2, H, TOPK], U32)
        top_f = sb("top_f", [P, 2, TOPK, 2 * H], BF16)
        cand = sb("cand", [P, 2 * H, TOPK, TOPK])
        best = sb("best", [P, 2 * H, TOPK])
        best_i = sb("best_i", [P, 2 * H, TOPK], U32)
        rank_u = sb("rank_u", [P, 2, 2 * H, TOPK], U32)
        rank_f = sb("rank_f", [P, 2, P], BF16)
        hot = sb("hot", [P, 2, TOPK, P], BF16)
        chosen = sb("chosen", [P, 2, P], BF16)
        chosen_u = sb("chosen_u", [P, 3, P], U32)
        to_turn = sb("to_turn", [P, 3, P])
        expd = sb("expd", [P, 2 * H, TOPK])
        tot = sb("tot", [P, 2, 2 * H])
        ids = sb("ids", [P, 2, P], BF16)
        rest = sb("rest", [P, P])
        parts = sb("parts", [P, 3, P], BF16)
        parts_m = sb("parts_m", [P, 3, 2, P], BF16)
        high_hot = sb("high_hot", [P, 8, P], BF16)
        value_hot = sb("value_hot", [P, 6, 8, P], BF16)

        hc_stage = sb("hc_stage", [P, 2, D])
        stage_ready = sem("ex_stage")
        x_back = sem("ex_x_back")
        turns = sem("ex_turns")
        apart = sem("ex_apart")
        steps = sem("ex_steps")
        turned_h = sem("ex_turned_h")
        hT_ready = sem("ex_hT")
        sims_full = sem("ex_sims_full")
        sims_read = sem("ex_sims_read")
        less_max = sem("ex_less_max")
        exp_done = sem("ex_exp")
        to_turn_ready = sem("ex_to_turn")
        turned = sem("ex_turned")
        ids_ready = sem("ex_ids")
        parts_ready = sem("ex_parts")
        rest_ready = sem("ex_rest")
        hots_ready = sem("ex_hots")
        g_full = sem("ex_g_full")
        g_ready = sem("ex_g_ready")
        w_full = sem("ex_w_full")
        z_ready = sem("ex_z")
        out_full = sem("ex_out_full")
        out_read = sem("ex_out_read")
        sim_bank = [banks[2], banks[3]]
        turn_bank, h_bank = banks[0], banks[1]
        block = ctx.enter_context(nc.Block())

        @block.sync
        def _(sp):
            sp.dma_start(x2[:], x_scratch).then_inc(x_back, 16)
            sp.wait_ge(x_back, 16)


        @block.scalar
        def _(act):
            def front(u):
                act.wait_ge(turned_h, u + 1)
                nc.scalar.activation(hcT[:], h_bank[:, 0:2 * P], ACT.Copy).then_inc(hT_ready, 1)
                nc.scalar.activation(hT[:], h_bank[:, 0:2 * P], ACT.Identity, bias=mean_col[:]).then_inc(hT_ready, 1)
                for q in range(2):
                    act.wait_ge(sims_full, 2 * u + q + 1)
                    nc.scalar.activation(sims[:, q].rearrange("p s h k -> p (s h k)"), sim_bank[q][:], ACT.Copy).then_inc(sims_read, 1)

            def exponentials(u):
                act.wait_ge(less_max, u + 1)
                nc.scalar.activation(expd[:], expd[:], ACT.Exp).then_inc(exp_done, 1)

            def turned_ids(u):
                act.wait_ge(turned, u + 1)
                nc.scalar.activation(ids[:], turn_bank[:, 0:256].rearrange("p (s t) -> p s t", s=2), ACT.Copy).then_inc(ids_ready, 1)
                nc.scalar.activation(parts[:, 0, :], turn_bank[:, 256:384], ACT.Copy).then_inc(parts_ready, 1)
                act.wait_ge(rest_ready, u + 1)
                nc.scalar.activation(parts[:, 1, :], rest[:], ACT.Copy).then_inc(parts_ready, 1)

            def activations(u):
                for k in range(2):
                    act.wait_ge(g_full, 2 * u + k + 1)
                    nc.scalar.activation(act_g[:, 4 * k:4 * k + 4, :], wide[k][:].rearrange("p (e t) -> p e t", e=4),
                                         ACT.Gelu_apprx_tanh).then_inc(g_ready, 1)

            def back(u):
                act.wait_ge(out_full, u + 1)
                nc.scalar.activation(hc[:, bass.ds(2 * u, 2), :], turn_bank[:, 0:256].rearrange("p (q d) -> p q d", q=2), ACT.Copy).then_inc(out_read, 1)

            nc.scalar.sem_inc(out_read, 1)
            front(0)
            exponentials(0)
            turned_ids(0)
            activations(0)
            front(1)
            with act.Fori(0, PAIRS - 2) as u:
                exponentials(u + 1)
                turned_ids(u + 1)
                activations(u + 1)
                front(u + 2)
                back(u)
            exponentials(PAIRS - 1)
            turned_ids(PAIRS - 1)
            activations(PAIRS - 1)
            back(PAIRS - 2)
            back(PAIRS - 1)

        @block.vector
        def _(dve):
            def front(u, base):
                link = Chain(dve, steps, base)
                dve.wait_ge(sims_read, 2 * u + 2)
                nc.vector.sem_inc(apart, 1)
                for q in range(2):
                    for s in range(2):
                        for h in range(H):
                            last = nc.vector.max(top[:, s, q, h, :], sims[:, q, s, h, :])
                link(last)
                nc.vector.sem_inc(apart, 1)
                for q in range(2):
                    for s in range(2):
                        for h in range(H):
                            last = nc.vector.max_index(top_i[:, s, q, h, :], top[:, s, q, h, :], sims[:, q, s, h, :])
                link(last)
                topv = top[:].rearrange("p s q h k -> p s (q h) k")
                nc.vector.tensor_copy(top_f[:], top_i[:].rearrange("p s q h k -> p s k (q h)")).then_inc(steps, 1)
                link.n += 1
                link(nc.vector.tensor_tensor(cand[:], spread(topv[:, 0], 3, TOPK), spread(topv[:, 1], 2, TOPK), ALU.add))
                nc.vector.sem_inc(apart, 1)
                for g in range(2 * H):
                    last = nc.vector.max(best[:, g, :], cand[:, g].rearrange("p i j -> p (i j)"))
                link(last)
                nc.vector.sem_inc(apart, 1)
                for g in range(2 * H):
                    last = nc.vector.max_index(best_i[:, g, :], best[:, g, :], cand[:, g].rearrange("p i j -> p (i j)"))
                link(last)
                nc.vector.tensor_tensor(expd[:], best[:], spread(best[:, :, 0], 2, TOPK), ALU.subtract).then_inc(less_max, 1)
                nc.vector.tensor_scalar(rank_u[:, 0], best_i[:], 3, None, ALU.logical_shift_right).then_inc(steps, 1)
                link.n += 1
                link(nc.vector.tensor_scalar(rank_u[:, 1], best_i[:], 7, None, ALU.bitwise_and))
                link(nc.vector.tensor_copy(rank_f[:].rearrange("p s (k g) -> p s k g", k=TOPK), rank_u[:].rearrange("p s g k -> p s k g")))
                link(nc.vector.tensor_tensor(hot[:], spread(rank_f[:], 2, TOPK), spread(low_ids[:, 0:TOPK, :], 1, 2), ALU.is_equal))
                hot4 = hot[:].rearrange("p s j (k g) -> p (s j) k g", k=TOPK)
                link(nc.vector.tensor_tensor(hot4, hot4, spread(top_f[:].rearrange("p s j g -> p (s j) g"), 2, TOPK), ALU.mult))
                dve.wait_ge(exp_done, u + 1)
                nc.vector.sem_inc(apart, 1)
                nc.vector.tensor_reduce(tot[:, 0, :], expd[:], AX.X, ALU.add).then_inc(steps, 1)
                link.n += 1
                link(nc.vector.tensor_tensor(hot[:, :, 0:4], hot[:, :, 0:4], hot[:, :, 4:8], ALU.add))
                nc.vector.reciprocal(tot[:, 1, :], tot[:, 0, :]).then_inc(steps, 1)
                link.n += 1
                link(nc.vector.tensor_tensor(hot[:, :, 0:2], hot[:, :, 0:2], hot[:, :, 2:4], ALU.add))
                link(nc.vector.tensor_tensor(chosen[:], hot[:, :, 0], hot[:, :, 1], ALU.add))
                link(nc.vector.scalar_tensor_tensor(chosen_u[:, 0, :], chosen[:, 0, :], float(NK), chosen[:, 1, :], ALU.mult, ALU.add))
                nc.vector.tensor_scalar(chosen_u[:, 1, :], chosen_u[:, 0, :], 127, None, ALU.bitwise_and).then_inc(steps, 1)
                link.n += 1
                link(nc.vector.tensor_scalar(chosen_u[:, 2, :], chosen_u[:, 0, :], 7, None, ALU.logical_shift_right))
                nc.vector.tensor_copy(to_turn[:, 0:2, :], chosen_u[:, 1:3, :]).then_inc(steps, 1)
                link.n += 1
                nc.vector.tensor_tensor(to_turn[:, 2, :].rearrange("p (k g) -> p g k", g=2 * H), expd[:],
                                        spread(tot[:, 1, :], 2, TOPK), ALU.mult).then_inc(to_turn_ready, 1)
                return link.n

            def one_hots(u, base):
                link = Chain(dve, steps, base)
                dve.wait_ge(ids_ready, u + 1)
                dve.wait_ge(parts_ready, 2 * u + 1)
                nc.vector.tensor_tensor(rest[:], turn_bank[:, 256:384], parts[:, 0, :], ALU.subtract).then_inc(rest_ready, 1)
                nc.vector.tensor_tensor(low_hot[:], spread(ids[:, 0, :], 1, P), low_ids[:], ALU.is_equal).then_inc(hots_ready, 1)
                nc.vector.tensor_tensor(high_hot[:], spread(ids[:, 1, :], 1, 8), low_ids[:, 0:8, :], ALU.is_equal).then_inc(steps, 1)
                link.n += 1
                dve.wait_ge(rest_ready, u + 1)
                dve.wait_ge(parts_ready, 2 * u + 2)
                link(nc.vector.tensor_tensor(parts[:, 2, :], rest[:], parts[:, 1, :], ALU.subtract))
                link(nc.vector.tensor_tensor(parts_m[:], spread(parts[:], 2, 2), spread(mask_b[:], 1, 3), ALU.mult))
                nc.vector.tensor_tensor(value_hot[:], spread(high_hot[:], 1, 6),
                                        spread(parts_m[:].rearrange("p s q t -> p (s q) t"), 2, 8), ALU.mult).then_inc(hots_ready, 1)
                return link.n

            def weigh(u):
                dve.wait_ge(g_ready, 2 * u + 2)
                for k in range(4):
                    dve.wait_ge(w_full, 4 * u + k + 1)
                    tok = slice(32 * k, 32 * k + 32)
                    w = wide[k // 2][:, 512 * (k % 2):512 * (k % 2) + 512].rearrange("p (t q e) -> p q e t", q=2, e=8)
                    nc.vector.tensor_tensor(z[:, :, :, tok].rearrange("p e q t -> p q e t"), w,
                                            act_g[:].rearrange("p e (q t) -> p q e t", q=2)[:, :, :, tok], ALU.mult).then_inc(z_ready, 1)

            n_front = front(0, 0)
            n_all = n_front + STEPS_HOTS
            with dve.Fori(0, PAIRS - 1) as u:
                base = u * n_all + n_front
                n = one_hots(u, base)
                assert n == STEPS_HOTS, n
                assert front(u + 1, base + n) == n_front
                weigh(u)
            one_hots(PAIRS - 1, (PAIRS - 1) * n_all + n_front)
            weigh(PAIRS - 1)

        @block.tensor
        def _(pe):
            def front(u):
                for q in range(2):
                    src = hc[:, 2 * u + q, :] if isinstance(u, int) else hc_stage[:, q, :]
                    mm = nc.tensor.transpose(h_bank[:, q * P:(q + 1) * P], src, ident[:])
                mm.then_inc(turned_h, 1)
                pe.wait_ge(hT_ready, 2 * u + 1)
                if not (isinstance(u, int) and u == 0):
                    pe.wait_ge(sims_read, 2 * u)
                for q in range(2):
                    nc.tensor.matmul(sim_bank[q][:], hcT[:, q * P:(q + 1) * P], w_eff[:], start=True, stop=False)
                    nc.tensor.matmul(sim_bank[q][:], ones[0:1, :], sim_bias[:], start=False, stop=True).then_inc(sims_full, 1)

            def activations(u):
                pe.wait_ge(hT_ready, 2 * u + 2)
                for k in range(2):
                    for e in range(4):
                        col = (4 * k + e) * P
                        mm = nc.tensor.matmul(wide[k][:, e * 2 * P:(e + 1) * 2 * P], downT[:, col:col + P], hT[:], start=True, stop=True)
                    mm.then_inc(g_full, 1)

            def turn(u):
                pe.wait_ge(to_turn_ready, u + 1)
                if not (isinstance(u, int) and u == 0):
                    pe.wait_ge(out_read, u)
                for s in range(3):
                    mm = nc.tensor.transpose(turn_bank[:, s * P:(s + 1) * P], to_turn[:, s, :], ident[:])
                mm.then_inc(turned, 1)

            def expert_weights(u):
                pe.wait_ge(hots_ready, 2 * u + 2)
                pe.wait_ge(g_ready, 2 * u + 2)
                for t in range(P):
                    col = 512 * (t // 32 % 2) + 16 * (t % 32)
                    for part in range(3):
                        mm = nc.tensor.matmul(wide[t // 64][:, col:col + 16], low_hot[:, :, t],
                                              value_hot[:, 2 * part:2 * part + 2, :, t].rearrange("p q e -> p (q e)"),
                                              start=(part == 0), stop=(part == 2))
                    if t % 32 == 31:
                        mm.then_inc(w_full, 1)

            def combine(u):
                pe.wait_ge(z_ready, 4 * u + 4)
                if not (isinstance(u, int) and u == PAIRS - 1):
                    pe.wait_ge(parts_ready, 2 * u + 3)
                    pe.wait_ge(rest_ready, u + 2)
                else:
                    pe.wait_ge(out_read, u + 1)
                for q in range(2):
                    for e in range(8):
                        mm = nc.tensor.matmul(turn_bank[:, q * D:(q + 1) * D], z[:, e, q, :], up[:, e, :], start=(e == 0), stop=(e == 7))
                mm.then_inc(out_full, 1)

            front(0)
            turn(0)
            activations(0)
            front(1)
            with pe.Fori(0, PAIRS - 2) as u:
                expert_weights(u)
                turn(u + 1)
                pe.wait_ge(z_ready, 4 * u + 4)
                activations(u + 1)
                pe.wait_ge(stage_ready, u + 1)
                front(u + 2)
                combine(u)
            expert_weights(PAIRS - 2)
            turn(PAIRS - 1)
            combine(PAIRS - 2)
            activations(PAIRS - 1)
            expert_weights(PAIRS - 1)
            combine(PAIRS - 1)

        @block.gpsimd
        def _(pool):
            with pool.Fori(1, PAIRS - 1) as u:
                pool.wait_ge(turned_h, u + 1)
                nc.gpsimd.sem_inc(turns, 1)
                nc.gpsimd.tensor_copy(hc_stage[:], hc[:, bass.ds(2 * u + 2, 2), :]).then_inc(stage_ready, 1)


STEPS_SECOND = 16


def build_second_layer(nc, a, xt, hc, gate0, mod, gate1, ident, half_neg, ring, obank, wide, out):
    with ExitStack() as ctx:
        def sb(name, shape, dt=F32):
            return ctx.enter_context(nc.sbuf_tensor(name, shape, dt))

        def sem(name):
            return ctx.enter_context(nc.semaphore(name))

        w_qkva = sb("w_qkva", [P, 3 * D])
        w_rkv = sb("w_rkv", [P, 3, D])
        cols = sb("cols", [P, 4])
        mod_cols = sb("mod_cols", [P, B, 2])
        mod_col = sb("mod_col", [P, 2])
        half_pos = sb("half_pos", [P, TB])
        centred = {r: sb(f"l1_centred_{r}", [P, TB, D]) for r in ("scan", "mix")}
        h_tok = {r: sb(f"l1_h_{r}", [P, TB, D]) for r in ("scan", "mix")}
        stats = {r: sb(f"l1_stats_{r}", [P, 4, TB]) for r in ("scan", "mix")}
        norms = sb("norms", [P, 4, TB])
        xnT = sb("xnT", [P, N])
        decay = sb("decay", [P, N])
        scanned = sb("scanned", [P, N])
        y = sb("y", [P, N])
        shifted = sb("shifted", [P, N + 1])
        w_now = sb("w_now", [P, 2, D])
        w_prev = sb("w_prev", [P, 2, D])
        rgate = sb("rgate", [P, N])
        kact = sb("kact", [P, N])
        loaded = sem("l1_loaded")
        consts = sem("l1_consts")
        centred_ready = {r: sem(f"l1_centred_ready_{r}") for r in ("scan", "mix")}
        squared = {r: sem(f"l1_squared_{r}") for r in ("scan", "mix")}
        mod_turned = sem("l1_mod_turned")
        mod_cols_ready = sem("l1_mod_cols")
        steps = sem("l1_steps")
        experts_scaled = sem("l1_experts_scaled")
        experts_added = sem("l1_experts_added")
        var_ready = sem("l1_var")
        rstd_ready = sem("l1_rstd")
        scan_h_ready = sem("l1_scan_h")
        scan_turned = sem("l1_scan_turned")
        xnT_ready = sem("l1_xnT")
        qkva_full = sem("l1_qkva")
        decay_ready = sem("l1_decay")
        y_ready = sem("l1_y")
        y_back = sem("l1_y_back")
        y_read = sem("l1_y_read")
        mix_h_ready = sem("l1_mix_h")
        mix_turned = sem("l1_mix_turned")
        shifted_ready = sem("l1_shifted")
        weights_ready = sem("l1_weights")
        r_full = sem("l1_r_full")
        k_full = sem("l1_k_full")
        relu_ready = sem("l1_relu")
        rgate_ready = sem("l1_rgate")
        kact_ready = sem("l1_kact")
        v_full = sem("l1_v")
        rv_ready = sem("l1_rv")
        mix_back = sem("l1_mix_back")
        mix_read = sem("l1_mix_read")
        x_ready = sem("l1_x")
        apart = sem("l1_apart")
        stored = sem("stored")
        mix_banks = [ring[1], obank[1]]
        block = ctx.enter_context(nc.Block())

        def half(k):
            return slice(k * HALF, (k + 1) * HALF)

        @block.sync
        def _(sp):
            sp.dma_start(w_qkva[:], a["w_qkva"]).then_inc(loaded, 16)
            sp.dma_start(w_rkv[:], a["w_rkv"]).then_inc(loaded, 16)
            sp.dma_start(cols[:, 0:3], a["cols"]).then_inc(loaded, 16)
            with sp.Fori(0, B) as b:
                sp.wait_ge(x_ready, b + 1)
                sp.dma_start(out[:, bass.ds(b * TB, TB), :], xt[:, bass.ds(b * TB, TB), :]).then_inc(stored, 16)
            sp.wait_ge(stored, 16 * B)

        @block.gpsimd
        def _(pool):
            def add_experts(b):
                tiles = bass.ds(b * TB, TB)
                gate = spread(gate0[:, bass.ds(b, 1), :].rearrange("p o d -> p (o d)"), 1, TB)
                nc.gpsimd.tensor_tensor(hc[:, tiles, :], hc[:, tiles, :], gate, ALU.mult).then_inc(experts_scaled, 1)
                pool.wait_ge(experts_scaled, b + 1)
                nc.gpsimd.tensor_tensor(xt[:, tiles, :], xt[:, tiles, :], hc[:, tiles, :], ALU.add).then_inc(experts_added, 1)

            def rstd(which, n):
                pool.wait_ge(var_ready, n)
                nc.gpsimd.tensor_tensor(stats[which][:, 3, :], stats[which][:, 2, :], half_neg[:, 0:TB], ALU.pow).then_inc(rstd_ready, 1)

            def scan_roots(b):
                rstd("scan", 3 * b + 1)
                pool.wait_ge(var_ready, 3 * b + 2)
                nc.gpsimd.tensor_tensor(norms[:, 1, :], norms[:, 0, :], half_pos[:], ALU.pow).then_inc(rstd_ready, 1)

            add_experts(0)
            pool.wait_ge(consts, 3)
            scan_roots(0)
            add_experts(1)
            with pool.Fori(1, B - 1) as b:
                rstd("mix", 3 * b)
                scan_roots(b)
                add_experts(b + 1)
            rstd("mix", 3 * (B - 1))
            scan_roots(B - 1)
            rstd("mix", 3 * B)

        @block.scalar
        def _(act):
            def squares(which, b):
                act.wait_ge(centred_ready[which], b + 1)
                nc.scalar.activation(h_tok[which][:], centred[which][:], ACT.Square).then_inc(squared[which], 1)

            def shifted_h(b):
                for k in range(2):
                    act.wait_ge(mix_turned, 2 * b + k + 1)
                    nc.scalar.activation(shifted[:, 1 + k * HALF:1 + (k + 1) * HALF], mix_banks[k][:], ACT.Identity,
                                         bias=mod_col[:, 0:1], scale=mod_col[:, 1:2]).then_inc(shifted_ready, 1)

            def scan_inputs(b):
                for k in range(2):
                    act.wait_ge(scan_turned, 2 * b + k + 1)
                    nc.scalar.activation(xnT[:, half(k)], ring[0][:], ACT.Copy, scale=cols[:, 3:4]).then_inc(xnT_ready, 1)
                for k in range(2):
                    act.wait_ge(qkva_full, 2 * b + k + 1)
                    nc.scalar.activation(decay[:, half(k)], obank[0][:], ACT.Sigmoid).then_inc(decay_ready, 1)

            def gates(b):
                for k in range(2):
                    act.wait_ge(k_full, 2 * b + k + 1)
                    nc.scalar.activation(kact[:, half(k)], mix_banks[0][:], ACT.Relu).then_inc(relu_ready, 1)
                    act.wait_ge(r_full, 2 * b + k + 1)
                    nc.scalar.activation(rgate[:, half(k)], mix_banks[1][:], ACT.Sigmoid).then_inc(rgate_ready, 1)
                    act.wait_ge(relu_ready, 2 * b + k + 1)
                    nc.scalar.activation(kact[:, half(k)], kact[:, half(k)], ACT.Square).then_inc(kact_ready, 1)

            act.wait_ge(consts, 3)
            act.wait_ge(mod_cols_ready, 4)
            squares("scan", 0)
            scan_inputs(0)
            with act.Fori(1, B) as b:
                squares("mix", b - 1)
                squares("scan", b)
                shifted_h(b - 1)
                gates(b - 1)
                scan_inputs(b)
            squares("mix", B - 1)
            shifted_h(B - 1)
            gates(B - 1)

        @block.vector
        def _(dve):
            def tiles_of(t, b):
                return t[:, bass.ds(b * TB, TB), :]

            def row(m, b):
                return spread(m[:, bass.ds(b, 1), :].rearrange("p o d -> p (o d)"), 1, TB)

            def centre(link, which, b):
                c, st, src = centred[which], stats[which], tiles_of(xt, b)
                nc.vector.sem_inc(apart, 1)
                link(nc.vector.tensor_reduce(st[:, 0, :], src, AX.X, ALU.add))
                link(nc.vector.tensor_scalar(st[:, 0, :], st[:, 0, :], 1.0 / D, None, ALU.mult))
                nc.vector.tensor_tensor(c[:], src, spread(st[:, 0, :], 2, D), ALU.subtract).then_inc(centred_ready[which], 1)

            def variance(link, which, b):
                sq, st = h_tok[which], stats[which]
                dve.wait_ge(squared[which], b + 1)
                nc.vector.sem_inc(apart, 1)
                link(nc.vector.tensor_reduce(st[:, 1, :], sq[:], AX.X, ALU.add))
                nc.vector.tensor_scalar(st[:, 2, :], st[:, 1, :], 1.0 / D, LN_EPS, ALU.mult, ALU.add).then_inc(var_ready, 1)

            def centre_mix(link, b):
                nc.vector.tensor_copy(mod_col[:], mod_cols[:, bass.ds(b, 1), :].rearrange("p o c -> p (o c)")).then_inc(steps, 1)
                link.n += 1
                centre(link, "mix", b)

            def mix_h(b):
                dve.wait_ge(rstd_ready, 3 * b + 3)
                nc.vector.tensor_tensor(h_tok["mix"][:], centred["mix"][:], spread(stats["mix"][:, 3, :], 2, D), ALU.mult).then_inc(mix_h_ready, 1)

            def scan_h(link, b):
                c, h = centred["scan"], h_tok["scan"]
                dve.wait_ge(rstd_ready, 3 * b + 1)
                link(nc.vector.tensor_tensor(c[:], c[:], spread(stats["scan"][:, 3, :], 2, D), ALU.mult))
                link(nc.vector.tensor_tensor(c[:], c[:], row(mod[:, 1], b), ALU.mult))
                link(nc.vector.tensor_tensor(h[:], c[:], row(mod[:, 0], b), ALU.add))
                link(nc.vector.tensor_tensor(c[:], h[:], h[:], ALU.mult))
                nc.vector.tensor_reduce(norms[:, 0, :], c[:], AX.X, ALU.add).then_inc(var_ready, 1)

            def unit_h(link, b):
                h = h_tok["scan"]
                dve.wait_ge(rstd_ready, 3 * b + 2)
                link(nc.vector.tensor_scalar(norms[:, 2, :], norms[:, 1, :], NORM_EPS, None, ALU.max))
                link(nc.vector.reciprocal(norms[:, 3, :], norms[:, 2, :]))
                nc.vector.tensor_tensor(h[:], h[:], spread(norms[:, 3, :], 2, D), ALU.mult).then_inc(scan_h_ready, 1)

            def scan(link, b):
                for k in range(2):
                    dve.wait_ge(decay_ready, 2 * b + k + 1)
                    link(nc.vector.tensor_tensor_scan(scanned[:, half(k)], decay[:, half(k)], wide[1][:, half(k)], 0.0 if k == 0 else scanned[:, HALF - 1:HALF], ALU.mult, ALU.add))
                    nc.vector.tensor_tensor(y[:, half(k)], scanned[:, half(k)], wide[0][:, half(k)], ALU.mult).then_inc(y_ready, 1)

            def add_back(b, which, full, banks, gate, read):
                for k in range(2):
                    tiles = slice(4 * k, 4 * k + 4)
                    dve.wait_ge(full, 2 * b + k + 1)
                    nc.vector.tensor_tensor(centred[which][:, tiles, :], banks[k][:].rearrange("p (t d) -> p t d", t=4), row(gate, b)[:, tiles, :], ALU.mult).then_inc(read, 1)
                dve.wait_ge(read, 2 * b + 2)
                return nc.vector.tensor_tensor(tiles_of(xt, b), tiles_of(xt, b), centred[which][:], ALU.add)

            def scan_out(link, b):
                link(add_back(b, "scan", y_back, [ring[0], ring[0]], mod[:, 2], y_read))

            def gated_v(b):
                for k in range(2):
                    dve.wait_ge(v_full, 2 * b + k + 1)
                    nc.vector.tensor_tensor(rgate[:, half(k)], rgate[:, half(k)], mix_banks[k][:], ALU.mult).then_inc(rv_ready, 1)

            def mix_out(b):
                add_back(b, "mix", mix_back, mix_banks, gate1, mix_read).then_inc(x_ready, 1)
                dve.wait_ge(x_ready, b + 1)

            nc.vector.memset(half_pos[:], 0.5).then_inc(consts, 1)
            nc.vector.memset(shifted[:, 0:1], 0.0).then_inc(consts, 1)
            dve.wait_ge(loaded, 48)
            nc.vector.tensor_scalar(cols[:, 3:4], cols[:, 0:1], float(D) ** 0.5, None, ALU.mult).then_inc(consts, 1)
            for i in range(2):
                nc.vector.tensor_scalar(w_now[:, i], w_rkv[:, i], cols[:, 1 + i:2 + i], None, ALU.mult).then_inc(weights_ready, 1)
            dve.wait_ge(weights_ready, 2)
            nc.vector.tensor_tensor(w_prev[:], w_rkv[:, 0:2], w_now[:], ALU.subtract).then_inc(weights_ready, 1)
            for n in range(4):
                dve.wait_ge(mod_turned, n + 1)
                nc.vector.tensor_copy(mod_cols[:, 2 * n:2 * n + 2, :], [ring[0], ring[1], obank[0], obank[1]][n][:].rearrange("p (b c t) -> p b c t", b=2, c=2)[:, :, :, 0]).then_inc(mod_cols_ready, 1)
            dve.wait_ge(mod_cols_ready, 4)
            link = Chain(dve, steps, 0)
            dve.wait_ge(experts_added, 1)
            centre(link, "scan", 0)
            variance(link, "scan", 0)
            scan_h(link, 0)
            unit_h(link, 0)
            scan(link, 0)
            scan_out(link, 0)
            done = link.n
            with dve.Fori(1, B) as b:
                link = Chain(dve, steps, done + (b - 1) * STEPS_SECOND)
                centre_mix(link, b - 1)
                dve.wait_ge(experts_added, b + 1)
                centre(link, "scan", b)
                variance(link, "mix", b - 1)
                variance(link, "scan", b)
                mix_h(b - 1)
                scan_h(link, b)
                unit_h(link, b)
                gated_v(b - 1)
                mix_out(b - 1)
                scan(link, b)
                scan_out(link, b)
                assert link.n == STEPS_SECOND, link.n
            link = Chain(dve, steps, done + (B - 1) * STEPS_SECOND)
            centre_mix(link, B - 1)
            variance(link, "mix", B - 1)
            mix_h(B - 1)
            gated_v(B - 1)
            mix_out(B - 1)

        @block.tensor
        def _(pe):
            def turn(bank, src, tiles):
                for i, t in enumerate(tiles):
                    mm = nc.tensor.transpose(bank[:, i * P:(i + 1) * P], src(t), ident[:])
                return mm

            def turn_mix(b):
                pe.wait_ge(mix_h_ready, b + 1)
                for k in range(2):
                    turn(mix_banks[k], lambda t: h_tok["mix"][:, t, :], range(4 * k, 4 * k + 4)).then_inc(mix_turned, 1)

            def turn_scan(b):
                pe.wait_ge(scan_h_ready, b + 1)
                for k in range(2):
                    if k == 1:
                        pe.wait_ge(xnT_ready, 2 * b + 1)
                    turn(ring[0], lambda t: h_tok["scan"][:, t, :], range(4 * k, 4 * k + 4)).then_inc(scan_turned, 1)

            def scan_products(b):
                for k in range(2):
                    pe.wait_ge(xnT_ready, 2 * b + k + 1)
                    if k == 1:
                        pe.wait_ge(decay_ready, 2 * b + 1)
                    for j, bank in ((1, wide[1][:, half(k)]), (0, wide[0][:, half(k)]), (2, obank[0][:])):
                        mm = nc.tensor.matmul(bank, w_qkva[:, j * D:(j + 1) * D], xnT[:, half(k)], start=True, stop=True)
                    mm.then_inc(qkva_full, 1)

            def turn_y_back(b):
                for k in range(2):
                    pe.wait_ge(y_ready, 2 * b + k + 1)
                    if k == 1:
                        pe.wait_ge(y_read, 2 * b + 1)
                    turn(ring[0], lambda t: y[:, t * P:(t + 1) * P], range(4 * k, 4 * k + 4)).then_inc(y_back, 1)

            def mix_products(b):
                pe.wait_ge(shifted_ready, 2 * b + 2)
                for k in range(2):
                    if k == 1:
                        pe.wait_ge(relu_ready, 2 * b + 1)
                    nc.tensor.matmul(mix_banks[0][:], w_now[:, 1, :], shifted[:, 1 + k * HALF:1 + (k + 1) * HALF], start=True, stop=False)
                    nc.tensor.matmul(mix_banks[0][:], w_prev[:, 1, :], shifted[:, half(k)], start=False, stop=True).then_inc(k_full, 1)
                    if k == 1:
                        pe.wait_ge(rgate_ready, 2 * b + 1)
                    nc.tensor.matmul(mix_banks[1][:], w_now[:, 0, :], shifted[:, 1 + k * HALF:1 + (k + 1) * HALF], start=True, stop=False)
                    nc.tensor.matmul(mix_banks[1][:], w_prev[:, 0, :], shifted[:, half(k)], start=False, stop=True).then_inc(r_full, 1)

            def mix_values(b):
                for k in range(2):
                    pe.wait_ge(kact_ready, 2 * b + 2)
                    nc.tensor.matmul(mix_banks[k][:], w_rkv[:, 2, :], kact[:, half(k)], start=True, stop=True).then_inc(v_full, 1)

            def turn_mix_back(b):
                for k in range(2):
                    pe.wait_ge(rv_ready, 2 * b + k + 1)
                    turn(mix_banks[k], lambda t: rgate[:, t * P:(t + 1) * P], range(4 * k, 4 * k + 4)).then_inc(mix_back, 1)

            for n, bank in enumerate([ring[0], ring[1], obank[0], obank[1]]):
                for i in range(4):
                    mm = nc.tensor.transpose(bank[:, i * P:(i + 1) * P], mod[:, 3 + i % 2, 2 * n + i // 2, :], ident[:])
                mm.then_inc(mod_turned, 1)
            pe.wait_ge(loaded, 48)
            pe.wait_ge(mod_cols_ready, 4)
            pe.wait_ge(weights_ready, 3)
            turn_scan(0)
            scan_products(0)
            turn_y_back(0)
            with pe.Fori(1, B) as b:
                turn_mix(b - 1)
                mix_products(b - 1)
                mix_values(b - 1)
                turn_scan(b)
                turn_mix_back(b - 1)
                scan_products(b)
                turn_y_back(b)
            turn_mix(B - 1)
            mix_products(B - 1)
            mix_values(B - 1)
            turn_mix_back(B - 1)


def build(nc, args, out):
    with ExitStack() as ctx:
        def sb(name, shape, dt=F32):
            return ctx.enter_context(nc.sbuf_tensor(name, shape, dt))

        bank2 = [ctx.enter_context(nc.psum_tensor(f"bank2_{i}", [P, N], F32)) for i in range(2)]
        ring = [ctx.enter_context(nc.psum_tensor(f"ring{i}", [P, 512], F32)) for i in range(2)]
        obank = [ctx.enter_context(nc.psum_tensor(f"obank{i}", [P, 512], F32)) for i in range(2)]
        xt = sb("xt", [P, TT, D])
        gate0 = sb("gate0", [P, B, D])
        ident = sb("ident_sb", [P, P])
        ones = sb("ones", [P, P])
        half_neg = sb("half_neg", [P, TT])
        w_eff = sb("w_eff", [P, G * NK])
        sim_bias = sb("sim_bias", [1, G * NK])
        mean_col = sb("mean_col", [P, 1])
        banks = ring + obank
        with nc.sbuf_tensor("mod0", [P, 5, B, D], F32) as mod:
            build_modulation(nc, 0, args["c0"], args["wmod0"], args["ident"][0:B, 0:B], mod, gate0, ones, bank2)
            build_attention(nc, args["x"], args["w_qk"], args["wv"], xt, mod, ident, args["ident"], half_neg,
                            bank2, ring, obank, out)
        x2 = ctx.enter_context(nc.sbuf_tensor("x2", [P, TT, D], F32))
        with ExitStack() as experts:
            def ex(name, shape, dt=F32):
                return experts.enter_context(nc.sbuf_tensor(name, shape, dt))

            count, half_mask = ex("count", [P, P]), ex("half_mask", [P, 2])
            low_ids = ex("low_ids", [P, P, P], BF16)
            mask_b = ex("mask_b", [P, 2, P], BF16)
            downT, up = ex("downT", [P, 8 * D]), ex("up", [P, 8, D])
            loads = ((count, "count"), (half_mask, "half_mask"), (downT, "downT"), (up, "up"))
            build_product_key_table(nc, args, xt, ones, half_neg, ident, banks, bank2[0], w_eff, sim_bias, mean_col,
                                    loads, count, half_mask, low_ids, mask_b)
            build_experts(nc, x2, out, xt, ident, ones, banks, bank2, w_eff, sim_bias, mean_col, count, low_ids, mask_b, downT, up)
        mod = sb("mod1", [P, 5, B, D])
        gate1 = sb("gate1", [P, B, D])
        build_modulation(nc, 1, args["c1"], args["wmod1"], args["ident"][0:B, 0:B], mod, gate1, None, bank2)
        build_second_layer(nc, args, x2, xt, gate0, mod, gate1, ident, half_neg, ring, obank, bank2, out)


def kernel(**inputs):
    import numpy as np
    import concourse.bacc as bacc
    from concourse import mybir
    from concourse.bass_utils import run_bass_kernel_spmd as run

    a = {k: np.asarray(v) for k, v in inputs.items()}
    lay = {
        "x": a["L0_attn_x"].reshape(64, 128, 128).transpose(1, 0, 2),
        "w_qk": np.concatenate([a["L0_attn_Wq"].reshape(8, 64, 128), a["L0_attn_Wk"].reshape(8, 64, 128)], axis=1).transpose(2, 0, 1),
        "wv": a["L0_attn_Wv"].reshape(8, 128, 128).transpose(2, 0, 1),
        "c0": a["L0_c"].T,
        "wmod0": a["L0_wmod"],
        "c1": a["L1_c"].T,
        "wmod1": a["L1_wmod"],
        "w_qkva": a["L1_attn_W_qkva"].T,
        "w_rkv": np.stack([a["L1_ffn_W_r"].T, a["L1_ffn_W_k"].T, a["L1_ffn_W_v"].T], axis=1),
        "cols": np.stack([a["L1_attn_gamma"], a["L1_ffn_mu_r"], a["L1_ffn_mu_k"]], axis=1),
        "w_q": a["L0_ffn_w_q"].reshape(128, 16, 128),
        "w_qT": a["L0_ffn_w_q"].reshape(128, 16, 128).transpose(2, 1, 0),
        "keysT": a["L0_ffn_keys"].transpose(3, 2, 0, 1).reshape(128, 16, 32),
        "bn_gamma": a["L0_ffn_bn_gamma"].reshape(16, 128).T,
        "bn_beta": a["L0_ffn_bn_beta"].reshape(16, 128).T,
        "downT": a["L0_ffn_down_embed"].T,
        "up": a["L0_ffn_up_embed"].reshape(8, 128, 128).transpose(1, 0, 2),
        "count": np.broadcast_to(np.arange(128, dtype=np.float32), (128, 128)),
        "half_mask": np.tile(np.kron(np.eye(2, dtype=np.float32), np.ones((8, 1), np.float32)), (8, 1)),
        "ident": np.eye(128, dtype=np.float32),
    }
    nc = bacc.Bacc("TRN2", target_bir_lowering=False, num_devices=1)
    arrays, args = {}, {}
    for name, v in lay.items():
        v = np.ascontiguousarray(v)
        arrays[f"in_{name}"] = v
        args[name] = nc.dram_tensor(f"in_{name}", v.shape, mybir.dt.from_np(v.dtype), kind="ExternalInput").ap()
    out = nc.dram_tensor("out_x", (128, 64, 128), mybir.dt.float32, kind="ExternalOutput").ap()
    build(nc, args, out)
    r = run(nc, [arrays], core_ids=[0])
    return r.results[0]["out_x"].transpose(1, 0, 2).reshape(8, 1024, 128)
```
